# Optimizing a Trainium2 kernel written in Bass

```python
import numpy as np
import jax
import jax.numpy as jnp

def _softmax(x, axis=-1):
    return jax.nn.softmax(x, axis=axis)

def _gelu(x):
    return jax.nn.gelu(x, approximate=True)

def _silu(x):
    return jax.nn.silu(x)

def _sigmoid(x):
    return jax.nn.sigmoid(x)

def _layernorm(x, axis=-1, eps=1e-05):
    m = jnp.mean(x, axis=axis, keepdims=True)
    v = jnp.var(x, axis=axis, keepdims=True)
    return (x - m) / jnp.sqrt(v + eps)

def _scatter_add(tgt, idx, src, axis=0):
    return tgt.at[idx].add(src)

def _segment_sum(src, seg, n):
    return jax.ops.segment_sum(src, seg, n)
kernel_name = 'mk_vit_tower_postln_d1_tok_img768_r4_c78f6d'

def setup_inputs(seed: int=0):
    np.random.seed(seed)
    _w = jnp.asarray

    def _rec_inputs():
        import jax
        import jax.numpy as jnp
        _rk = jax.random.key(seed)
        x = -9.30917e-05 + 1.0002 * jax.random.normal(jax.random.fold_in(_rk, 1), (64, 3, 112, 112), jnp.float32)
        return x
    x = _rec_inputs()

    def _L0_tok_setup():
        import jax, jax.numpy as jnp
        import numpy as np
        DN = ('NCHW', 'OIHW', 'NCHW')
        G = 7

        def conv(x, w, stride, pad, groups=1):
            return jax.lax.conv_general_dilated(x, w, (stride, stride), [(pad, pad), (pad, pad)], feature_group_count=groups, dimension_numbers=DN)

        def gelu(x):
            return jax.nn.gelu(x, approximate=False)

        def bn(x, s, b):
            return x * s[None, :, None, None] + b[None, :, None, None]

        def region_layer_dw(x, wdw, sdw, bdw, wpw, spw, bpw):
            B, C, H, W = x.shape
            h, w = (H // G, W // G)
            xr = x.reshape(B, C, G, h, G, w).transpose(0, 2, 4, 1, 3, 5).reshape(B, G * G * C, h, w)
            y = gelu(bn(conv(xr, wdw, 1, 1, groups=G * G * C), sdw, bdw))
            y = bn(conv(y, wpw, 1, 0, groups=G * G), spw, bpw)
            xr = y + xr
            return xr.reshape(B, G, G, C, h, w).transpose(0, 3, 1, 4, 2, 5).reshape(B, C, H, W)
        key = jax.random.key(seed)
        ks = jax.random.split(key, 8)
        B, C0, H, W = (32, 3, 224, 224)
        E = 192
        C1 = E // 16
        C2 = E // 4
        R = G * G
        rn = lambda k, shp, sc: jax.random.normal(k, shp, jnp.float32) * sc
        return {'x': rn(ks[0], (B, C0, H, W), 1.0), 'w0': rn(ks[1], (C1, C0, 3, 3), 0.2), 's0': jnp.ones((C1,), jnp.float32), 'b0': jnp.zeros((C1,), jnp.float32), 'wdw': rn(ks[2], (R * C1, 1, 3, 3), 0.2), 'sdw': jnp.ones((R * C1,), jnp.float32), 'bdw': jnp.zeros((R * C1,), jnp.float32), 'wpw': rn(ks[3], (R * C1, C1, 1, 1), 0.1), 'spw': jnp.ones((R * C1,), jnp.float32), 'bpw': jnp.zeros((R * C1,), jnp.float32), 'w1': rn(ks[4], (C2, C1, 4, 4), 0.05), 's1': jnp.ones((C2,), jnp.float32), 'b1': jnp.zeros((C2,), jnp.float32), 'w2': rn(ks[5], (C2, C2, 2, 2), 0.05), 's2': jnp.ones((C2,), jnp.float32), 'b2': jnp.zeros((C2,), jnp.float32), 'w3': rn(ks[6], (E, C2, 2, 2), 0.05), 's3': jnp.ones((E,), jnp.float32), 'b3': jnp.zeros((E,), jnp.float32)}
    _L0_tok_all = _L0_tok_setup()
    _L0_tok_in = {k: v for k, v in _L0_tok_all.items() if k in ('w0', 's0', 'b0', 'wdw', 'sdw', 'bdw', 'wpw', 'spw', 'bpw', 'w1', 's1', 'b1', 'w2', 's2', 'b2', 'w3', 's3', 'b3')}
    del _L0_tok_all

    def _L0_attn_setup():
        import jax, jax.numpy as jnp
        import numpy as np
        DIM = 192
        GP_NUM = 49
        key = jax.random.key(seed)
        ks = jax.random.split(key, 7)
        b, n, d = (8, 512, DIM)
        s = d ** (-0.5)
        x = jax.random.normal(ks[0], (b, n, d), dtype=jnp.float32)
        W_qkv = jax.random.normal(ks[1], (d, 3 * d), dtype=jnp.float32) * s
        b_qkv = jnp.zeros((3 * d,), dtype=jnp.float32)
        W_proj = jax.random.normal(ks[2], (d, d), dtype=jnp.float32) * s
        b_proj = jnp.zeros((d,), dtype=jnp.float32)
        W_gp = jax.random.normal(ks[3], (d, GP_NUM), dtype=jnp.float32) * s
        alpha = jax.random.normal(ks[4], (), dtype=jnp.float32)
        return {'x': x, 'W_qkv': W_qkv, 'b_qkv': b_qkv, 'W_proj': W_proj, 'b_proj': b_proj, 'W_gp': W_gp, 'alpha': alpha}
    _L0_attn_all = _L0_attn_setup()
    _L0_attn_in = {k: v for k, v in _L0_attn_all.items() if k in ('W_qkv', 'b_qkv', 'W_proj', 'b_proj', 'W_gp', 'alpha')}
    del _L0_attn_all

    def _L0_ffn_setup():
        import jax, jax.numpy as jnp
        import numpy as np
        key = jax.random.key(seed)
        ks = jax.random.split(key, 6)
        B, N, D, E, S, H = (4, 1024, 192, 4, 256, 768)
        sc = lambda d: 1.0 / np.sqrt(d)
        return {'x': jax.random.normal(ks[0], (B, N, D), dtype=jnp.float32), 'phi': jax.random.normal(ks[1], (E, S, D), dtype=jnp.float32) * sc(D), 'w1': jax.random.normal(ks[2], (E, D, H), dtype=jnp.float32) * sc(D), 'b1': jnp.zeros((E, H), dtype=jnp.float32), 'w2': jax.random.normal(ks[3], (E, H, D), dtype=jnp.float32) * sc(H), 'b2': jnp.zeros((E, D), dtype=jnp.float32)}
    _L0_ffn_all = _L0_ffn_setup()
    _L0_ffn_in = {k: v for k, v in _L0_ffn_all.items() if k in ('phi', 'w1', 'b1', 'w2', 'b2')}
    del _L0_ffn_all
    return {'x': x, 'L0_tok_w0': _L0_tok_in['w0'], 'L0_tok_s0': _L0_tok_in['s0'], 'L0_tok_b0': _L0_tok_in['b0'], 'L0_tok_wdw': _L0_tok_in['wdw'], 'L0_tok_sdw': _L0_tok_in['sdw'], 'L0_tok_bdw': _L0_tok_in['bdw'], 'L0_tok_wpw': _L0_tok_in['wpw'], 'L0_tok_spw': _L0_tok_in['spw'], 'L0_tok_bpw': _L0_tok_in['bpw'], 'L0_tok_w1': _L0_tok_in['w1'], 'L0_tok_s1': _L0_tok_in['s1'], 'L0_tok_b1': _L0_tok_in['b1'], 'L0_tok_w2': _L0_tok_in['w2'], 'L0_tok_s2': _L0_tok_in['s2'], 'L0_tok_b2': _L0_tok_in['b2'], 'L0_tok_w3': _L0_tok_in['w3'], 'L0_tok_s3': _L0_tok_in['s3'], 'L0_tok_b3': _L0_tok_in['b3'], 'L0_attn_W_qkv': _L0_attn_in['W_qkv'], 'L0_attn_b_qkv': _L0_attn_in['b_qkv'], 'L0_attn_W_proj': _L0_attn_in['W_proj'], 'L0_attn_b_proj': _L0_attn_in['b_proj'], 'L0_attn_W_gp': _L0_attn_in['W_gp'], 'L0_attn_alpha': _L0_attn_in['alpha'], 'L0_ffn_phi': _L0_ffn_in['phi'], 'L0_ffn_w1': _L0_ffn_in['w1'], 'L0_ffn_b1': _L0_ffn_in['b1'], 'L0_ffn_w2': _L0_ffn_in['w2'], 'L0_ffn_b2': _L0_ffn_in['b2']}

def reference(x, L0_tok_w0, L0_tok_s0, L0_tok_b0, L0_tok_wdw, L0_tok_sdw, L0_tok_bdw, L0_tok_wpw, L0_tok_spw, L0_tok_bpw, L0_tok_w1, L0_tok_s1, L0_tok_b1, L0_tok_w2, L0_tok_s2, L0_tok_b2, L0_tok_w3, L0_tok_s3, L0_tok_b3, L0_attn_W_qkv, L0_attn_b_qkv, L0_attn_W_proj, L0_attn_b_proj, L0_attn_W_gp, L0_attn_alpha, L0_ffn_phi, L0_ffn_w1, L0_ffn_b1, L0_ffn_w2, L0_ffn_b2):
    import jax
    import jax.numpy as jnp

    def _L0_tok_ref(x, w0, s0, b0, wdw, sdw, bdw, wpw, spw, bpw, w1, s1, b1, w2, s2, b2, w3, s3, b3):
        import jax, jax.numpy as jnp
        import numpy as np
        DN = ('NCHW', 'OIHW', 'NCHW')
        G = 7

        def conv(x, w, stride, pad, groups=1):
            return jax.lax.conv_general_dilated(x, w, (stride, stride), [(pad, pad), (pad, pad)], feature_group_count=groups, dimension_numbers=DN)

        def gelu(x):
            return jax.nn.gelu(x, approximate=False)

        def bn(x, s, b):
            return x * s[None, :, None, None] + b[None, :, None, None]

        def region_layer_dw(x, wdw, sdw, bdw, wpw, spw, bpw):
            B, C, H, W = x.shape
            h, w = (H // G, W // G)
            xr = x.reshape(B, C, G, h, G, w).transpose(0, 2, 4, 1, 3, 5).reshape(B, G * G * C, h, w)
            y = gelu(bn(conv(xr, wdw, 1, 1, groups=G * G * C), sdw, bdw))
            y = bn(conv(y, wpw, 1, 0, groups=G * G), spw, bpw)
            xr = y + xr
            return xr.reshape(B, G, G, C, h, w).transpose(0, 3, 1, 4, 2, 5).reshape(B, C, H, W)
        x = gelu(bn(conv(x, w0, 1, 1), s0, b0))
        x = region_layer_dw(x, wdw, sdw, bdw, wpw, spw, bpw)
        x = gelu(x)
        x = gelu(bn(conv(x, w1, 4, 0), s1, b1))
        x = gelu(bn(conv(x, w2, 2, 0), s2, b2))
        x = bn(conv(x, w3, 2, 0), s3, b3)
        B, E, Hp, Wp = x.shape
        return x.reshape(B, E, Hp * Wp).transpose(0, 2, 1)

    def _L0_attn_ref(x, W_qkv, b_qkv, W_proj, b_proj, W_gp, alpha):
        import jax, jax.numpy as jnp
        import numpy as np
        DIM = 192
        GP_NUM = 49
        d = x.shape[-1]
        scale = d ** (-0.5)
        qkv = x @ W_qkv + b_qkv
        q, k, v = jnp.split(qkv, 3, axis=-1)
        attn_scores = jnp.einsum('bnd,bmd->bnm', q, k) * scale
        gw = jax.nn.softmax(jax.nn.gelu(v @ W_gp, approximate=False), axis=-1)
        group_weight = jnp.einsum('bng,bmg->bnm', gw, gw)
        attn_scores = jax.nn.softmax(attn_scores * group_weight, axis=-1)
        a = jax.nn.sigmoid(alpha)
        attn_weights = (1.0 - a) * attn_scores + a * group_weight
        out = jnp.einsum('bnm,bmd->bnd', attn_weights, v)
        return out @ W_proj + b_proj

    def _L0_ffn_ref(x, phi, w1, b1, w2, b2):
        import jax, jax.numpy as jnp
        import numpy as np
        logits = jnp.einsum('bnd,esd->bnes', x, phi)
        B, N, E, S = logits.shape
        dispatch = jax.nn.softmax(logits, axis=1)
        combine = jax.nn.softmax(logits.reshape(B, N, E * S), axis=-1).reshape(B, N, E, S)
        slots = jnp.einsum('bnd,bnes->besd', x, dispatch)
        h = jax.nn.gelu(jnp.einsum('besd,edh->besh', slots, w1) + b1[None, :, None, :])
        y = jnp.einsum('besh,ehd->besd', h, w2) + b2[None, :, None, :]
        out = jnp.einsum('besd,bnes->bnd', y, combine)
        return out
    h = _L0_tok_ref(x, L0_tok_w0, L0_tok_s0, L0_tok_b0, L0_tok_wdw, L0_tok_sdw, L0_tok_bdw, L0_tok_wpw, L0_tok_spw, L0_tok_bpw, L0_tok_w1, L0_tok_s1, L0_tok_b1, L0_tok_w2, L0_tok_s2, L0_tok_b2, L0_tok_w3, L0_tok_s3, L0_tok_b3)
    h = _layernorm(h + _L0_attn_ref(h, L0_attn_W_qkv, L0_attn_b_qkv, L0_attn_W_proj, L0_attn_b_proj, L0_attn_W_gp, L0_attn_alpha), axis=-1)
    h = _layernorm(h + _L0_ffn_ref(h, L0_ffn_phi, L0_ffn_w1, L0_ffn_b1, L0_ffn_w2, L0_ffn_b2), axis=-1)
    return h

_drawn_inputs = setup_inputs


def setup_inputs(seed=0):
    import zlib

    import numpy as np

    out = dict(_drawn_inputs(seed))
    spreads = {'L0_tok_s0': (1.0, 0.2),
     'L0_tok_b0': (0.0, 0.1),
     'L0_tok_sdw': (1.0, 0.6),
     'L0_tok_bdw': (0.0, 0.8),
     'L0_tok_spw': (1.0, 0.6),
     'L0_tok_bpw': (0.0, 0.271),
     'L0_tok_s1': (1.0, 0.2),
     'L0_tok_b1': (0.0, 0.1),
     'L0_tok_s2': (1.0, 0.2),
     'L0_tok_b2': (0.0, 0.1),
     'L0_tok_s3': (1.0, 0.2),
     'L0_tok_b3': (0.0, 0.1),
     'L0_attn_b_qkv': (0.0, 0.1),
     'L0_attn_b_proj': (0.0, 0.1),
     'L0_ffn_b1': (0.0, 0.1),
     'L0_ffn_b2': (0.0, 0.1)}
    factors = {'L0_attn_W_gp': 8.0}
    for name, (base, spread) in spreads.items():
        noise = np.random.default_rng([zlib.crc32(name.encode()), seed]).standard_normal(out[name].shape)
        drawn = base * np.exp(spread * noise) if base else spread * noise
        out[name] = jnp.asarray(drawn.astype(out[name].dtype))
    for name, factor in factors.items():
        out[name] = (out[name] * factor).astype(out[name].dtype)
    return out
```

```python
from contextlib import ExitStack

import numpy as np
import concourse.bass as bass
from concourse import mybir

F32 = mybir.dt.float32
ALU = mybir.AluOpType
ACT = mybir.ActivationFunctionType
AX_X = mybir.AxisListType.X

P = 128
IMAGES, CIN, SIDE = 64, 3, 112
GRID = 7
RS = SIDE // GRID
CH = 12
CB = P // RS
CR = CH - CB
REGIONS = GRID * GRID
HALF = IMAGES // 2
E = 192
EH = E // 2
C2 = 48
TOKENS = GRID * GRID
HALO = RS + 2
KX = CIN * HALO
XW = SIDE + 2
GW = RS + 2
BC = 4
CHUNKS = HALF // BC
NREG = HALF * RS
Q = RS // 4
SLOT = 64
TW = 441 + REGIONS + 588 + REGIONS
O_DW, O_BDW, O_PW, O_BPW = 0, 441, 490, 1078


def conv_phase(nc, a, XT, ident):
    x = a["x"]
    with ExitStack() as ctx:
        def sb(name, shape, dt=F32):
            return ctx.enter_context(nc.sbuf_tensor(name, shape, dt))

        def sem(name):
            return ctx.enter_context(nc.semaphore(name))

        X = sb("X", [KX, 2, HALF, XW])
        G = sb("G", [P, 3, HALF, GRID, GW])
        D = sb("D", [P, 2, 3, NREG])
        H1 = sb("H1", [96, 2, 2, HALF, 28])
        H2 = sb("H2", [96, 2, HALF, 14])
        W0 = sb("W0", [KX, 3, CH, RS])
        WD = sb("WD", [P, 2, 2, 3, P])
        WP = sb("WP", [P, 2, 448])
        W1 = sb("W1", [P, 2, 2, 4, 96])
        W2 = sb("W2", [96, 2, 2, 96])
        W3 = sb("W3", [96, 2, 2, 96])
        AC = sb("AC", [P, 2, GRID, 3, RS])
        ACt = sb("ACt", [P, GRID, 3, RS])
        TAB = sb("TAB", [P, 2, TW])
        BV = sb("BV", [P, 2, 2, GRID])
        mY = sb("mY", [P, HALO])
        mX = sb("mX", [KX, HALO])
        mC = sb("mC", [P, CB])
        m4 = sb("m4", [P, Q])
        SEL = sb("SEL", [48, 5, P])
        b0v = sb("b0v", [P, 2])
        b1v = sb("b1v", [96, 1])
        b2v = sb("b2v", [96, 1])
        b3v = sb("b3v", [96, 2])
        raw = H1[:, :, :, :, :].rearrange("p t h b x -> p (t h b x)")
        T12 = raw[0:CH, 1344:1344 + TW]
        s12 = raw[0:CH, 2471:2471 + REGIONS + 588]
        w0s = sb("w0s", [CIN, CH, 9])
        s0s = sb("s0s", [CIN, CH])
        w1s = raw[0:C2, 0:192]
        w2s = raw[0:C2, 192:384]
        w3s = raw[:, 384:768].rearrange("o (h n) -> o h n", h=2)
        w2p = raw[0:C2, 768:960].rearrange("o (x y c) -> o x y c", x=2, y=2)
        w3p = raw[:, 960:1344].rearrange("o (h x y c) -> o h x y c", h=2, x=2, y=2)
        s123 = sb("s123", [96, 4])
        b0s = sb("b0s", [CH, 1])
        w1t = raw[0:C2, 3108:3300].rearrange("p (k o) -> p k o", k=4)
        w0c = sb("w0c", [CIN, 9, CH])
        zrow = sb("zrow", [1, SIDE])
        ps = ctx.enter_context(nc.psum_tensor("ps", [P, 8, 512], F32))
        CST_DONE = 19
        PREP_DONE = 60
        SCALED, TRANSPOSED = 10, 10 + 6 + 1 + 15 + 6
        TSPLIT = ((0, 490), (490, 980), (980, TW))
        X0 = D[0:KX, 0, :, 0:CH * RS].rearrange("p t (c y) -> p t c y", y=RS)

        x_cleared = sem("x_cleared")
        x_loaded = sem("x_loaded")
        par = sem("par")
        cst = sem("cst")
        prep = sem("prep")
        tr = sem("tr")
        c0_mm = sem("c0_mm")
        c0_act = sem("c0_act")
        wt = sem("wt")
        dw_mm = sem("dw_mm")
        dw_act = sem("dw_act")
        pw_mm = sem("pw_mm")
        pw_add = sem("pw_add")
        g3 = sem("g3")
        c1_mm = sem("c1_mm")
        c1_act = sem("c1_act")
        c3_dve = sem("c3_dve")
        chained = sem("chained")
        block = ctx.enter_context(nc.Block())
        NPAR = 26

        @block.sync
        def _(sp):
            def rows(gy_row, first, last):
                for h in range(2):
                    for c in range(CIN):
                        src = x[h * HALF:(h + 1) * HALF, c]
                        p = c * HALO
                        sp.dma_start(X[p + 1:p + 1 + RS, h, :, 1:1 + SIDE],
                                     src[:, bass.ds(gy_row, RS), :].rearrange("b y x -> y b x")).then_inc(x_loaded, 16)
                        if not first:
                            sp.dma_start(X[p:p + 1, h, :, 1:1 + SIDE],
                                         src[:, bass.ds(gy_row - 1, 1), :].rearrange("b y x -> y b x")).then_inc(x_loaded, 16)
                        if not last:
                            sp.dma_start(X[p + HALO - 1:p + HALO, h, :, 1:1 + SIDE],
                                         src[:, bass.ds(gy_row + RS, 1), :].rearrange("b y x -> y b x")).then_inc(x_loaded, 16)
                        else:
                            sp.dma_start(X[p + HALO - 1:p + HALO, h, :, 1:1 + SIDE],
                                         zrow[0:1, :].unsqueeze(1).broadcast_to([1, HALF, SIDE])).then_inc(x_loaded, 16)

            sp.wait_ge(x_cleared, 1)
            rows(0, True, False)
            with sp.Fori(1, GRID - 1) as gy:
                sp.wait_ge(c0_mm, gy * CHUNKS)
                rows(gy * RS, False, False)
            sp.wait_ge(c0_mm, (GRID - 1) * CHUNKS)
            rows((GRID - 1) * RS, False, True)

        @block.scalar
        def _(act):
            def param(dst, src):
                act.dma_start(dst, src, allow_slow_non_contiguous=True).then_inc(par, 16)

            param(w0s[:, :, :], a["w0"].rearrange("o c a b -> c o (a b)"))
            param(s0s[:, :], a["s0"].rearrange("(a o) -> a o", a=1).broadcast_to([CIN, CH]))
            param(T12[:, O_DW:O_BDW].rearrange("c (r t) -> c r t", t=9), a["wdw"].rearrange("(r c) u a b -> c r (u a b)", c=CH))
            param(s12[:, 0:REGIONS], a["sdw"].rearrange("(r c) -> c r", c=CH))
            param(T12[:, O_BDW:O_PW], a["bdw"].rearrange("(r c) -> c r", c=CH))
            param(T12[:, O_BPW:TW], a["bpw"].rearrange("(r c) -> c r", c=CH))
            param(T12[:, O_PW:O_BPW], a["wpw"].rearrange("q c u v -> c (q u v)"))
            param(s12[:, REGIONS:], a["spw"].rearrange("(a q) -> a q", a=1).broadcast_to([CH, 588]))
            param(b0s[:, :], a["b0"].rearrange("(c u) -> c u", u=1))
            param(w1s[:, :], a["w1"].rearrange("o c a b -> o (c a b)"))
            param(w2s[:, :], a["w2"].rearrange("o c a b -> o (c a b)"))
            param(w3s[:, :, :], a["w3"].rearrange("(h o) c a b -> o h (c a b)", h=2))
            param(s123[0:C2, 0:1], a["s1"].rearrange("(c u) -> c u", u=1))
            param(s123[0:C2, 1:2], a["s2"].rearrange("(c u) -> c u", u=1))
            param(s123[:, 2:4], a["s3"].rearrange("(h o) -> o h", h=2))
            param(b3v[:, :], a["b3"].rearrange("(h o) -> o h", h=2))
            for h in range(2):
                param(b1v[C2 * h:C2 * h + C2, :], a["b1"].rearrange("(c u) -> c u", u=1))
                param(b2v[C2 * h:C2 * h + C2, :], a["b2"].rearrange("(c u) -> c u", u=1))

            act.wait_ge(prep, PREP_DONE)
            with act.Fori(0, GRID) as gy:
                for c in range(CHUNKS):
                    s = c % 2 * 3
                    act.wait_ge(c0_mm, gy * CHUNKS + c + 1)
                    for t in range(3):
                        k = t // 2
                        dst = G[:, t, BC * c:BC * c + BC, :, 1:1 + RS]
                        src = ps[:, s + t, 0:BC * SIDE].rearrange("p (b g x) -> p b g x", b=BC, g=GRID)
                        ins = act.activation(dst, src, ACT.Gelu, bias=b0v[:, k:k + 1])
                    ins.then_inc(c0_act, 1)

                def last_gelu(g):
                    for t in range(3):
                        act.wait_ge(pw_add, gy * 21 + 3 * g + t + 1)
                        v = G[:, t, :, g, 1:1 + RS]
                        act.activation(v, v, ACT.Gelu).then_inc(g3, 1)

                for g in range(GRID):
                    act.wait_ge(wt, gy * GRID + g + 1)
                    for t in range(3):
                        act.wait_ge(dw_mm, gy * 21 + 3 * g + t + 1)
                        if g >= 2:
                            act.wait_ge(pw_mm, gy * 21 + 3 * (g - 1))
                        act.activation(D[:, g % 2, t, :], ps[:, t, :], ACT.Gelu,
                                       bias=BV[:, 0, t // 2, g:g + 1]).then_inc(dw_act, 1)
                    if g >= 1:
                        last_gelu(g - 1)
                last_gelu(GRID - 1)
                n = 0
                for h in range(2):
                    for t in range(2):
                        for i in range(2):
                            act.wait_ge(c1_mm, gy * 12 + n + 1)
                            act.activation(H1[:, t, h, 16 * i:16 * i + 16, :],
                                           ps[0:96, 6 + n % 2, 0:448].rearrange("p (b x) -> p b x", b=16),
                                           ACT.Gelu, bias=b1v[:, 0:1]).then_inc(c1_act, 1)
                            n += 1
                for h in range(2):
                    act.wait_ge(c1_mm, gy * 12 + n + 1)
                    act.activation(H2[:, h, :, :], ps[0:96, 6 + n % 2, 0:448].rearrange("p (b x) -> p b x", b=HALF),
                                   ACT.Gelu, bias=b2v[:, 0:1]).then_inc(c1_act, 1)
                    n += 1

        @block.gpsimd
        def _(pool):
            n = [0]

            def step(ins):
                n[0] += 1
                ins.then_inc(cst, 1)
                pool.wait_ge(cst, n[0])

            def mark(v, pattern, base, slope):
                step(pool.affine_select(out=v, in_=v, compare_op=ALU.not_equal, fill=1.0, base=base,
                                        pattern=pattern, channel_multiplier=slope))

            pool.memset(zrow[:, :], 0.0)
            pool.memset(X[:, :, :, :], 0.0).then_inc(x_cleared, 1)
            pool.wait_ge(x_cleared, 1)
            step(pool.memset(ident[:, :], 0.0))
            mark(ident[:, :], [[-1, P]], 0, 1)
            step(pool.memset(mY[:, :], 0.0))
            step(pool.memset(SEL[:, :, :], 0.0))
            mark(SEL[0:CH, 0, :].rearrange("c (j y) -> c j y", y=RS), [[-1, CB], [0, RS]], 0, 1)
            mark(SEL[0:CH, 1, :].rearrange("c (h j y) -> c h j y", h=2, y=RS), [[0, 2], [-1, CR], [0, RS]], -CB, 1)
            mark(SEL[0:CIN, 2, 0:KX].rearrange("c (j y) -> c j y", y=HALO), [[-1, CIN], [0, HALO]], 0, 1)
            mark(SEL[:, 3, :].rearrange("c (j y r) -> c j y r", j=CB, r=4), [[-4, CB], [0, Q], [-1, 4]], 0, 1)
            for h in range(2):
                mark(SEL[:, 4, 64 * h:64 * h + 64].rearrange("c (j y r) -> c j y r", j=CR, r=4),
                     [[-4, CR], [0, Q], [-1, 4]], -4 * CB, 1)
            step(pool.memset(mC[:, :], 1.0))
            step(pool.affine_select(out=mC[:, :], in_=mC[:, :], compare_op=ALU.is_ge, fill=0.0,
                                    base=0, pattern=[[-RS, CB]], channel_multiplier=1))
            step(pool.affine_select(out=mC[:, :], in_=mC[:, :], compare_op=ALU.is_ge, fill=0.0,
                                    base=RS - 1, pattern=[[RS, CB]], channel_multiplier=-1))
            step(pool.memset(WP[:, :, :], 0.0))
            step(pool.memset(W2[:, :, :, :], 0.0))
            step(pool.memset(G[:, :, :, :, 0:1], 0.0))
            step(pool.memset(G[:, :, :, :, GW - 1:GW], 0.0))
            step(pool.memset(XT[:, :, :, :], 0.0))
            step(pool.memset(XT[96:97, 1, :, :], 1.0))
            assert n[0] == CST_DONE, n[0]

        @block.vector
        def _(dve):
            n = [0]

            def step(ins, wait=True):
                n[0] += 1
                ins.then_inc(prep, 1)
                if wait:
                    dve.wait_ge(prep, n[0])

            dve.wait_ge(cst, CST_DONE)
            step(dve.tensor_reduce(mY[:, 1:1 + RS], ident[:, :].rearrange("p (j y) -> p y j", y=RS), AX_X, ALU.add))
            step(dve.tensor_reduce(mX[:, :], ident[0:KX, 0:KX].rearrange("p (j y) -> p y j", y=HALO), AX_X, ALU.add))
            step(dve.tensor_reduce(m4[:, :], mY[:, 1:1 + RS].rearrange("p (j r) -> p j r", r=4), AX_X, ALU.add))
            dve.wait_ge(par, 16 * 20)
            v = T12[:, O_DW:O_BDW].rearrange("c (r t) -> c r t", t=9)
            step(dve.tensor_tensor(v, v, s12[:, 0:REGIONS].unsqueeze(2).broadcast_to([CH, REGIONS, 9]), ALU.mult))
            v = T12[:, O_PW:O_BPW]
            step(dve.tensor_tensor(v, v, s12[:, REGIONS:], ALU.mult))
            step(dve.tensor_tensor(w0c[:, :, :], w0s[:, :, :].rearrange("c o t -> c t o"),
                                   s0s[:, :].unsqueeze(1).broadcast_to([CIN, 9, CH]), ALU.mult))
            step(dve.tensor_scalar(w1s[:, :], w1s[:, :], s123[0:C2, 0:1], None, ALU.mult))
            step(dve.tensor_scalar(w2p[:, :, :, :], w2s[:, :].rearrange("o (c y x) -> o x y c", y=2, x=2),
                                   s123[0:C2, 1:2], None, ALU.mult))
            for h in range(2):
                step(dve.tensor_scalar(w3p[:, h], w3s[:, h, :].rearrange("o (c y x) -> o x y c", y=2, x=2),
                                       s123[:, 2 + h:3 + h], None, ALU.mult))
            assert n[0] == SCALED
            dve.wait_ge(tr, 1)
            for k in range(2):
                for j, (lo, hi) in enumerate(TSPLIT):
                    step(dve.tensor_copy(TAB[:, k, lo:hi], ps[:, 3 * k + j, 0:hi - lo]), False)
            dve.wait_ge(tr, 2)
            step(dve.tensor_copy(b0v[:, :], ps[:, 7, 0:2]), False)
            w0r = ps[0:KX, 6, 0:9 * CH].rearrange("p (y x c) -> p y x c", y=3, x=3)
            acc = W0[:, :, :, :]
            tmp = X0[:, :, :, :]
            for dx in range(3):
                for dy in range(3):
                    m = mX[:, dy:dy + RS].unsqueeze(1).broadcast_to([KX, CH, RS])
                    w = w0r[:, dy, dx, :].unsqueeze(2).broadcast_to([KX, CH, RS])
                    if dy == 0:
                        step(dve.tensor_tensor(acc[:, dx], w, m, ALU.mult))
                    else:
                        step(dve.tensor_tensor(tmp[:, dx], w, m, ALU.mult))
                        step(dve.tensor_tensor(acc[:, dx], acc[:, dx], tmp[:, dx], ALU.add))
            dve.wait_ge(tr, 3)
            step(dve.tensor_copy(w1t[:, :, :], ps[0:C2, 0, 0:4 * C2].rearrange("p (k o) -> p k o", k=4)), False)
            for kx in range(2):
                for t in range(2):
                    step(dve.tensor_copy(W2[:, t, kx, C2 * t:C2 * t + C2], ps[0:96, 1, C2 * kx:C2 * kx + C2]), False)
            step(dve.tensor_copy(W3[:, :, :, :], ps[0:96, 2, 0:384].rearrange("p (k h o) -> p k h o", k=2, h=2)), False)
            assert n[0] == TRANSPOSED
            dve.wait_ge(tr, 4)
            for k in range(2):
                for t in range(2):
                    for q in range(2):
                        step(dve.tensor_scalar(W1[:, k, t, :, C2 * q:C2 * q + C2],
                                               ps[:, 3 + k, 0:4 * C2].rearrange("p (k o) -> p k o", k=4),
                                               m4[:, 2 * t + q:2 * t + q + 1], None, ALU.mult), False)
            dve.wait_ge(prep, n[0])
            while n[0] < PREP_DONE:
                step(dve.nop(), False)
            assert n[0] == PREP_DONE, n[0]

            with dve.Fori(0, GRID) as gy:
                done = [0]

                def chain(ins):
                    done[0] += 1
                    ins.then_inc(chained, 1)
                    dve.wait_ge(chained, gy * 10 + done[0])

                dve.wait_ge(pw_add, gy * 21)
                dve.wait_ge(dw_act, gy * 21)
                dve.wait_ge(wt, gy * GRID)
                dve.wait_ge(pw_mm, gy * 21)
                for i, o in enumerate((O_BDW, O_BPW)):
                    dve.tensor_copy(BV[:, i], TAB[:, :, bass.ds(gy * GRID + o, GRID)])
                for k in range(2):
                    r = TAB[:, k, bass.ds(gy * (GRID * 9), GRID * 9)].rearrange("p (g y x) -> p g y x", g=GRID, y=3)
                    for dy in range(3):
                        m = mY[:, dy:dy + RS].unsqueeze(1).unsqueeze(1).broadcast_to([P, GRID, 3, RS])
                        w = r[:, :, dy, :].unsqueeze(3).broadcast_to([P, GRID, 3, RS])
                        if dy == 0:
                            chain(dve.tensor_tensor(AC[:, k], w, m, ALU.mult))
                        else:
                            chain(dve.tensor_tensor(ACt[:, :, :, :], w, m, ALU.mult))
                            chain(dve.tensor_tensor(AC[:, k], AC[:, k], ACt[:, :, :, :], ALU.add))

                def matrices(g):
                    s = g % 2
                    if g >= 2:
                        dve.wait_ge(pw_mm, gy * 21 + 3 * (g - 1))
                    for k in range(2):
                        dve.tensor_tensor(WD[:, s, k].rearrange("p x (c y) -> p x c y", y=RS),
                                          AC[:, k, g].unsqueeze(2).broadcast_to([P, 3, CB, RS]),
                                          mC[:, :].unsqueeze(1).unsqueeze(3).broadcast_to([P, 3, CB, RS]), ALU.mult)
                    my = mY[:, 1:1 + RS]
                    for k, col, lo, n_, rows_ in ((0, 0, 0, CH, slice(0, P)), (1, 192, 0, CB, slice(0, P)),
                                                  (1, 320, CB, CR, slice(0, 64)), (1, 384, CB, CR, slice(64, P))):
                        np_ = rows_.stop - rows_.start
                        w = TAB[rows_, k, bass.ds(gy * (GRID * CH) + (O_PW + g * CH + lo), n_)]
                        ins = dve.tensor_tensor(WP[rows_, s, col:col + RS * n_].rearrange("p (c y) -> p c y", y=RS),
                                                w.unsqueeze(2).broadcast_to([np_, n_, RS]),
                                                my[rows_].unsqueeze(1).broadcast_to([np_, n_, RS]), ALU.mult)
                    ins.then_inc(wt, 1)

                def add(g):
                    for t in range(3):
                        dve.wait_ge(pw_mm, gy * 21 + 3 * g + t + 1)
                        v = G[:, t, :, g, 1:1 + RS]
                        dve.scalar_tensor_tensor(out=v, in0=ps[:, 3 + t, :].rearrange("p (b x) -> p b x", b=HALF),
                                                 scalar=BV[:, 1, t // 2, g:g + 1], in1=v,
                                                 op0=ALU.add, op1=ALU.add).then_inc(pw_add, 1)

                matrices(0)
                matrices(1)
                for g in range(GRID):
                    add(g)
                    if g + 2 < GRID:
                        matrices(g + 2)
                for o in range(2):
                    dve.wait_ge(c1_mm, gy * 12 + 11 + o)
                    for h in range(2):
                        dve.tensor_scalar(XT[0:96, o, :, bass.ds(gy * GRID + SLOT * h, GRID)],
                                          ps[0:96, 6 + o, 224 * h:224 * h + 224].rearrange("p (b x) -> p b x", b=HALF),
                                          b3v[:, o:o + 1], None, ALU.add).then_inc(c3_dve, 1)

        @block.tensor
        def _(pe):
            mm = nc.tensor.matmul
            pe.wait_ge(prep, SCALED)
            for k in range(2):
                for j, (lo, hi) in enumerate(TSPLIT):
                    ins = mm(ps[:, 3 * k + j, 0:hi - lo], SEL[0:CH, k, :], T12[:, lo:hi], start=True, stop=True)
            ins.then_inc(tr, 1)
            mm(ps[0:KX, 6, 0:9 * CH], SEL[0:CIN, 2, 0:KX], w0c[:, :, :].rearrange("c t o -> c (t o)"), start=True, stop=True)
            for k in range(2):
                ins = mm(ps[:, 7, k:k + 1], SEL[0:CH, k, :], b0s[:, :], start=True, stop=True)
            ins.then_inc(tr, 1)
            pe.wait_ge(prep, SCALED + 6)
            for kx in range(4):
                nc.tensor.transpose(ps[0:C2, 0, C2 * kx:C2 * kx + C2], w1s[:, kx:kx + 4 * (C2 - 1) + 1:4], ident[0:C2, 0:C2])
            for kx in range(2):
                v = w2p[:, kx].rearrange("o y c -> o (y c)")
                nc.tensor.transpose(ps[0:96, 1, C2 * kx:C2 * kx + C2], v, ident[0:C2, 0:C2])
                for h in range(2):
                    v = w3p[:, h, kx].rearrange("o y c -> o (y c)")
                    ins = nc.tensor.transpose(ps[0:96, 2, 192 * kx + 96 * h:192 * kx + 96 * h + 96], v, ident[0:96, 0:96])
            ins.then_inc(tr, 1)
            pe.wait_ge(prep, TRANSPOSED)
            for k in range(2):
                ins = mm(ps[:, 3 + k, 0:4 * C2], SEL[:, 3 + k, :], w1t[:, :, :].rearrange("p k o -> p (k o)"), start=True, stop=True)
            ins.then_inc(tr, 1)
            pe.wait_ge(prep, PREP_DONE)
            pe.wait_ge(x_loaded, 16 * 12)

            with pe.Fori(0, GRID) as gy:
                pe.wait_ge(x_loaded, gy * (16 * 18) + 16 * 12)
                for c in range(CHUNKS):
                    s = c % 2 * 3
                    if c == 0:
                        pe.wait_ge(dw_act, gy * 21)
                        pe.wait_ge(c1_mm, gy * 12)
                    elif c == 1:
                        pe.wait_ge(pw_add, gy * 21)
                    else:
                        pe.wait_ge(c0_act, gy * CHUNKS + c - 1)
                    W0v = W0[:, :, :, :].rearrange("p x c y -> p x (c y)")
                    for t, (out, h, cols) in enumerate(((ps[:, s], 0, slice(0, P)), (ps[:, s + 1], 1, slice(0, P)),
                                                        (ps[0:64, s + 2], 0, slice(P, 192)), (ps[64:P, s + 2], 1, slice(P, 192)))):
                        for kx in range(3):
                            ins = mm(out[:, 0:BC * SIDE], W0v[:, kx, cols], X[:, h, BC * c:BC * c + BC, kx:kx + SIDE],
                                     start=(kx == 0), stop=(kx == 2))
                    ins.then_inc(c0_mm, 1)

                def depthwise(g):
                    pe.wait_ge(wt, gy * GRID + g + 1)
                    for t in range(3):
                        if g == 0:
                            pe.wait_ge(c0_act, gy * CHUNKS + CHUNKS)
                        else:
                            pe.wait_ge(dw_act, gy * 21 + 3 * (g - 1) + t + 1)
                        for kx in range(3):
                            ins = mm(ps[:, t, :], WD[:, g % 2, t // 2, kx, :], G[:, t, :, g, kx:kx + RS],
                                     start=(kx == 0), stop=(kx == 2))
                        ins.then_inc(dw_mm, 1)

                def pointwise(g):
                    w = WP[:, g % 2, :]
                    d = D[:, g % 2]
                    for t in range(2):
                        pe.wait_ge(dw_act, gy * 21 + 3 * g + 3)
                        if g >= 1:
                            pe.wait_ge(pw_add, gy * 21 + 3 * (g - 1) + t + 1)
                        half = slice(64 * t, 64 * t + 64)
                        mm(ps[:, 3 + t, :], w[:, 0:P], d[:, t, :], start=True, stop=False)
                        mm(ps[:, 3 + t, :], w[half, 192:320], d[half, 2, :], start=False, stop=True).then_inc(pw_mm, 1)
                    if g >= 1:
                        pe.wait_ge(pw_add, gy * 21 + 3 * g)
                    mm(ps[:, 5, :], w[:, 320:448], d[:, 2, :], start=True, stop=False)
                    mm(ps[0:64, 5, :], w[:, P:192], d[:, 0, :], start=False, stop=True)
                    mm(ps[64:P, 5, :], w[:, P:192], d[:, 1, :], start=False, stop=True).then_inc(pw_mm, 1)

                depthwise(0)
                for g in range(GRID):
                    if g + 1 < GRID:
                        depthwise(g + 1)
                    pointwise(g)
                pe.wait_ge(g3, gy * 21 + 21)
                n = 0
                for h in range(2):
                    for t in range(2):
                        for i in range(2):
                            if n < 2:
                                pe.wait_ge(c3_dve, gy * 4)
                            else:
                                pe.wait_ge(c1_act, gy * 10 + n - 1)
                            out = ps[0:96, 6 + n % 2, 0:448]
                            b = slice(16 * i, 16 * i + 16)
                            half = slice(64 * h, 64 * h + 64)
                            for kx in range(4):
                                big = G[:, h, b, :, 1 + kx:1 + RS:4]
                                rest = G[half, 2, b, :, 1 + kx:1 + RS:4]
                                mm(out, W1[:, 0, t, kx, :], big, start=(kx == 0), stop=False)
                                ins = mm(out, W1[half, 1, t, kx, :], rest, start=False, stop=(kx == 3))
                            ins.then_inc(c1_mm, 1)
                            n += 1
                for h in range(2):
                    pe.wait_ge(c1_act, gy * 10 + 4 * h + 4)
                    pe.wait_ge(c1_act, gy * 10 + n - 1)
                    out = ps[0:96, 6 + n % 2, 0:448]
                    for t in range(2):
                        for kx in range(2):
                            ins = mm(out, W2[:, t, kx, :], H1[:, t, h, :, kx:28:2], start=(t + kx == 0), stop=(t + kx == 2))
                    ins.then_inc(c1_mm, 1)
                    n += 1
                pe.wait_ge(c1_act, gy * 10 + 10)
                for o in range(2):
                    for h in range(2):
                        for kx in range(2):
                            ins = mm(ps[0:96, 6 + o, 224 * h:224 * h + 224], W3[:, kx, o, :], H2[:, h, :, kx:14:2],
                                     start=(kx == 0), stop=(kx == 1))
                    ins.then_inc(c1_mm, 1)


def attention_phase(nc, a, XT, Y1, ident):
    PAIRS = HALF
    KG = 49
    EA = EH + 1
    HK = ((slice(0, EH), 0), (slice(0, EA), 1))
    with ExitStack() as ctx:
        def sb(name, shape, dt=F32):
            return ctx.enter_context(nc.sbuf_tensor(name, shape, dt))

        def sem(name):
            return ctx.enter_context(nc.semaphore(name))

        WQ = sb("WQ", [EA, 2, 3 * E])
        WQT = sb("WQT", [EH, 3, 2, E + 1])
        WGP = sb("WGP", [EH, 2, KG])
        WPJ = sb("WPJ", [EH, 2, E])
        GM = sb("GM", [EA, 2, E + 1])
        WR = sb("WR", [EA, 2, KG + 2 * E])
        XP = sb("XP", [EA, 2, 2, P])
        UT = sb("UT", [EA, 2, 2, P])
        VP = sb("VP", [P, PAIRS, 2 * E])
        SC = sb("SC", [P, PAIRS, KG])
        GA = sb("GA", [P, PAIRS, KG])
        GG = sb("GG", [P, PAIRS, KG])
        GT = sb("GT", [P, 2, P])
        red = sb("red", [P, PAIRS])
        inv = sb("inv", [P, PAIRS])
        al = sb("al", [P, 3])
        BD = sb("BD", [P, 2, P])
        BT = sb("BT", [P, 2, P])
        st = sb("st", [P, 2, 6])
        ms = sb("ms", [P, 2, 2])
        yb = sb("yb", [P, 2, E])
        scratch = sb("scratch", [P, 1])
        mv = sb("mv", [P, PAIRS, 2])
        eps = sb("eps", [P, PAIRS, 2])
        ps = ctx.enter_context(nc.psum_tensor("psa", [P, 8, 512], F32))

        par = sem("a_par")
        prep = sem("a_prep")
        tr = sem("a_tr")
        zero = sem("a_zero")
        xp = sem("a_xp")
        u_mm = sem("a_u_mm")
        u_cp = sem("a_u_cp")
        s_mm = sem("a_s_mm")
        s_cp = sem("a_s_cp")
        glu = sem("a_glu")
        soft = sem("a_soft")
        ex = sem("a_ex")
        gt_mm = sem("a_gt_mm")
        gt_cp = sem("a_gt_cp")
        gg_mm = sem("a_gg_mm")
        gg_cp = sem("a_gg_cp")
        bd = sem("a_bd")
        bt_mm = sem("a_bt_mm")
        bt_cp = sem("a_bt_cp")
        o_mm = sem("a_o_mm")
        o_cp = sem("a_o_cp")
        stat = sem("a_stat")
        rstd = sem("a_rstd")
        block = ctx.enter_context(nc.Block())

        @block.sync
        def _(sp):
            def param(dst, src):
                sp.dma_start(dst, src).then_inc(par, 16)

            param(WQ[0:EH, :, :], a["wqkv"].rearrange("(h k) n -> k h n", h=2))
            param(WQ[EH:EA, 1, :], a["bqkv"].rearrange("(u n) -> u n", u=1))
            param(WGP[:, :, :], a["wgp"].rearrange("(h k) n -> k h n", h=2))
            param(WPJ[:, :, :], a["wproj"].rearrange("(h k) n -> k h n", h=2))
            param(WR[EH:EA, 1, KG + E:], a["bproj"].rearrange("(u n) -> u n", u=1))
            param(al[:, 0:1], a["alpha"].rearrange("(u n) -> u n", u=1).broadcast_to([P, 1]))

        @block.gpsimd
        def _(pool):
            pool.memset(BD[:, :, :], 0.0)
            pool.memset(eps[:, :, 0:1], 1e-5)
            pool.memset(eps[:, :, 1:2], -0.5).then_inc(zero, 1)
            pool.wait_ge(stat, 2 + 3 * PAIRS)
            pool.tensor_tensor(mv[:, :, 1:2], mv[:, :, 1:2], eps[:, :, 0:1], ALU.add).then_inc(rstd, 1)
            pool.wait_ge(rstd, 1)
            pool.tensor_tensor(mv[:, :, 1:2], mv[:, :, 1:2], eps[:, :, 1:2], ALU.pow).then_inc(rstd, 1)

        @block.tensor
        def _(pe):
            mm = nc.tensor.matmul
            pe.wait_ge(par, 16 * 6)
            for w in range(3):
                for o in range(2):
                    nc.tensor.transpose(ps[0:EH, 2 * w + o, 0:EH], WQ[0:EH, 0, E * w + EH * o:E * w + EH * o + EH], ident[0:EH, 0:EH])
                    ins = nc.tensor.transpose(ps[0:EH, 2 * w + o, EH:E + 1], WQ[:, 1, E * w + EH * o:E * w + EH * o + EH], ident[0:EA, 0:EA])
            ins.then_inc(tr, 1)
            pe.wait_ge(prep, 6)
            for i, (lo, n) in enumerate(((0, EH), (EH, EA))):
                for o in range(2):
                    mm(ps[0:n, i, 0:E + 1], WQT[:, 0, o, lo:lo + n], WQT[:, 1, o, :], start=(o == 0), stop=(o == 1))
                for o in range(2):
                    mm(ps[0:n, 2 + i, 0:KG], WQT[:, 2, o, lo:lo + n], WGP[:, o, :], start=(o == 0), stop=(o == 1))
                for o in range(2):
                    ins = mm(ps[0:n, 4 + i, 0:E], WQT[:, 2, o, lo:lo + n], WPJ[:, o, :], start=(o == 0), stop=(o == 1))
            ins.then_inc(tr, 1)
            pe.wait_ge(prep, 14)

            with pe.Fori(0, PAIRS // 2) as i2:
                j = i2 * 2
                for s in range(2):
                    pe.wait_ge(xp, j + (s + 1))
                    x = XP[:, s]
                    if s == 0:
                        pe.wait_ge(u_cp, j)
                    else:
                        pe.wait_ge(u_cp, j + 1)
                    for o, n in ((0, EH), (1, EA)):
                        for rows, h in HK:
                            ins = mm(ps[0:n, 0, P * o:P * o + P], GM[rows, h, EH * o:EH * o + n], x[rows, h, :],
                                     start=(h == 0), stop=(h == 1))
                    ins.then_inc(u_mm, 1)
                    pe.wait_ge(s_cp, j + s)
                    pe.wait_ge(glu, j + s)
                    for rows, h in HK:
                        mm(ps[:, 1, 0:KG + 2 * E], x[rows, h, :], WR[rows, h, :], start=(h == 0), stop=(h == 1))
                    pe.wait_ge(u_cp, j + (s + 1))
                    for i in range(2):
                        c = slice(SLOT * i, SLOT * i + SLOT)
                        for rows, h in HK:
                            ins = mm(ps[c, 2, 0:KG], UT[rows, s, h, c], x[rows, h, SLOT * i:SLOT * i + KG],
                                     start=(h == 0), stop=(h == 1))
                    ins.then_inc(s_mm, 1)
            pe.wait_ge(soft, 5)
            with pe.Fori(0, PAIRS // 2) as i2:
                j = i2 * 2
                for s in range(2):
                    pe.wait_ge(gt_cp, j + s)
                    pe.wait_ge(bd, j + (s + 1))
                    nc.tensor.transpose(ps[:, 0, 0:P], BD[:, s, :], ident[:, :]).then_inc(gt_mm, 1)
                    pe.wait_ge(gt_cp, j + (s + 1))
                    pe.wait_ge(gg_cp, j + s)
                    for i in range(2):
                        c = slice(SLOT * i, SLOT * i + SLOT)
                        ins = mm(ps[c, 1, 0:KG], GT[:, s, c], GT[:, s, SLOT * i:SLOT * i + KG], start=True, stop=True)
                    ins.then_inc(gg_mm, 1)
            with pe.Fori(0, PAIRS // 2) as i2:
                j = i2 * 2
                for s in range(2):
                    pe.wait_ge(bd, j + (PAIRS + s + 1))
                    pe.wait_ge(bt_cp, j + s)
                    nc.tensor.transpose(ps[:, 3, 0:P], BD[:, s, :], ident[:, :]).then_inc(bt_mm, 1)
                    pe.wait_ge(bt_cp, j + (s + 1))
                    pe.wait_ge(o_cp, j + s)
                    mm(ps[:, 2, 0:E], BT[:, s, :], VP[:, bass.ds(j + s, 1), 0:E], start=True, stop=True).then_inc(o_mm, 1)

        @block.scalar
        def _(act):
            act.wait_ge(par, 16 * 6)
            act.activation(al[:, 1:2], al[:, 0:1], ACT.Sigmoid)
            act.activation(al[:, 2:3], al[:, 0:1], ACT.Sigmoid, scale=-1.0).then_inc(ex, 1)
            with act.Fori(0, PAIRS) as j:
                act.wait_ge(s_mm, j + 1)
                act.activation(GA[:, bass.ds(j, 1), :], ps[:, 1, 0:KG], ACT.Gelu)
                act.activation(VP[:, bass.ds(j, 1), :], ps[:, 1, KG:KG + 2 * E], ACT.Copy).then_inc(glu, 1)
            act.wait_ge(soft, 2)
            act.activation(GA[:, :, :], GA[:, :, :], ACT.Exp).then_inc(ex, 1)
            act.wait_ge(soft, 7)
            act.activation(SC[:, :, :], SC[:, :, :], ACT.Exp).then_inc(ex, 1)

        @block.vector
        def _(dve):
            dve.wait_ge(tr, 1)
            for w in range(3):
                for o in range(2):
                    dve.tensor_copy(WQT[:, w, o, :], ps[0:EH, 2 * w + o, 0:E + 1]).then_inc(prep, 1)
            dve.wait_ge(tr, 2)
            for i, n in enumerate((EH, EA)):
                dve.tensor_copy(GM[0:n, i, :], ps[0:n, i, 0:E + 1]).then_inc(prep, 1)
                dve.tensor_copy(WR[0:n, i, 0:KG], ps[0:n, 2 + i, 0:KG]).then_inc(prep, 1)
                dve.tensor_copy(WR[0:n, i, KG:KG + E], ps[0:n, 4 + i, 0:E]).then_inc(prep, 1)
            dve.memset(WR[0:EH, :, KG + E:], 0.0).then_inc(prep, 1)
            dve.wait_ge(prep, 13)
            for i in range(2):
                ins = dve.tensor_copy(WR[0:EH, i, KG + E + EH * i:KG + E + EH * i + EH], ident[0:EH, 0:EH])
            ins.then_inc(prep, 1)

            with dve.Fori(0, PAIRS // 2) as i2:
                j = i2 * 2
                for s in range(2):
                    dve.wait_ge(s_mm, j)
                    dve.tensor_copy(XP[0:EH, s, 0, :], XT[0:EH, 0, bass.ds(j + s, 1), :])
                    dve.tensor_copy(XP[:, s, 1, :], XT[0:EA, 1, bass.ds(j + s, 1), :]).then_inc(xp, 1)
                for s in range(2):
                    dve.wait_ge(u_mm, j + (s + 1))
                    dve.tensor_copy(UT[0:EH, s, 0, :], ps[0:EH, 0, 0:P])
                    dve.tensor_copy(UT[:, s, 1, :], ps[0:EA, 0, P:2 * P]).then_inc(u_cp, 1)
                    dve.wait_ge(s_mm, j + (s + 1))
                    dve.tensor_scalar(SC[:, bass.ds(j + s, 1), :], ps[:, 2, 0:KG], float(E) ** -0.5, None, ALU.mult).then_inc(s_cp, 1)

            done = [0]

            def step(ins):
                done[0] += 1
                ins.then_inc(soft, 1)
                dve.wait_ge(soft, done[0])

            def wide(v):
                return v[:, :].unsqueeze(2).broadcast_to([P, PAIRS, KG])

            dve.wait_ge(glu, PAIRS)
            step(dve.tensor_reduce(red[:, :], GA[:, :, :], AX_X, ALU.max))
            step(dve.tensor_tensor(GA[:, :, :], GA[:, :, :], wide(red), ALU.subtract))
            dve.wait_ge(ex, 2)
            step(dve.tensor_reduce(red[:, :], GA[:, :, :], AX_X, ALU.add))
            step(dve.reciprocal(inv[:, :], red[:, :]))
            step(dve.tensor_tensor(GA[:, :, :], GA[:, :, :], wide(inv), ALU.mult))
            dve.wait_ge(zero, 1)
            with dve.Fori(0, PAIRS // 2) as i2:
                j = i2 * 2
                for s in range(2):
                    dve.wait_ge(gt_mm, j)
                    dve.tensor_copy(BD[:, s, 0:KG], GA[:, bass.ds(j + s, 1), :]).then_inc(bd, 1)
                for s in range(2):
                    dve.wait_ge(gt_mm, j + (s + 1))
                    dve.wait_ge(gg_mm, j)
                    dve.tensor_copy(GT[:, s, :], ps[:, 0, 0:P]).then_inc(gt_cp, 1)
                    dve.wait_ge(gg_mm, j + (s + 1))
                    dve.tensor_copy(GG[:, bass.ds(j + s, 1), :], ps[:, 1, 0:KG]).then_inc(gg_cp, 1)
            dve.wait_ge(gg_cp, PAIRS)
            dve.wait_ge(s_cp, PAIRS)
            dve.tensor_tensor(SC[:, :, :], SC[:, :, :], GG[:, :, :], ALU.mult).then_inc(stat, 1)
            dve.wait_ge(stat, 1)
            step(dve.tensor_reduce(red[:, :], SC[:, :, :], AX_X, ALU.max))
            step(dve.tensor_tensor(SC[:, :, :], SC[:, :, :], wide(red), ALU.subtract))
            dve.wait_ge(ex, 3)
            step(dve.tensor_reduce(red[:, :], SC[:, :, :], AX_X, ALU.add))
            step(dve.reciprocal(inv[:, :], red[:, :]))
            step(dve.tensor_tensor(SC[:, :, :], SC[:, :, :], wide(inv), ALU.mult))
            step(dve.tensor_scalar(SC[:, :, :], SC[:, :, :], al[:, 2:3], None, ALU.mult))
            step(dve.scalar_tensor_tensor(out=SC[:, :, :], in0=GG[:, :, :], scalar=al[:, 1:2], in1=SC[:, :, :],
                                          op0=ALU.mult, op1=ALU.add))
            dve.memset(BD[SLOT:P, :, 0:SLOT], 0.0).then_inc(stat, 1)
            dve.wait_ge(stat, 2)
            with dve.Fori(0, PAIRS // 2) as i2:
                j = i2 * 2
                for s in range(2):
                    dve.wait_ge(bt_mm, j)
                    for i in range(2):
                        r = slice(SLOT * i, SLOT * i + SLOT)
                        ins = dve.tensor_copy(BD[r, s, SLOT * i:SLOT * i + KG], SC[r, bass.ds(j + s, 1), :])
                    ins.then_inc(bd, 1)
                for s in range(2):
                    dve.wait_ge(bt_mm, j + (s + 1))
                    dve.wait_ge(o_mm, j)
                    dve.tensor_copy(BT[:, s, :], ps[:, 3, 0:P]).then_inc(bt_cp, 1)
                    dve.wait_ge(o_mm, j + (s + 1))
                    dve.tensor_tensor(yb[:, s, :].unsqueeze(1), ps[:, 2, 0:E].unsqueeze(1), VP[:, bass.ds(j + s, 1), E:],
                                      ALU.add).then_inc(o_cp, 1)
                    dve.wait_ge(o_cp, j + (s + 1))
                    dve.bn_stats(st[:, s, :], yb[:, s, :]).then_inc(stat, 1)
                    dve.wait_ge(stat, (j + s) * 3 + 3)
                    dve.memset(scratch[:, :], 0.0)
                    dve.bn_aggr(ms[:, s, :], st[:, s, :]).then_inc(stat, 1)
                    dve.tensor_copy(Y1[:, bass.ds(j + s, 1), :], yb[:, s, :].unsqueeze(1))
                    dve.wait_ge(stat, (j + s) * 3 + 4)
                    dve.tensor_copy(mv[:, bass.ds(j + s, 1), :], ms[:, s, :].unsqueeze(1)).then_inc(stat, 1)
            dve.wait_ge(rstd, 2)
            wide2 = [mv[:, :, i:i + 1].broadcast_to([P, PAIRS, E]) for i in range(2)]
            step(dve.tensor_tensor(Y1[:, :, :], Y1[:, :, :], wide2[0], ALU.subtract))
            step(dve.tensor_tensor(Y1[:, :, :], Y1[:, :, :], wide2[1], ALU.mult))


EXPERTS, HID = 4, 768
SLOTS = 256
NS = EXPERTS * SLOTS
SCH = NS // P
HH = HID // 2
UNITS = EXPERTS * 2 * 2 * 2
LAG = 2
PREP = ("y0", "y1", "l0", "l1", "t0", "t1", "exp", "w0", "w1", "w2", "w3", "w4", "w5", "dt", "c0", "c1", "d0", "d1")
PREP_AT = (0, 1, 3, 4, 6, 7, 9, 10, 11, 13, 14, 15, 17, 18, 21, 22, 23, 25)
ROTATING = 3


def unit(u):
    return u // 8, u // 4 % 2, u // 2 % 2, u % 2


def ffn_stage(first, last):
    events = []
    for u in range(UNITS + LAG):
        if u < UNITS:
            events.append(("h", u))
        if u >= LAG:
            events.append(("z", u - LAG))
            if (u - LAG) % 8 == 7:
                events.append(("ze", (u - LAG) // 8))
        if u < UNITS:
            e, old = (u // 8 - 1) % EXPERTS, u < 8
            if not (old and first):
                if u % 8 in (3, 4):
                    events.append(("zt", e, u % 8 - 3, old))
                if u % 8 in (5, 6):
                    events.append(("w2", e, u % 8 - 5, old))
                if u == 7:
                    events.append(("out",))
                if u == 10 and not first:
                    events.append(("norm",))
            if not last:
                events += [("prep", PREP[i]) for i, at in enumerate(PREP_AT) if at == u]
    if last:
        events += [("zt", 3, 0, False), ("zt", 3, 1, False), ("w2", 3, 0, False), ("w2", 3, 1, False), ("out",), ("norm",)]
    return events


def jobs_of(events):
    place, n = {}, 0
    for ev in events:
        if ev[0] == "zt" or (ev[0] == "prep" and ev[1] not in ("exp", "dt")):
            place[ev] = n
            n += 1
    return place, n


JOBS = 16
FIRST_JOBS = jobs_of(ffn_stage(True, False))[1]
STAGE_JOBS = jobs_of(ffn_stage(False, False))[1]
assert STAGE_JOBS % ROTATING == 0


def jobs_before(j, first):
    return JOBS if first else j * STAGE_JOBS + (JOBS + FIRST_JOBS - STAGE_JOBS)


def bank_of(first, n):
    return (JOBS + (0 if first else FIRST_JOBS) + n) % ROTATING


def ffn_phase(nc, a, Y1, ident, out):
    PAIRS = HALF
    KT = TOKENS
    EA = EH + 1
    HK = ((slice(0, EH), 0), (slice(0, EA), 1))
    with ExitStack() as ctx:
        def sb(name, shape, dt=F32):
            return ctx.enter_context(nc.sbuf_tensor(name, shape, dt))

        def sem(name):
            return ctx.enter_context(nc.semaphore(name))

        PH = sb("PH", [P, SCH, E])
        PT = sb("PT", [EH, 2, NS])
        W1 = sb("FW1", [EA, 2, EXPERTS * HID])
        W2 = sb("FW2", [P, EXPERTS * HID // P, E])
        B2 = sb("FB2", [P, EXPERTS, E])
        YP = sb("YP", [P, 2, E])
        YT = sb("YT", [EA, 2, 2, P])
        LS = sb("LS", [P, NS])
        C = sb("C", [P, NS])
        CT = sb("CT", [P, 2, SCH, P])
        CS = sb("CS", [P, 2, EXPERTS])
        LT = sb("LT", [P, 2 * SCH, KT])
        DT = sb("DT", [P, 2 * SCH, SLOT])
        D = sb("FD", [P, 2, NS])
        R = sb("R", [P, 2, EXPERTS * HID])
        HS = sb("HS", [P, 4, HH])
        ZS = sb("ZS", [P, 2, HID])
        ZT = sb("ZT", [P, 2, 3, P])
        mx = sb("mx", [P, 2])
        mt = sb("mt", [P, 2 * SCH])
        mi = sb("mi", [P, 2 * SCH])
        ss = sb("ss", [P, 2])
        acc = sb("acc", [P, E])
        o = sb("fo", [P, 2, E])
        st = sb("fst", [P, 6])
        scratch = sb("fscratch", [P, 1])
        mv = sb("fmv", [P, 2])
        eps = sb("feps", [P, 2])
        ps = ctx.enter_context(nc.psum_tensor("psf", [P, 8, 512], F32))
        HB, ZB, OB, MB = 0, 2, 4, 5

        par = sem("f_par")
        prep = sem("f_prep")
        tr = sem("f_tr")
        zero = sem("f_zero")
        yp = sem("f_yp")
        m_mm = sem("f_m_mm")
        m_cp = sem("f_m_cp")
        negmax = sem("f_negmax")
        c_ex = sem("f_c_ex")
        lt_sub = sem("f_lt_sub")
        lt_ex = sem("f_lt_ex")
        dt_ok = sem("f_dt_ok")
        h_mm = sem("f_h_mm")
        h_act = sem("f_h_act")
        z_mm = sem("f_z_mm")
        z_cp = sem("f_z_cp")
        w_mm = sem("f_w_mm")
        link = sem("f_link")
        olink = sem("f_olink")
        var = sem("f_var")
        rstd = sem("f_rstd")
        o_ok = sem("f_o_ok")
        o_st = sem("f_o_st")
        block = ctx.enter_context(nc.Block())
        LINKS, OLINKS, O_READ = 8, 9, 5

        def stages(eng, body):
            body(0, 0, True, False)
            with eng.Fori(0, PAIRS // 2 - 1) as i:
                for s in range(2):
                    body(i * 2 + (1 + s), (1 + s) % 2, False, False)
            body(PAIRS - 1, 1, False, True)

        @block.sync
        def _(sp):
            def param(dst, src):
                sp.dma_start(dst, src).then_inc(par, 16)

            param(PH[:, :, :], a["phi"].rearrange("e (k p) d -> p (e k) d", p=P))
            for h, lo in ((0, 0), (1, EH)):
                param(W1[0:EH, h, :].rearrange("k (e n) -> k e n", e=EXPERTS), a["fw1"][:, lo:lo + EH, :].rearrange("e k n -> k e n"))
            param(W1[EH:EA, 1, :], a["fb1"].rearrange("(u e) n -> u (e n)", u=1))
            param(W2[:, :, :], a["fw2"].rearrange("e (k p) d -> p (e k) d", p=P))
            param(B2[:, :, :], a["fb2"].rearrange("(u e) n -> u e n", u=1).broadcast_to([P, EXPERTS, E]))

            with sp.Fori(0, PAIRS // 2) as i:
                for s in range(2):
                    sp.wait_ge(o_ok, i * 2 + (s + 1))
                    for h in range(2):
                        sp.dma_start(out[bass.ds(i * 2 + (s + HALF * h), 1), :, :].rearrange("b n d -> (b n) d"),
                                     o[SLOT * h:SLOT * h + KT, s, :]).then_inc(o_st, 16)
            sp.wait_ge(o_st, 32 * PAIRS)

        @block.gpsimd
        def _(pool):
            pool.memset(DT[:, :, :], 0.0).then_inc(zero, 1)
            pool.wait_ge(zero, 1)
            pool.memset(YT[EH:EA, :, :, :], 1.0).then_inc(zero, 1)
            pool.wait_ge(zero, 2)
            pool.memset(eps[:, 0:1], 1e-5)
            pool.memset(eps[:, 1:2], -0.5).then_inc(zero, 1)
            pool.tensor_copy(YP[:, 0, :], Y1[:, 0, :]).then_inc(yp, 1)
            pool.wait_ge(zero, 3)

            def rsqrt(j):
                pool.wait_ge(var, j + 1)
                pool.tensor_tensor(mv[:, 1:2], mv[:, 1:2], eps[:, 0:1], ALU.add).then_inc(rstd, 1)
                pool.wait_ge(rstd, j * 2 + 1)
                pool.tensor_tensor(mv[:, 1:2], mv[:, 1:2], eps[:, 1:2], ALU.pow).then_inc(rstd, 1)

            def body(j, s, first, last):
                if not last:
                    pool.wait_ge(m_cp, jobs_before(j, first))
                    pool.tensor_copy(YP[:, 1 - s, :].unsqueeze(1), Y1[:, bass.ds(j + 1, 1), :]).then_inc(yp, 1)
                if not first:
                    rsqrt(j - 1)
                if last:
                    rsqrt(j)

            stages(pool, body)

        @block.tensor
        def _(pe):
            mm = nc.tensor.matmul
            pe.wait_ge(par, 16 * 6)
            for h in range(2):
                for c in range(SCH):
                    ins = nc.tensor.transpose(ps[0:EH, 2 * h + c // 4, P * (c % 4):P * (c % 4) + P],
                                              PH[:, c, EH * h:EH * h + EH], ident[:, :])
            ins.then_inc(tr, 1)
            pe.wait_ge(prep, 4)

            def routing(name, q, s, k, b, y_done):
                if name in ("exp", "dt"):
                    return
                if not (isinstance(k, int) and k < ROTATING):
                    pe.wait_ge(m_cp, k - (ROTATING - 1))
                i = int(name[1])
                if name[0] == "y":
                    pe.wait_ge(yp, q + 1)
                    ins = nc.tensor.transpose(b[0:EH, 0:P], YP[:, s, EH * i:EH * i + EH], ident[:, :])
                if name[0] == "l":
                    pe.wait_ge(m_cp, y_done)
                    for h in range(2):
                        ins = mm(b[:, :], YT[0:EH, s, h, :], PT[:, h, 512 * i:512 * i + 512], start=(h == 0), stop=(h == 1))
                if name[0] == "t":
                    for c in range(4):
                        lo = P * (4 * i + c)
                        for h in range(2):
                            ins = mm(b[:, P * c:P * c + P], PT[:, h, lo:lo + P], YT[0:EH, s, h, :], start=(h == 0), stop=(h == 1))
                if name[0] == "w":
                    for rows, h in HK:
                        ins = mm(b[:, :], YT[rows, s, h, :], W1[rows, h, 512 * i:512 * i + 512], start=(h == 0), stop=(h == 1))
                if name[0] == "c":
                    pe.wait_ge(c_ex, q + 1)
                    for c in range(4):
                        lo = P * (4 * i + c)
                        ins = nc.tensor.transpose(b[:, P * c:P * c + P], C[:, lo:lo + P], ident[:, :])
                if name[0] == "d":
                    pe.wait_ge(dt_ok, q + 1)
                    for c in range(4):
                        v = DT[:, 2 * (4 * i + c):2 * (4 * i + c) + 2, :].rearrange("p i n -> p (i n)")
                        ins = nc.tensor.transpose(b[:, P * c:P * c + P], v, ident[:, :])
                ins.then_inc(m_mm, 1)

            k = 0
            for name in PREP:
                routing(name, 0, 0, k, ps[:, MB + k % ROTATING, :], 2)
                k += name not in ("exp", "dt")

            def body(j, s, first, last):
                k0 = jobs_before(j, first)
                events = ffn_stage(first, last)
                place, _ = jobs_of(events)
                pe.wait_ge(m_cp, k0)
                for ev in events:
                    kind, n = ev[0], place.get(ev)
                    if n is not None:
                        b = ps[:, MB + bank_of(first, n), :]
                    if kind == "h":
                        e, i, half, c = unit(ev[1])
                        if not (first and ev[1] < 2):
                            pe.wait_ge(h_act, j * UNITS + (ev[1] - 1))
                        rows = slice(SLOT * i, SLOT * i + KT)
                        lo, r = SLOTS * e + P * c, HID * e + HH * half
                        mm(ps[:, HB + ev[1] % 2, 0:HH], D[rows, s, lo:lo + P], R[rows, s, r:r + HH],
                           start=True, stop=True).then_inc(h_mm, 1)
                    if kind == "z":
                        e, i, half, c = unit(ev[1])
                        pe.wait_ge(h_act, j * UNITS + (ev[1] + 1))
                        if ev[1] % 8 == 0 and not (first and e == 0):
                            pe.wait_ge(z_cp, j * EXPERTS + e)
                        rows = slice(SLOT * i, SLOT * i + SLOT)
                        mm(ps[rows, ZB + half, 0:HH], CT[:, s, 2 * e + c, rows], HS[:, ev[1] % 4, :],
                           start=(c == 0), stop=(c == 1)).then_inc(z_mm, 1)
                    if kind == "zt":
                        _, e, g, old = ev
                        pe.wait_ge(m_cp, k0 + (n - (ROTATING - 1)))
                        pe.wait_ge(z_cp, j * EXPERTS + (e + 1 - EXPERTS * old))
                        for x in range(3):
                            lo = P * (3 * g + x)
                            ins = nc.tensor.transpose(b[:, P * x:P * x + P], ZS[:, e % 2, lo:lo + P], ident[:, :])
                        ins.then_inc(m_mm, 1)
                    if kind == "w2":
                        _, e, g, old = ev
                        pe.wait_ge(m_cp, k0 + (place[("zt", e, g, old)] + 1))
                        if e == 0 and g == 0 and not first:
                            pe.wait_ge(olink, j * OLINKS + (O_READ - OLINKS))
                        for x in range(3):
                            ins = mm(ps[:, OB, 0:E], ZT[:, g, x, :], W2[:, 6 * e + 3 * g + x, :],
                                     start=(e + g + x == 0), stop=(e == 3 and g == 1 and x == 2))
                        ins.then_inc(w_mm, 1)
                    if kind == "prep":
                        y_done = k0 + (place[("prep", "y1")] + 1)
                        routing(ev[1], j + 1, 1 - s, k0 + n if n is not None else 0,
                                b if n is not None else None, y_done)

            stages(pe, body)

        @block.scalar
        def _(act):
            def exps(q, s):
                act.wait_ge(negmax, q + 1)
                for e in range(EXPERTS):
                    lo = SLOTS * e
                    ins = act.activation(C[:, lo:lo + SLOTS], LS[:, lo:lo + SLOTS], ACT.Exp, bias=mx[:, 1:2],
                                         accum_out=CS[:, s, e:e + 1])
                ins.then_inc(c_ex, 1)
                act.wait_ge(lt_sub, q + 1)
                act.activation(LT[:, :, :], LT[:, :, :], ACT.Exp).then_inc(lt_ex, 1)

            exps(0, 0)

            def body(j, s, first, last):
                for ev in ffn_stage(first, last):
                    if ev == ("prep", "exp"):
                        if not first:
                            act.wait_ge(olink, j * OLINKS + (6 - OLINKS))
                        exps(j + 1, 1 - s)
                    if ev[0] == "h":
                        u = ev[1]
                        act.wait_ge(h_mm, j * UNITS + (u + 1))
                        if not (first and u < 4):
                            act.wait_ge(z_mm, j * UNITS + (u - 3))
                        act.activation(HS[:, u % 4, :], ps[:, HB + u % 2, 0:HH], ACT.Gelu_apprx_tanh).then_inc(h_act, 1)

            stages(act, body)

        @block.vector
        def _(dve):
            dve.wait_ge(tr, 1)
            for h in range(2):
                for c in range(2):
                    dve.tensor_copy(PT[:, h, 512 * c:512 * c + 512], ps[0:EH, 2 * h + c, :]).then_inc(prep, 1)

            def job(name, q, s, k, b):
                def step(n, ins):
                    ins.then_inc(link, 1)
                    dve.wait_ge(link, q * LINKS + n)

                if name == "exp":
                    return
                if name == "dt":
                    dve.wait_ge(lt_ex, q + 1)
                    step(6, dve.tensor_reduce(mt[:, :], LT[:, :, :], AX_X, ALU.add))
                    step(7, dve.reciprocal(mi[:, :], mt[:, :]))
                    dve.tensor_tensor(DT[:, :, 0:KT], LT[:, :, :], mi[:, :].unsqueeze(2).broadcast_to([P, 2 * SCH, KT]),
                                      ALU.mult).then_inc(dt_ok, 1)
                    dve.wait_ge(dt_ok, q + 1)
                    dve.nop().then_inc(link, 1)
                    return
                i = int(name[1])
                dve.wait_ge(m_mm, k + 1)
                if name[0] == "y":
                    dve.tensor_copy(YT[0:EH, s, i, :], b[0:EH, 0:P]).then_inc(m_cp, 1)
                if name[0] == "l":
                    dve.tensor_copy(LS[:, 512 * i:512 * i + 512], b[:, :]).then_inc(m_cp, 1)
                    if i == 1:
                        dve.wait_ge(m_cp, k + 1)
                        step(1, dve.tensor_reduce(mx[:, 0:1], LS[:, :], AX_X, ALU.max))
                        dve.tensor_scalar(mx[:, 1:2], mx[:, 0:1], -1.0, None, ALU.mult).then_inc(negmax, 1)
                        dve.wait_ge(negmax, q + 1)
                        dve.nop().then_inc(link, 1)
                        dve.wait_ge(link, q * LINKS + 2)
                if name[0] == "t":
                    v = b[:, :].rearrange("p (g n) -> p g n", n=SLOT)[:, :, 0:KT]
                    g = slice(SCH * i, SCH * i + SCH)
                    step(3 + i, dve.tensor_reduce(mt[:, g], v, AX_X, ALU.max))
                    dve.tensor_tensor(LT[:, g, :], v, mt[:, g].unsqueeze(2).broadcast_to([P, SCH, KT]),
                                      ALU.subtract).then_inc(m_cp, 1)
                    if i == 1:
                        dve.wait_ge(m_cp, k + 1)
                        dve.nop().then_inc(link, 1)
                        dve.wait_ge(link, q * LINKS + 5)
                        dve.nop().then_inc(lt_sub, 1)
                if name[0] == "w":
                    dve.tensor_copy(R[:, s, 512 * i:512 * i + 512], b[:, :]).then_inc(m_cp, 1)
                if name[0] == "c":
                    dve.tensor_copy(CT[:, s, 4 * i:4 * i + 4, :], b[:, :].rearrange("p (c n) -> p c n", n=P)).then_inc(m_cp, 1)
                if name[0] == "d":
                    dve.tensor_copy(D[:, s, 512 * i:512 * i + 512], b[:, :]).then_inc(m_cp, 1)

            dve.wait_ge(zero, 3)
            dve.wait_ge(par, 16 * 6)
            k = 0
            for name in PREP:
                job(name, 0, 0, k, ps[:, MB + k % ROTATING, :])
                k += name not in ("exp", "dt")

            def end(q, s):
                def step(n, ins):
                    ins.then_inc(olink, 1)
                    dve.wait_ge(olink, q * OLINKS + n)

                step(1, dve.tensor_scalar(acc[:, :], B2[:, 0, :], CS[:, s, 0:1], None, ALU.mult))
                for e in range(1, EXPERTS):
                    step(1 + e, dve.scalar_tensor_tensor(out=acc[:, :], in0=B2[:, e, :], scalar=CS[:, s, e:e + 1], in1=acc[:, :],
                                                         op0=ALU.mult, op1=ALU.add))
                dve.wait_ge(w_mm, q * (2 * EXPERTS) + 2 * EXPERTS)
                step(O_READ, dve.tensor_tensor(acc[:, :], acc[:, :], ps[:, OB, 0:E], ALU.add))
                step(6, dve.tensor_reduce(ss[:, 0:1], CS[:, s, :], AX_X, ALU.add))
                step(7, dve.reciprocal(ss[:, 1:2], ss[:, 0:1]))
                step(8, dve.scalar_tensor_tensor(out=acc[:, :].unsqueeze(1), in0=acc[:, :].unsqueeze(1), scalar=ss[:, 1:2],
                                                 in1=Y1[:, bass.ds(q, 1), :], op0=ALU.mult, op1=ALU.add))
                step(9, dve.bn_stats(st[:, :], acc[:, :]))
                dve.memset(scratch[:, :], 0.0)
                dve.bn_aggr(mv[:, :], st[:, :]).then_inc(var, 1)

            def norm(q, s):
                dve.wait_ge(rstd, q * 2 + 2)
                dve.wait_ge(o_st, q * 32)
                dve.tensor_scalar(o[:, s, :], acc[:, :], mv[:, 0:1], mv[:, 1:2], ALU.subtract, ALU.mult).then_inc(o_ok, 1)
                dve.wait_ge(o_ok, q + 1)

            def body(j, s, first, last):
                k0 = jobs_before(j, first)
                events = ffn_stage(first, last)
                place, _ = jobs_of(events)
                for at, ev in enumerate(events):
                    kind, n = ev[0], place.get(ev)
                    if n is not None:
                        b = ps[:, MB + bank_of(first, n), :]
                    if kind == "ze":
                        dve.wait_ge(z_mm, j * UNITS + 8 * (ev[1] + 1))
                        dve.tensor_copy(ZS[:, ev[1] % 2, :].rearrange("p (h n) -> p h n", h=2), ps[:, ZB:ZB + 2, 0:HH]).then_inc(z_cp, 1)
                    if kind == "zt":
                        _, e, g, old = ev
                        dve.wait_ge(m_mm, k0 + (n + 1))
                        before = 2 * e + g - 1 - 2 * EXPERTS * old
                        if not (first and before < 1):
                            dve.wait_ge(w_mm, j * (2 * EXPERTS) + before)
                        dve.tensor_copy(ZT[:, g, :, :], b[:, 0:3 * P].rearrange("p (x n) -> p x n", n=P)).then_inc(m_cp, 1)
                    if kind == "prep":
                        job(ev[1], j + 1, 1 - s, k0 + n if n is not None else 0, b if n is not None else None)
                    if kind in ("out", "norm"):
                        now = last and at > len(events) - 3
                        q, t = (j, s) if now else (j - 1, 1 - s)
                        if kind == "out":
                            end(q, t)
                        else:
                            norm(q, t)

            stages(dve, body)


def tower(nc, a, out):
    with ExitStack() as ctx:
        ident = ctx.enter_context(nc.sbuf_tensor("ident", [P, P], F32))
        Y1 = ctx.enter_context(nc.sbuf_tensor("Y1", [P, HALF, E], F32))
        with ExitStack() as tokens:
            XT = tokens.enter_context(nc.sbuf_tensor("XT", [EH + 1, 2, HALF, P], F32))
            conv_phase(nc, a, XT, ident)
            attention_phase(nc, a, XT, Y1, ident)
        ffn_phase(nc, a, Y1, ident, out)


_NAMES = {"x": "x", "wqkv": "L0_attn_W_qkv", "bqkv": "L0_attn_b_qkv", "wproj": "L0_attn_W_proj",
          "bproj": "L0_attn_b_proj", "wgp": "L0_attn_W_gp", "alpha": "L0_attn_alpha", "phi": "L0_ffn_phi",
          "fw1": "L0_ffn_w1", "fb1": "L0_ffn_b1", "fw2": "L0_ffn_w2", "fb2": "L0_ffn_b2",
          **{n: "L0_tok_" + n for n in ("w0", "s0", "b0", "wdw", "sdw", "bdw", "wpw", "spw", "bpw",
                                        "w1", "s1", "b1", "w2", "s2", "b2", "w3", "s3", "b3")}}


def kernel(**inputs):
    import concourse.bacc as bacc
    from concourse.bass_utils import run_bass_kernel_spmd

    nc = bacc.Bacc("TRN2", target_bir_lowering=False, num_devices=1)
    arrays, a = {}, {}
    for short, name in _NAMES.items():
        v = np.ascontiguousarray(inputs[name])
        if v.ndim == 0:
            v = v.reshape(1)
        arrays[f"in_{short}"] = v
        a[short] = nc.dram_tensor(f"in_{short}", v.shape, mybir.dt.from_np(v.dtype), kind="ExternalInput").ap()
    out = nc.dram_tensor("out_tokens", (IMAGES, TOKENS, E), F32, kind="ExternalOutput").ap()
    tower(nc, a, out)
    r = run_bass_kernel_spmd(nc, [arrays], core_ids=[0])
    return r.results[0]["out_tokens"]
```

```python
from contextlib import ExitStack

import numpy as np
import concourse.bass as bass
from concourse import mybir

F32 = mybir.dt.float32
F32R = mybir.dt.float32r
ALU = mybir.AluOpType
ACT = mybir.ActivationFunctionType
AX_X = mybir.AxisListType.X

P = 128
IMAGES, CIN, SIDE = 64, 3, 112
GRID = 7
RS = SIDE // GRID
CH = 12
CB = P // RS
CR = CH - CB
REGIONS = GRID * GRID
HALF = IMAGES // 2
E = 192
EH = E // 2
C2 = 48
TOKENS = GRID * GRID
HALO = RS + 2
KX = CIN * HALO
KLO = 64
KS = KLO + KX
XW = SIDE + 2
GW = RS + 2
BC = 4
CHUNKS = HALF // BC
NREG = HALF * RS
Q = RS // 4
SLOT = 64
TW = 441 + REGIONS + 588 + REGIONS
O_DW, O_BDW, O_PW, O_BPW = 0, 441, 490, 1078


def conv_phase(nc, a, XT, Y1, ident):
    x = a["x"]
    with ExitStack() as ctx:
        def sb(name, shape, dt=F32):
            return ctx.enter_context(nc.sbuf_tensor(name, shape, dt))

        def sem(name):
            return ctx.enter_context(nc.semaphore(name))

        X = sb("X", [KX, 2, HALF, XW])
        XS = sb("XS", [KS, 2, 2, BC, XW], F32R)
        G = sb("G", [P, 3, HALF, GRID, GW])
        D = sb("D", [P, 2, 3, NREG])
        space = Y1[:, :, :].rearrange("p j d -> p (j d)")
        H1 = space[0:96, 0:3584].rearrange("p (t h b x) -> p t h b x", t=2, h=2, b=HALF)
        H2 = space[0:96, 3584:4480].rearrange("p (h b x) -> p h b x", h=2, b=HALF)
        W0 = sb("W0", [KS, 2, 3, 5 * 64], F32R)
        WD = sb("WD", [P, 2, 2, 3, P])
        WP = sb("WP", [P, 2, 448])
        W1 = sb("W1", [P, 2, 2, 4, 96])
        W2 = sb("W2", [96, 2, 2, 96])
        W3 = sb("W3", [96, 2, 2, 96])
        AC = sb("AC", [P, 2, GRID, 3, RS])
        ACt = sb("ACt", [P, GRID, 3, RS])
        TAB = sb("TAB", [P, 2, TW])
        BV = sb("BV", [P, 2, 2, GRID])
        mY = sb("mY", [P, HALO])
        mX = sb("mX", [KS, HALO])
        mC = sb("mC", [P, CB])
        m4 = sb("m4", [P, Q])
        SEL = space[0:C2, 4480:5120].rearrange("p (s n) -> p s n", n=P)
        b0v = sb("b0v", [P, 2])
        b1v = sb("b1v", [96, 1])
        b2v = sb("b2v", [96, 1])
        b3v = sb("b3v", [96, 2])
        raw = H1[:, :, :, :, :].rearrange("p t h b x -> p (t h b x)")
        T12 = raw[0:CH, 1344:1344 + TW]
        s12 = raw[0:CH, 2471:2471 + REGIONS + 588]
        w0s = sb("w0s", [CIN, CH, 9])
        s0s = sb("s0s", [CIN, CH])
        w1s = raw[0:C2, 0:192]
        w2s = raw[0:C2, 192:384]
        w3s = raw[:, 384:768].rearrange("o (h n) -> o h n", h=2)
        w2p = raw[0:C2, 768:960].rearrange("o (x y c) -> o x y c", x=2, y=2)
        w3p = raw[:, 960:1344].rearrange("o (h x y c) -> o h x y c", h=2, x=2, y=2)
        s123 = sb("s123", [96, 4])
        b0s = sb("b0s", [CH, 1])
        w1t = raw[0:C2, 3108:3300].rearrange("p (k o) -> p k o", k=4)
        w0c = sb("w0c", [CIN, 9, CH])
        zrow = sb("zrow", [1, SIDE])
        ps = ctx.enter_context(nc.psum_tensor("ps", [P, 8, 512], F32))
        CST_DONE = 21
        PREP_DONE = 72
        SCALED = 14
        TRANSPOSED = SCALED + 6 + 1 + 15 + 2 + 4 + 4 + 6
        TSPLIT = ((0, 490), (490, 980), (980, TW))
        X0, X1 = (D[0:KS, s, :, 0:CH * RS].rearrange("p t (c y) -> p t c y", y=RS) for s in range(2))

        x_cleared = sem("x_cleared")
        x_loaded = sem("x_loaded")
        x_hi = sem("x_hi")
        x_split = sem("x_split")
        par = sem("par")
        cst = sem("cst")
        prep = sem("prep")
        tr = sem("tr")
        c0_mm = sem("c0_mm")
        c0_act = sem("c0_act")
        wt = sem("wt")
        dw_mm = sem("dw_mm")
        dw_act = sem("dw_act")
        pw_mm = sem("pw_mm")
        pw_add = sem("pw_add")
        g3 = sem("g3")
        c1_mm = sem("c1_mm")
        c1_act = sem("c1_act")
        c3_dve = sem("c3_dve")
        chained = sem("chained")
        block = ctx.enter_context(nc.Block())
        NPAR = 26

        @block.sync
        def _(sp):
            def rows(gy_row, first, last):
                for h in range(2):
                    for c in range(CIN):
                        src = x[h * HALF:(h + 1) * HALF, c]
                        p = c * HALO
                        sp.dma_start(X[p + 1:p + 1 + RS, h, :, 1:1 + SIDE],
                                     src[:, bass.ds(gy_row, RS), :].rearrange("b y x -> y b x")).then_inc(x_loaded, 16)
                        if not first:
                            sp.dma_start(X[p:p + 1, h, :, 1:1 + SIDE],
                                         src[:, bass.ds(gy_row - 1, 1), :].rearrange("b y x -> y b x")).then_inc(x_loaded, 16)
                        if not last:
                            sp.dma_start(X[p + HALO - 1:p + HALO, h, :, 1:1 + SIDE],
                                         src[:, bass.ds(gy_row + RS, 1), :].rearrange("b y x -> y b x")).then_inc(x_loaded, 16)
                        else:
                            sp.dma_start(X[p + HALO - 1:p + HALO, h, :, 1:1 + SIDE],
                                         zrow[0:1, :].unsqueeze(1).broadcast_to([1, HALF, SIDE])).then_inc(x_loaded, 16)

            sp.wait_ge(x_cleared, 1)
            rows(0, True, False)
            with sp.Fori(1, GRID - 1) as gy:
                sp.wait_ge(x_split, gy * CHUNKS)
                rows(gy * RS, False, False)
            sp.wait_ge(x_split, (GRID - 1) * CHUNKS)
            rows((GRID - 1) * RS, False, True)

        @block.scalar
        def _(act):
            def param(dst, src):
                act.dma_start(dst, src, allow_slow_non_contiguous=True).then_inc(par, 16)

            param(w0s[:, :, :], a["w0"].rearrange("o c a b -> c o (a b)"))
            param(s0s[:, :], a["s0"].rearrange("(a o) -> a o", a=1).broadcast_to([CIN, CH]))
            param(T12[:, O_DW:O_BDW].rearrange("c (r t) -> c r t", t=9), a["wdw"].rearrange("(r c) u a b -> c r (u a b)", c=CH))
            param(s12[:, 0:REGIONS], a["sdw"].rearrange("(r c) -> c r", c=CH))
            param(T12[:, O_BDW:O_PW], a["bdw"].rearrange("(r c) -> c r", c=CH))
            param(T12[:, O_BPW:TW], a["bpw"].rearrange("(r c) -> c r", c=CH))
            param(T12[:, O_PW:O_BPW], a["wpw"].rearrange("q c u v -> c (q u v)"))
            param(s12[:, REGIONS:], a["spw"].rearrange("(a q) -> a q", a=1).broadcast_to([CH, 588]))
            param(b0s[:, :], a["b0"].rearrange("(c u) -> c u", u=1))
            param(w1s[:, :], a["w1"].rearrange("o c a b -> o (c a b)"))
            param(w2s[:, :], a["w2"].rearrange("o c a b -> o (c a b)"))
            param(w3s[:, :, :], a["w3"].rearrange("(h o) c a b -> o h (c a b)", h=2))
            param(s123[0:C2, 0:1], a["s1"].rearrange("(c u) -> c u", u=1))
            param(s123[0:C2, 1:2], a["s2"].rearrange("(c u) -> c u", u=1))
            param(s123[:, 2:4], a["s3"].rearrange("(h o) -> o h", h=2))
            param(b3v[:, :], a["b3"].rearrange("(h o) -> o h", h=2))
            for h in range(2):
                param(b1v[C2 * h:C2 * h + C2, :], a["b1"].rearrange("(c u) -> c u", u=1))
                param(b2v[C2 * h:C2 * h + C2, :], a["b2"].rearrange("(c u) -> c u", u=1))

            act.nop().then_inc(dw_act, 1)
            act.wait_ge(prep, PREP_DONE)
            with act.Fori(0, GRID) as gy:
                for c in range(CHUNKS):
                    s = c % 2 * 3
                    act.wait_ge(c0_mm, gy * CHUNKS + 1 + c + 1)
                    for t in range(3):
                        k = t // 2
                        dst = G[:, t, BC * c:BC * c + BC, :, 1:1 + RS]
                        src = ps[:, s + t, 0:BC * SIDE].rearrange("p (b g x) -> p b g x", b=BC, g=GRID)
                        ins = act.activation(dst, src, ACT.Gelu, bias=b0v[:, k:k + 1])
                    ins.then_inc(c0_act, 1)

                def last_gelu(g):
                    for t in range(3):
                        act.wait_ge(pw_add, gy * 21 + 1 + 3 * g + t + 1)
                        v = G[:, t, :, g, 1:1 + RS]
                        act.activation(v, v, ACT.Gelu).then_inc(g3, 1)

                for g in range(GRID):
                    act.wait_ge(wt, gy * GRID + 1 + g + 1)
                    for t in range(3):
                        act.wait_ge(dw_mm, gy * 21 + 3 * g + t + 1)
                        if g >= 2:
                            act.wait_ge(pw_mm, gy * 21 + 1 + 3 * (g - 1))
                        act.activation(D[:, g % 2, t, :], ps[:, t, :], ACT.Gelu,
                                       bias=BV[:, 0, t // 2, g:g + 1]).then_inc(dw_act, 1)
                    if g >= 1:
                        last_gelu(g - 1)
                last_gelu(GRID - 1)
                n = 0
                for h in range(2):
                    for t in range(2):
                        for i in range(2):
                            act.wait_ge(c1_mm, gy * 12 + 1 + n + 1)
                            act.activation(H1[:, t, h, 16 * i:16 * i + 16, :],
                                           ps[0:96, 6 + n % 2, 0:448].rearrange("p (b x) -> p b x", b=16),
                                           ACT.Gelu, bias=b1v[:, 0:1]).then_inc(c1_act, 1)
                            n += 1
                for h in range(2):
                    act.wait_ge(c1_mm, gy * 12 + 1 + n + 1)
                    act.activation(H2[:, h, :, :], ps[0:96, 6 + n % 2, 0:448].rearrange("p (b x) -> p b x", b=HALF),
                                   ACT.Gelu, bias=b2v[:, 0:1]).then_inc(c1_act, 1)
                    n += 1

        @block.gpsimd
        def _(pool):
            n = [0]

            def step(ins):
                n[0] += 1
                ins.then_inc(cst, 1)
                pool.wait_ge(cst, n[0])

            def mark(v, pattern, base, slope):
                step(pool.affine_select(out=v, in_=v, compare_op=ALU.not_equal, fill=1.0, base=base,
                                        pattern=pattern, channel_multiplier=slope))

            pool.memset(zrow[:, :], 0.0)
            pool.memset(X[:, :, :, :], 0.0).then_inc(x_cleared, 1)
            pool.wait_ge(x_cleared, 1)
            step(pool.memset(ident[:, :], 0.0))
            mark(ident[:, :], [[-1, P]], 0, 1)
            step(pool.memset(mY[:, :], 0.0))
            step(pool.memset(SEL[:, :, :], 0.0))
            mark(SEL[0:CH, 0, :].rearrange("c (j y) -> c j y", y=RS), [[-1, CB], [0, RS]], 0, 1)
            mark(SEL[0:CH, 1, :].rearrange("c (h j y) -> c h j y", h=2, y=RS), [[0, 2], [-1, CR], [0, RS]], -CB, 1)
            for lo in (0, KLO):
                mark(SEL[0:CIN, 2, lo:lo + KX].rearrange("c (j y) -> c j y", y=HALO), [[-1, CIN], [0, HALO]], 0, 1)
            mark(SEL[:, 3, :].rearrange("c (j y r) -> c j y r", j=CB, r=4), [[-4, CB], [0, Q], [-1, 4]], 0, 1)
            for h in range(2):
                mark(SEL[:, 4, 64 * h:64 * h + 64].rearrange("c (j y r) -> c j y r", j=CR, r=4),
                     [[-4, CR], [0, Q], [-1, 4]], -4 * CB, 1)
            step(pool.memset(mC[:, :], 1.0))
            step(pool.affine_select(out=mC[:, :], in_=mC[:, :], compare_op=ALU.is_ge, fill=0.0,
                                    base=0, pattern=[[-RS, CB]], channel_multiplier=1))
            step(pool.affine_select(out=mC[:, :], in_=mC[:, :], compare_op=ALU.is_ge, fill=0.0,
                                    base=RS - 1, pattern=[[RS, CB]], channel_multiplier=-1))
            step(pool.memset(WP[:, :, :], 0.0))
            step(pool.memset(W2[:, :, :, :], 0.0))
            step(pool.memset(G[:, :, :, :, 0:1], 0.0))
            step(pool.memset(G[:, :, :, :, GW - 1:GW], 0.0))
            step(pool.memset(XT[:, :, :, :], 0.0))
            step(pool.memset(XT[96:97, 1, :, :], 1.0))
            step(pool.memset(D[:, :, :, :], 0.0))
            assert n[0] == CST_DONE, n[0]

        @block.vector
        def _(dve):
            n = [0]

            def step(ins, wait=True):
                n[0] += 1
                ins.then_inc(prep, 1)
                if wait:
                    dve.wait_ge(prep, n[0])

            for s_ in (pw_add, wt, c3_dve):
                dve.nop().then_inc(s_, 1)
            dve.wait_ge(cst, CST_DONE)
            step(dve.tensor_reduce(mY[:, 1:1 + RS], ident[:, :].rearrange("p (j y) -> p y j", y=RS), AX_X, ALU.add))
            step(dve.tensor_tensor(mX[:, :], ident[0:KS, 0:HALO], ident[0:KS, HALO:2 * HALO], ALU.add))
            for j in (2 * HALO, KLO, KLO + HALO, KLO + 2 * HALO):
                step(dve.tensor_tensor(mX[:, :], mX[:, :], ident[0:KS, j:j + HALO], ALU.add))
            step(dve.tensor_reduce(m4[:, :], mY[:, 1:1 + RS].rearrange("p (j r) -> p j r", r=4), AX_X, ALU.add))
            dve.wait_ge(par, 16 * 20)
            v = T12[:, O_DW:O_BDW].rearrange("c (r t) -> c r t", t=9)
            step(dve.tensor_tensor(v, v, s12[:, 0:REGIONS].unsqueeze(2).broadcast_to([CH, REGIONS, 9]), ALU.mult))
            v = T12[:, O_PW:O_BPW]
            step(dve.tensor_tensor(v, v, s12[:, REGIONS:], ALU.mult))
            step(dve.tensor_tensor(w0c[:, :, :], w0s[:, :, :].rearrange("c o t -> c t o"),
                                   s0s[:, :].unsqueeze(1).broadcast_to([CIN, 9, CH]), ALU.mult))
            step(dve.tensor_scalar(w1s[:, :], w1s[:, :], s123[0:C2, 0:1], None, ALU.mult))
            step(dve.tensor_scalar(w2p[:, :, :, :], w2s[:, :].rearrange("o (c y x) -> o x y c", y=2, x=2),
                                   s123[0:C2, 1:2], None, ALU.mult))
            for h in range(2):
                step(dve.tensor_scalar(w3p[:, h], w3s[:, h, :].rearrange("o (c y x) -> o x y c", y=2, x=2),
                                       s123[:, 2 + h:3 + h], None, ALU.mult))
            assert n[0] == SCALED, n[0]
            dve.wait_ge(tr, 1)
            for k in range(2):
                for j, (lo, hi) in enumerate(TSPLIT):
                    step(dve.tensor_copy(TAB[:, k, lo:hi], ps[:, 3 * k + j, 0:hi - lo]), False)
            dve.wait_ge(tr, 2)
            step(dve.tensor_copy(b0v[:, :], ps[:, 7, 0:2]), False)
            w0r = ps[0:KS, 6, 0:9 * CH].rearrange("p (y x c) -> p y x c", y=3, x=3)
            for dx in range(3):
                for dy in range(3):
                    m = mX[:, dy:dy + RS].unsqueeze(1).broadcast_to([KS, CH, RS])
                    w = w0r[:, dy, dx, :].unsqueeze(2).broadcast_to([KS, CH, RS])
                    if dy == 0:
                        step(dve.tensor_tensor(X0[:, dx], w, m, ALU.mult))
                    else:
                        step(dve.tensor_tensor(X1[:, dx], w, m, ALU.mult))
                        step(dve.tensor_tensor(X0[:, dx], X0[:, dx], X1[:, dx], ALU.add))
            zeros = D[0:KS, 1, :, CH * RS:CH * RS + 320]
            for part in range(2):
                step(dve.tensor_copy(W0[:, part, :, :], zeros))
            full = D[0:KS, 0, :, 0:CH * RS]
            for lo, n_, to in ((0, P, 0), (P, 64, 192)):
                hi, v = W0[:, 0, :, to:to + n_], full[:, :, lo:lo + n_]
                step(dve.tensor_copy(hi, v))
                step(dve.tensor_tensor(W0[:, 1, :, to:to + n_], v, hi.bitcast(F32), ALU.subtract))
            for slot in range(2):
                for h in range(2):
                    step(dve.tensor_copy(XS[:, slot, h].rearrange("p b x -> p (b x)"), D[0:KS, 1, 0, 0:1].broadcast_to([KS, BC * XW])))
            dve.wait_ge(tr, 3)
            step(dve.tensor_copy(w1t[:, :, :], ps[0:C2, 0, 0:4 * C2].rearrange("p (k o) -> p k o", k=4)), False)
            for kx in range(2):
                for t in range(2):
                    step(dve.tensor_copy(W2[:, t, kx, C2 * t:C2 * t + C2], ps[0:96, 1, C2 * kx:C2 * kx + C2]), False)
            step(dve.tensor_copy(W3[:, :, :, :], ps[0:96, 2, 0:384].rearrange("p (k h o) -> p k h o", k=2, h=2)), False)
            assert n[0] == TRANSPOSED, n[0]
            dve.wait_ge(tr, 4)
            for k in range(2):
                for t in range(2):
                    for q in range(2):
                        step(dve.tensor_scalar(W1[:, k, t, :, C2 * q:C2 * q + C2],
                                               ps[:, 3 + k, 0:4 * C2].rearrange("p (k o) -> p k o", k=4),
                                               m4[:, 2 * t + q:2 * t + q + 1], None, ALU.mult), False)
            dve.wait_ge(prep, n[0])
            while n[0] < PREP_DONE:
                step(dve.nop(), False)
            assert n[0] == PREP_DONE, n[0]

            with dve.Fori(0, GRID) as gy:
                done = [0]

                def chain(ins):
                    done[0] += 1
                    ins.then_inc(chained, 1)
                    dve.wait_ge(chained, gy * 10 + done[0])

                def split(c):
                    if c >= 2:
                        dve.wait_ge(c0_mm, gy * CHUNKS + 1 + c - 1)
                    v = X[:, :, BC * c:BC * c + BC, :]
                    hi = XS[0:KX, c % 2]
                    for h in range(2):
                        ins = dve.tensor_copy(hi[:, h], v[:, h])
                    ins.then_inc(x_hi, 1)
                    dve.wait_ge(x_hi, gy * CHUNKS + c + 1)
                    for h in range(2):
                        ins = dve.tensor_tensor(XS[KLO:KS, c % 2, h], v[:, h], hi[:, h].bitcast(F32), ALU.subtract)
                    ins.then_inc(x_split, 1)

                dve.wait_ge(x_loaded, gy * (16 * 18) + 16 * 12)
                dve.wait_ge(c0_mm, gy * CHUNKS + 1)
                split(0)
                split(1)
                dve.wait_ge(pw_add, gy * 21 + 1)
                dve.wait_ge(dw_act, gy * 21 + 1)
                dve.wait_ge(wt, gy * GRID + 1)
                dve.wait_ge(pw_mm, gy * 21 + 1)
                for i, o in enumerate((O_BDW, O_BPW)):
                    dve.tensor_copy(BV[:, i], TAB[:, :, bass.ds(gy * GRID + o, GRID)])
                for k in range(2):
                    r = TAB[:, k, bass.ds(gy * (GRID * 9), GRID * 9)].rearrange("p (g y x) -> p g y x", g=GRID, y=3)
                    for dy in range(3):
                        m = mY[:, dy:dy + RS].unsqueeze(1).unsqueeze(1).broadcast_to([P, GRID, 3, RS])
                        w = r[:, :, dy, :].unsqueeze(3).broadcast_to([P, GRID, 3, RS])
                        if dy == 0:
                            chain(dve.tensor_tensor(AC[:, k], w, m, ALU.mult))
                        else:
                            chain(dve.tensor_tensor(ACt[:, :, :, :], w, m, ALU.mult))
                            chain(dve.tensor_tensor(AC[:, k], AC[:, k], ACt[:, :, :, :], ALU.add))

                def matrices(g):
                    s = g % 2
                    if g >= 2:
                        dve.wait_ge(pw_mm, gy * 21 + 1 + 3 * (g - 1))
                    for k in range(2):
                        dve.tensor_tensor(WD[:, s, k].rearrange("p x (c y) -> p x c y", y=RS),
                                          AC[:, k, g].unsqueeze(2).broadcast_to([P, 3, CB, RS]),
                                          mC[:, :].unsqueeze(1).unsqueeze(3).broadcast_to([P, 3, CB, RS]), ALU.mult)
                    my = mY[:, 1:1 + RS]
                    for k, col, lo, n_, rows_ in ((0, 0, 0, CH, slice(0, P)), (1, 192, 0, CB, slice(0, P)),
                                                  (1, 320, CB, CR, slice(0, 64)), (1, 384, CB, CR, slice(64, P))):
                        np_ = rows_.stop - rows_.start
                        w = TAB[rows_, k, bass.ds(gy * (GRID * CH) + (O_PW + g * CH + lo), n_)]
                        ins = dve.tensor_tensor(WP[rows_, s, col:col + RS * n_].rearrange("p (c y) -> p c y", y=RS),
                                                w.unsqueeze(2).broadcast_to([np_, n_, RS]),
                                                my[rows_].unsqueeze(1).broadcast_to([np_, n_, RS]), ALU.mult)
                    ins.then_inc(wt, 1)

                def add(g):
                    for t in range(3):
                        dve.wait_ge(pw_mm, gy * 21 + 1 + 3 * g + t + 1)
                        v = G[:, t, :, g, 1:1 + RS]
                        dve.scalar_tensor_tensor(out=v, in0=ps[:, 3 + t, :].rearrange("p (b x) -> p b x", b=HALF),
                                                 scalar=BV[:, 1, t // 2, g:g + 1], in1=v,
                                                 op0=ALU.add, op1=ALU.add).then_inc(pw_add, 1)

                for c in range(2, CHUNKS):
                    split(c)
                    if c >= CHUNKS - 2:
                        matrices(c - (CHUNKS - 2))
                for g in range(GRID):
                    add(g)
                    if g + 2 < GRID:
                        matrices(g + 2)
                for o in range(2):
                    dve.wait_ge(c1_mm, gy * 12 + 1 + 11 + o)
                    for h in range(2):
                        dve.tensor_scalar(XT[0:96, o, :, bass.ds(gy * GRID + SLOT * h, GRID)],
                                          ps[0:96, 6 + o, 224 * h:224 * h + 224].rearrange("p (b x) -> p b x", b=HALF),
                                          b3v[:, o:o + 1], None, ALU.add).then_inc(c3_dve, 1)

        @block.tensor
        def _(pe):
            mm = nc.tensor.matmul
            for s in (pw_mm, c1_mm, c0_mm):
                pe.nop().then_inc(s, 1)
            pe.wait_ge(prep, SCALED)
            for k in range(2):
                for j, (lo, hi) in enumerate(TSPLIT):
                    ins = mm(ps[:, 3 * k + j, 0:hi - lo], SEL[0:CH, k, :], T12[:, lo:hi], start=True, stop=True)
            ins.then_inc(tr, 1)
            mm(ps[0:KS, 6, 0:9 * CH], SEL[0:CIN, 2, 0:KS], w0c[:, :, :].rearrange("c t o -> c (t o)"), start=True, stop=True)
            for k in range(2):
                ins = mm(ps[:, 7, k:k + 1], SEL[0:CH, k, :], b0s[:, :], start=True, stop=True)
            ins.then_inc(tr, 1)
            pe.wait_ge(prep, SCALED + 6)
            for kx in range(4):
                nc.tensor.transpose(ps[0:C2, 0, C2 * kx:C2 * kx + C2], w1s[:, kx:kx + 4 * (C2 - 1) + 1:4], ident[0:C2, 0:C2])
            for kx in range(2):
                v = w2p[:, kx].rearrange("o y c -> o (y c)")
                nc.tensor.transpose(ps[0:96, 1, C2 * kx:C2 * kx + C2], v, ident[0:C2, 0:C2])
                for h in range(2):
                    v = w3p[:, h, kx].rearrange("o y c -> o (y c)")
                    ins = nc.tensor.transpose(ps[0:96, 2, 192 * kx + 96 * h:192 * kx + 96 * h + 96], v, ident[0:96, 0:96])
            ins.then_inc(tr, 1)
            pe.wait_ge(prep, TRANSPOSED)
            for k in range(2):
                ins = mm(ps[:, 3 + k, 0:4 * C2], SEL[:, 3 + k, :], w1t[:, :, :].rearrange("p k o -> p (k o)"), start=True, stop=True)
            ins.then_inc(tr, 1)
            pe.wait_ge(prep, PREP_DONE)
            with pe.Fori(0, GRID) as gy:
                for c in range(CHUNKS):
                    s = c % 2 * 3
                    if c == 0:
                        pe.wait_ge(dw_act, gy * 21 + 1)
                        pe.wait_ge(c1_mm, gy * 12 + 1)
                    elif c == 1:
                        pe.wait_ge(pw_add, gy * 21 + 1)
                    else:
                        pe.wait_ge(c0_act, gy * CHUNKS + c - 1)
                    pe.wait_ge(x_split, gy * CHUNKS + c + 1)
                    for out, h, lo, first, last in ((ps[:, s], 0, 0, True, True), (ps[:, s + 1], 1, 0, True, True),
                                                    (ps[:, s + 2], 0, 192, True, False), (ps[:, s + 2], 1, P, False, True)):
                        for kx in range(3):
                            for part in range(2):
                                ins = mm(out[:, 0:BC * SIDE], W0[:, part, kx, lo:lo + P], XS[:, c % 2, h, :, kx:kx + SIDE],
                                         start=(first and kx + part == 0), stop=(last and kx + part == 3))
                    ins.then_inc(c0_mm, 1)

                def depthwise(g):
                    pe.wait_ge(wt, gy * GRID + 1 + g + 1)
                    for t in range(3):
                        if g == 0:
                            pe.wait_ge(c0_act, gy * CHUNKS + CHUNKS)
                        else:
                            pe.wait_ge(dw_act, gy * 21 + 1 + 3 * (g - 1) + t + 1)
                        for kx in range(3):
                            ins = mm(ps[:, t, :], WD[:, g % 2, t // 2, kx, :], G[:, t, :, g, kx:kx + RS],
                                     start=(kx == 0), stop=(kx == 2))
                        ins.then_inc(dw_mm, 1)

                def pointwise(g):
                    w = WP[:, g % 2, :]
                    d = D[:, g % 2]
                    for t in range(2):
                        pe.wait_ge(dw_act, gy * 21 + 1 + 3 * g + 3)
                        if g >= 1:
                            pe.wait_ge(pw_add, gy * 21 + 1 + 3 * (g - 1) + t + 1)
                        half = slice(64 * t, 64 * t + 64)
                        mm(ps[:, 3 + t, :], w[:, 0:P], d[:, t, :], start=True, stop=False)
                        mm(ps[:, 3 + t, :], w[half, 192:320], d[half, 2, :], start=False, stop=True).then_inc(pw_mm, 1)
                    if g >= 1:
                        pe.wait_ge(pw_add, gy * 21 + 1 + 3 * g)
                    mm(ps[:, 5, :], w[:, 320:448], d[:, 2, :], start=True, stop=False)
                    mm(ps[0:64, 5, :], w[:, P:192], d[:, 0, :], start=False, stop=True)
                    mm(ps[64:P, 5, :], w[:, P:192], d[:, 1, :], start=False, stop=True).then_inc(pw_mm, 1)

                depthwise(0)
                for g in range(GRID):
                    if g + 1 < GRID:
                        depthwise(g + 1)
                    pointwise(g)
                pe.wait_ge(g3, gy * 21 + 21)
                n = 0
                for h in range(2):
                    for t in range(2):
                        for i in range(2):
                            if n < 2:
                                pe.wait_ge(c3_dve, gy * 4 + 1)
                            else:
                                pe.wait_ge(c1_act, gy * 10 + n - 1)
                            out = ps[0:96, 6 + n % 2, 0:448]
                            b = slice(16 * i, 16 * i + 16)
                            half = slice(64 * h, 64 * h + 64)
                            for kx in range(4):
                                big = G[:, h, b, :, 1 + kx:1 + RS:4]
                                rest = G[half, 2, b, :, 1 + kx:1 + RS:4]
                                mm(out, W1[:, 0, t, kx, :], big, start=(kx == 0), stop=False)
                                ins = mm(out, W1[half, 1, t, kx, :], rest, start=False, stop=(kx == 3))
                            ins.then_inc(c1_mm, 1)
                            n += 1
                for h in range(2):
                    pe.wait_ge(c1_act, gy * 10 + 4 * h + 4)
                    pe.wait_ge(c1_act, gy * 10 + n - 1)
                    out = ps[0:96, 6 + n % 2, 0:448]
                    for t in range(2):
                        for kx in range(2):
                            ins = mm(out, W2[:, t, kx, :], H1[:, t, h, :, kx:28:2], start=(t + kx == 0), stop=(t + kx == 2))
                    ins.then_inc(c1_mm, 1)
                    n += 1
                pe.wait_ge(c1_act, gy * 10 + 10)
                for o in range(2):
                    for h in range(2):
                        for kx in range(2):
                            ins = mm(ps[0:96, 6 + o, 224 * h:224 * h + 224], W3[:, kx, o, :], H2[:, h, :, kx:14:2],
                                     start=(kx == 0), stop=(kx == 1))
                    ins.then_inc(c1_mm, 1)


def attention_phase(nc, a, XT, Y1, ident):
    PAIRS = HALF
    KG = 49
    EA = EH + 1
    HK = ((slice(0, EH), 0), (slice(0, EA), 1))
    with ExitStack() as ctx:
        def sb(name, shape, dt=F32):
            return ctx.enter_context(nc.sbuf_tensor(name, shape, dt))

        def sem(name):
            return ctx.enter_context(nc.semaphore(name))

        WQ = sb("WQ", [EA, 2, 3 * E])
        WQT = sb("WQT", [EH, 3, 2, E + 1])
        WGP = sb("WGP", [EH, 2, KG])
        WPJ = sb("WPJ", [EH, 2, E])
        GM = sb("GM", [EA, 2, E + 1])
        WR = sb("WR", [EA, 2, KG + 2 * E])
        XP = sb("XP", [EA, 2, 2, P])
        UT = sb("UT", [EA, 2, 2, P])
        VP = sb("VP", [P, PAIRS, 2 * E])
        SC = sb("SC", [P, PAIRS, KG])
        GA = sb("GA", [P, PAIRS, KG])
        GG = sb("GG", [P, PAIRS, KG])
        GT = sb("GT", [P, 2, P])
        red = sb("red", [P, PAIRS])
        inv = sb("inv", [P, PAIRS])
        al = sb("al", [P, 3])
        BD = sb("BD", [P, 2, P])
        BT = sb("BT", [P, 2, P])
        st = sb("st", [P, 2, 6])
        ms = sb("ms", [P, 2, 2])
        yb = sb("yb", [P, 2, E])
        scratch = sb("scratch", [P, 1])
        mv = sb("mv", [P, PAIRS, 2])
        eps = sb("eps", [P, PAIRS, 2])
        ps = ctx.enter_context(nc.psum_tensor("psa", [P, 8, 512], F32))

        par = sem("a_par")
        prep = sem("a_prep")
        tr = sem("a_tr")
        zero = sem("a_zero")
        xp = sem("a_xp")
        u_mm = sem("a_u_mm")
        u_cp = sem("a_u_cp")
        s_mm = sem("a_s_mm")
        s_cp = sem("a_s_cp")
        glu = sem("a_glu")
        soft = sem("a_soft")
        ex = sem("a_ex")
        gt_mm = sem("a_gt_mm")
        gt_cp = sem("a_gt_cp")
        gg_mm = sem("a_gg_mm")
        gg_cp = sem("a_gg_cp")
        bd = sem("a_bd")
        bt_mm = sem("a_bt_mm")
        bt_cp = sem("a_bt_cp")
        o_mm = sem("a_o_mm")
        o_cp = sem("a_o_cp")
        stat = sem("a_stat")
        rstd = sem("a_rstd")
        block = ctx.enter_context(nc.Block())

        @block.sync
        def _(sp):
            def param(dst, src):
                sp.dma_start(dst, src).then_inc(par, 16)

            param(WQ[0:EH, :, :], a["wqkv"].rearrange("(h k) n -> k h n", h=2))
            param(WQ[EH:EA, 1, :], a["bqkv"].rearrange("(u n) -> u n", u=1))
            param(WGP[:, :, :], a["wgp"].rearrange("(h k) n -> k h n", h=2))
            param(WPJ[:, :, :], a["wproj"].rearrange("(h k) n -> k h n", h=2))
            param(WR[EH:EA, 1, KG + E:], a["bproj"].rearrange("(u n) -> u n", u=1))
            param(al[:, 0:1], a["alpha"].rearrange("(u n) -> u n", u=1).broadcast_to([P, 1]))

        @block.gpsimd
        def _(pool):
            pool.memset(BD[:, :, :], 0.0)
            pool.memset(eps[:, :, 0:1], 1e-5)
            pool.memset(eps[:, :, 1:2], -0.5).then_inc(zero, 1)
            pool.wait_ge(stat, 2 + 3 * PAIRS)
            pool.tensor_tensor(mv[:, :, 1:2], mv[:, :, 1:2], eps[:, :, 0:1], ALU.add).then_inc(rstd, 1)
            pool.wait_ge(rstd, 1)
            pool.tensor_tensor(mv[:, :, 1:2], mv[:, :, 1:2], eps[:, :, 1:2], ALU.pow).then_inc(rstd, 1)

        @block.tensor
        def _(pe):
            mm = nc.tensor.matmul
            for done in (s_mm, gt_mm, gg_mm, bt_mm, o_mm):
                pe.nop().then_inc(done, 1)
            pe.wait_ge(par, 16 * 6)
            for w in range(3):
                for o in range(2):
                    nc.tensor.transpose(ps[0:EH, 2 * w + o, 0:EH], WQ[0:EH, 0, E * w + EH * o:E * w + EH * o + EH], ident[0:EH, 0:EH])
                    ins = nc.tensor.transpose(ps[0:EH, 2 * w + o, EH:E + 1], WQ[:, 1, E * w + EH * o:E * w + EH * o + EH], ident[0:EA, 0:EA])
            ins.then_inc(tr, 1)
            pe.wait_ge(prep, 6)
            for i, (lo, n) in enumerate(((0, EH), (EH, EA))):
                for o in range(2):
                    mm(ps[0:n, i, 0:E + 1], WQT[:, 0, o, lo:lo + n], WQT[:, 1, o, :], start=(o == 0), stop=(o == 1))
                for o in range(2):
                    mm(ps[0:n, 2 + i, 0:KG], WQT[:, 2, o, lo:lo + n], WGP[:, o, :], start=(o == 0), stop=(o == 1))
                for o in range(2):
                    ins = mm(ps[0:n, 4 + i, 0:E], WQT[:, 2, o, lo:lo + n], WPJ[:, o, :], start=(o == 0), stop=(o == 1))
            ins.then_inc(tr, 1)
            pe.wait_ge(prep, 14)

            with pe.Fori(0, PAIRS // 2) as i2:
                j = i2 * 2
                for s in range(2):
                    pe.wait_ge(xp, j + (s + 1))
                    x = XP[:, s]
                    if s == 0:
                        pe.wait_ge(u_cp, j + 1)
                    else:
                        pe.wait_ge(u_cp, j + 2)
                    for o, n in ((0, EH), (1, EA)):
                        for rows, h in HK:
                            ins = mm(ps[0:n, 0, P * o:P * o + P], GM[rows, h, EH * o:EH * o + n], x[rows, h, :],
                                     start=(h == 0), stop=(h == 1))
                    ins.then_inc(u_mm, 1)
                    pe.wait_ge(s_cp, j + (s + 1))
                    pe.wait_ge(glu, j + (s + 1))
                    for rows, h in HK:
                        mm(ps[:, 1, 0:KG + 2 * E], x[rows, h, :], WR[rows, h, :], start=(h == 0), stop=(h == 1))
                    pe.wait_ge(u_cp, j + (s + 2))
                    for i in range(2):
                        c = slice(SLOT * i, SLOT * i + SLOT)
                        for rows, h in HK:
                            ins = mm(ps[c, 2, 0:KG], UT[rows, s, h, c], x[rows, h, SLOT * i:SLOT * i + KG],
                                     start=(h == 0), stop=(h == 1))
                    ins.then_inc(s_mm, 1)
            pe.wait_ge(soft, 5)
            with pe.Fori(0, PAIRS // 2) as i2:
                j = i2 * 2
                for s in range(2):
                    pe.wait_ge(gt_cp, j + (s + 1))
                    pe.wait_ge(bd, j + (s + 1))
                    nc.tensor.transpose(ps[:, 0, 0:P], BD[:, s, :], ident[:, :]).then_inc(gt_mm, 1)
                    pe.wait_ge(gt_cp, j + (s + 2))
                    pe.wait_ge(gg_cp, j + (s + 1))
                    for i in range(2):
                        c = slice(SLOT * i, SLOT * i + SLOT)
                        ins = mm(ps[c, 1, 0:KG], GT[:, s, c], GT[:, s, SLOT * i:SLOT * i + KG], start=True, stop=True)
                    ins.then_inc(gg_mm, 1)
            with pe.Fori(0, PAIRS // 2) as i2:
                j = i2 * 2
                for s in range(2):
                    pe.wait_ge(bd, j + (PAIRS + s + 1))
                    pe.wait_ge(bt_cp, j + (s + 1))
                    nc.tensor.transpose(ps[:, 3, 0:P], BD[:, s, :], ident[:, :]).then_inc(bt_mm, 1)
                    pe.wait_ge(bt_cp, j + (s + 2))
                    pe.wait_ge(o_cp, j + (s + 1))
                    mm(ps[:, 2, 0:E], BT[:, s, :], VP[:, bass.ds(j + s, 1), 0:E], start=True, stop=True).then_inc(o_mm, 1)

        @block.scalar
        def _(act):
            act.nop().then_inc(glu, 1)
            act.wait_ge(par, 16 * 6)
            act.activation(al[:, 1:2], al[:, 0:1], ACT.Sigmoid)
            act.activation(al[:, 2:3], al[:, 0:1], ACT.Sigmoid, scale=-1.0).then_inc(ex, 1)
            with act.Fori(0, PAIRS) as j:
                act.wait_ge(s_mm, j + 2)
                act.activation(GA[:, bass.ds(j, 1), :], ps[:, 1, 0:KG], ACT.Gelu)
                act.activation(VP[:, bass.ds(j, 1), :], ps[:, 1, KG:KG + 2 * E], ACT.Copy).then_inc(glu, 1)
            act.wait_ge(soft, 2)
            act.activation(GA[:, :, :], GA[:, :, :], ACT.Exp).then_inc(ex, 1)
            act.wait_ge(soft, 7)
            act.activation(SC[:, :, :], SC[:, :, :], ACT.Exp).then_inc(ex, 1)

        @block.vector
        def _(dve):
            for ready in (u_cp, s_cp, gt_cp, gg_cp, bt_cp, o_cp):
                dve.nop().then_inc(ready, 1)
            dve.wait_ge(tr, 1)
            for w in range(3):
                for o in range(2):
                    dve.tensor_copy(WQT[:, w, o, :], ps[0:EH, 2 * w + o, 0:E + 1]).then_inc(prep, 1)
            dve.wait_ge(tr, 2)
            for i, n in enumerate((EH, EA)):
                dve.tensor_copy(GM[0:n, i, :], ps[0:n, i, 0:E + 1]).then_inc(prep, 1)
                dve.tensor_copy(WR[0:n, i, 0:KG], ps[0:n, 2 + i, 0:KG]).then_inc(prep, 1)
                dve.tensor_copy(WR[0:n, i, KG:KG + E], ps[0:n, 4 + i, 0:E]).then_inc(prep, 1)
            dve.memset(WR[0:EH, :, KG + E:], 0.0).then_inc(prep, 1)
            dve.wait_ge(prep, 13)
            for i in range(2):
                ins = dve.tensor_copy(WR[0:EH, i, KG + E + EH * i:KG + E + EH * i + EH], ident[0:EH, 0:EH])
            ins.then_inc(prep, 1)

            with dve.Fori(0, PAIRS // 2) as i2:
                j = i2 * 2
                for s in range(2):
                    dve.wait_ge(s_mm, j + 1)
                    dve.tensor_copy(XP[0:EH, s, 0, :], XT[0:EH, 0, bass.ds(j + s, 1), :])
                    dve.tensor_copy(XP[:, s, 1, :], XT[0:EA, 1, bass.ds(j + s, 1), :]).then_inc(xp, 1)
                for s in range(2):
                    dve.wait_ge(u_mm, j + (s + 1))
                    dve.tensor_copy(UT[0:EH, s, 0, :], ps[0:EH, 0, 0:P])
                    dve.tensor_copy(UT[:, s, 1, :], ps[0:EA, 0, P:2 * P]).then_inc(u_cp, 1)
                    dve.wait_ge(s_mm, j + (s + 2))
                    dve.tensor_scalar(SC[:, bass.ds(j + s, 1), :], ps[:, 2, 0:KG], float(E) ** -0.5, None, ALU.mult).then_inc(s_cp, 1)

            done = [0]

            def step(ins):
                done[0] += 1
                ins.then_inc(soft, 1)
                dve.wait_ge(soft, done[0])

            def wide(v):
                return v[:, :].unsqueeze(2).broadcast_to([P, PAIRS, KG])

            dve.wait_ge(glu, PAIRS + 1)
            step(dve.tensor_reduce(red[:, :], GA[:, :, :], AX_X, ALU.max))
            step(dve.tensor_tensor(GA[:, :, :], GA[:, :, :], wide(red), ALU.subtract))
            dve.wait_ge(ex, 2)
            step(dve.tensor_reduce(red[:, :], GA[:, :, :], AX_X, ALU.add))
            step(dve.reciprocal(inv[:, :], red[:, :]))
            step(dve.tensor_tensor(GA[:, :, :], GA[:, :, :], wide(inv), ALU.mult))
            dve.wait_ge(zero, 1)
            with dve.Fori(0, PAIRS // 2) as i2:
                j = i2 * 2
                for s in range(2):
                    dve.wait_ge(gt_mm, j + 1)
                    dve.tensor_copy(BD[:, s, 0:KG], GA[:, bass.ds(j + s, 1), :]).then_inc(bd, 1)
                for s in range(2):
                    dve.wait_ge(gt_mm, j + (s + 2))
                    dve.wait_ge(gg_mm, j + 1)
                    dve.tensor_copy(GT[:, s, :], ps[:, 0, 0:P]).then_inc(gt_cp, 1)
                    dve.wait_ge(gg_mm, j + (s + 2))
                    dve.tensor_copy(GG[:, bass.ds(j + s, 1), :], ps[:, 1, 0:KG]).then_inc(gg_cp, 1)
            dve.wait_ge(gg_cp, PAIRS + 1)
            dve.wait_ge(s_cp, PAIRS + 1)
            dve.tensor_tensor(SC[:, :, :], SC[:, :, :], GG[:, :, :], ALU.mult).then_inc(stat, 1)
            dve.wait_ge(stat, 1)
            step(dve.tensor_reduce(red[:, :], SC[:, :, :], AX_X, ALU.max))
            step(dve.tensor_tensor(SC[:, :, :], SC[:, :, :], wide(red), ALU.subtract))
            dve.wait_ge(ex, 3)
            step(dve.tensor_reduce(red[:, :], SC[:, :, :], AX_X, ALU.add))
            step(dve.reciprocal(inv[:, :], red[:, :]))
            step(dve.tensor_tensor(SC[:, :, :], SC[:, :, :], wide(inv), ALU.mult))
            step(dve.tensor_scalar(SC[:, :, :], SC[:, :, :], al[:, 2:3], None, ALU.mult))
            step(dve.scalar_tensor_tensor(out=SC[:, :, :], in0=GG[:, :, :], scalar=al[:, 1:2], in1=SC[:, :, :],
                                          op0=ALU.mult, op1=ALU.add))
            dve.memset(BD[SLOT:P, :, 0:SLOT], 0.0).then_inc(stat, 1)
            dve.wait_ge(stat, 2)
            with dve.Fori(0, PAIRS // 2) as i2:
                j = i2 * 2
                for s in range(2):
                    dve.wait_ge(bt_mm, j + 1)
                    for i in range(2):
                        r = slice(SLOT * i, SLOT * i + SLOT)
                        ins = dve.tensor_copy(BD[r, s, SLOT * i:SLOT * i + KG], SC[r, bass.ds(j + s, 1), :])
                    ins.then_inc(bd, 1)
                for s in range(2):
                    dve.wait_ge(bt_mm, j + (s + 2))
                    dve.wait_ge(o_mm, j + 1)
                    dve.tensor_copy(BT[:, s, :], ps[:, 3, 0:P]).then_inc(bt_cp, 1)
                    dve.wait_ge(o_mm, j + (s + 2))
                    dve.tensor_tensor(yb[:, s, :].unsqueeze(1), ps[:, 2, 0:E].unsqueeze(1), VP[:, bass.ds(j + s, 1), E:],
                                      ALU.add).then_inc(o_cp, 1)
                    dve.wait_ge(o_cp, j + (s + 2))
                    dve.bn_stats(st[:, s, :], yb[:, s, :]).then_inc(stat, 1)
                    dve.wait_ge(stat, (j + s) * 3 + 3)
                    dve.memset(scratch[:, :], 0.0)
                    dve.bn_aggr(ms[:, s, :], st[:, s, :]).then_inc(stat, 1)
                    dve.tensor_copy(Y1[:, bass.ds(j + s, 1), :], yb[:, s, :].unsqueeze(1))
                    dve.wait_ge(stat, (j + s) * 3 + 4)
                    dve.tensor_copy(mv[:, bass.ds(j + s, 1), :], ms[:, s, :].unsqueeze(1)).then_inc(stat, 1)
            dve.wait_ge(rstd, 2)
            wide2 = [mv[:, :, i:i + 1].broadcast_to([P, PAIRS, E]) for i in range(2)]
            step(dve.tensor_tensor(Y1[:, :, :], Y1[:, :, :], wide2[0], ALU.subtract))
            step(dve.tensor_tensor(Y1[:, :, :], Y1[:, :, :], wide2[1], ALU.mult))


EXPERTS, HID = 4, 768
SLOTS = 256
NS = EXPERTS * SLOTS
SCH = NS // P
HH = HID // 2
STEP = 8
UNITS = EXPERTS * STEP
LAG = 3
ROTATING = 3
JOBS = ("y", "l", "t", "w", "d", "c", "zt")


def unit(u):
    return u // 8, u // 4 % 2, u // 2 % 2, u % 2


def pair_items():
    items = [(("y", 0), 1 - UNITS), (("y", 1), 1 - UNITS), (("l", 0), 3 - UNITS), (("l", 1), 4 - UNITS),
             (("t", 0), 7 - UNITS), (("t", 1), 9 - UNITS), (("exp",), 12 - UNITS), (("dt",), 17 - UNITS)]
    for e in range(EXPERTS):
        s = STEP * (e - 1)
        items += [(("w", e, 0), s + 1), (("d", e), s + 2), (("w", e, 1), s + 4), (("c", e), s + 6)]
        for half in range(2):
            s = STEP * e + 4 * half
            items += [(("ze", e, half), s + 3 + LAG), (("zt", e, half), s + 5 + LAG), (("w2", e, half), s + 8 + LAG)]
    items += [(("h", u), u) for u in range(UNITS)] + [(("z", u), u + LAG) for u in range(UNITS)]
    return items + [(("out",), UNITS + 8), (("norm",), UNITS + 12)]


ORDER = ("h", "z", "ze", "w2", "zt", "y", "l", "t", "exp", "dt", "w", "d", "c", "out", "norm")


def ffn_stage(pairs):
    found = [(at + UNITS * r, ORDER.index(item[0]), item, r) for r in pairs for item, at in pair_items()
             if 0 <= at + UNITS * r < UNITS]
    return [(r, item) for _, _, item, r in sorted(found)]


def jobs_of(pairs):
    jobs = [x for x in ffn_stage(pairs) if x[1][0] in JOBS]
    return {x: n for n, x in enumerate(jobs)}


JOBS_BEFORE_0 = len(jobs_of((1,)))
JOBS_BEFORE_1 = JOBS_BEFORE_0 + len(jobs_of((0, 1)))
STAGE_JOBS = len(jobs_of((-1, 0, 1)))
assert STAGE_JOBS % ROTATING == 0


class Stage:

    def __init__(self, j, parity, pairs):
        self.j, self.parity, self.pairs = j, parity, pairs
        self.events, self.jobs = ffn_stage(pairs), jobs_of(pairs)
        self.fixed = isinstance(j, int) and j < 1
        if self.fixed:
            self.first = JOBS_BEFORE_0 if j == 0 else 0
        else:
            self.first = JOBS_BEFORE_1 - (JOBS_BEFORE_0 if pairs == (-1,) else 0)

    def times(self, r, per, more):
        if isinstance(self.j, int):
            v = (self.j + r) * per + more
            return v if v > 0 else None
        assert (1 + r) * per + more > 0
        return self.j * per + (r * per + more)

    def job(self, n):
        if self.fixed:
            return self.first + n if self.first + n > 0 else None
        return self.times(-1, STAGE_JOBS, self.first + n)

    def bank(self, n):
        return (self.first + n) % ROTATING

    def ready(self, r, *items):
        return self.job(max([self.jobs[r, i] + 1 for i in items if (r, i) in self.jobs], default=0))


def ffn_phase(nc, a, Y1, ident, out):
    PAIRS = HALF
    KT = TOKENS
    EA = EH + 1
    HK = ((slice(0, EH), 0), (slice(0, EA), 1))
    IMG = (slice(0, SLOT), slice(SLOT, P))
    with ExitStack() as ctx:
        def sb(name, shape, dt=F32):
            return ctx.enter_context(nc.sbuf_tensor(name, shape, dt))

        def sem(name):
            return ctx.enter_context(nc.semaphore(name))

        PT = sb("PT", [EH, 2, NS])
        W1 = sb("FW1", [EA, 2, EXPERTS * HID])
        W2 = sb("FW2", [P, EXPERTS * HID // P, E])
        B2 = sb("FB2", [P, EXPERTS, E])
        YP = sb("YP", [P, 2, E])
        YT = sb("YT", [EA, 2, 2, P])
        LS = sb("LS", [P, NS])
        C = sb("C", [P, 2, NS])
        CS = sb("CS", [P, 2, EXPERTS])
        LT = sb("LT", [P, SCH, 2, KT])
        DT = sb("DT", [P, 2, SCH, 2, 2, SLOT])
        CT = sb("CT", [P, 2, 2, 2, 3 * SLOT], F32R)
        D = sb("FD", [P, 2, 2, 2, SLOTS], F32R)
        R = sb("R", [P, 2, 2, HID], F32R)
        HF = sb("HF", [P, 2, HH])
        HI = sb("HI", [P, 4, HH], F32R)
        HL = sb("HL", [P, 4, HH], F32R)
        ZS = sb("ZS", [P, 2, 2, HH])
        ZT = sb("ZT", [P, 2, 3, P])
        zs0 = sb("zs0", [P, SLOT])
        mx = sb("mx", [P, 2])
        mt = sb("mt", [P, 2 * SCH])
        mi = sb("mi", [P, 2 * SCH])
        ss = sb("ss", [P, 2])
        acc = sb("acc", [P, E])
        o = sb("fo", [P, 2, E])
        st = sb("fst", [P, 6])
        scratch = sb("fscratch", [P, 1])
        mv = sb("fmv", [P, 2])
        eps = sb("feps", [P, 2])
        PH = ZS[:, :, :, :].rearrange("p a b n -> p (a b n)")[:, 0:SCH * E].rearrange("p (c d) -> p c d", d=E)
        ps = ctx.enter_context(nc.psum_tensor("psf", [P, 8, 512], F32))
        HB, ZB, OB, MB = 0, 2, 4, 5

        par = sem("f_par")
        prep = sem("f_prep")
        tr = sem("f_tr")
        zero = sem("f_zero")
        yp = sem("f_yp")
        m_mm = sem("f_m_mm")
        m_hi = sem("f_m_hi")
        m_cp = sem("f_m_cp")
        negmax = sem("f_negmax")
        c_ex = sem("f_c_ex")
        lt_sub = sem("f_lt_sub")
        lt_ex = sem("f_lt_ex")
        dt_ok = sem("f_dt_ok")
        h_mm = sem("f_h_mm")
        h_act = sem("f_h_act")
        h_lo = sem("f_h_lo")
        z_mm = sem("f_z_mm")
        z_cp = sem("f_z_cp")
        w_mm = sem("f_w_mm")
        link = sem("f_link")
        olink = sem("f_olink")
        var = sem("f_var")
        rstd = sem("f_rstd")
        o_ok = sem("f_o_ok")
        o_st = sem("f_o_st")
        stored = sem("f_stored")
        block = ctx.enter_context(nc.Block())
        LINKS, OLINKS, O_READ, CS_READ = 6, 9, 5, 6
        HIGHS = 4 * EXPERTS

        def stages(eng, body):
            body(Stage(-1, 1, (1,)))
            body(Stage(0, 0, (0, 1)))
            with eng.Fori(0, PAIRS // 2 - 1) as i:
                for s in range(2):
                    body(Stage(i * 2 + (1 + s), (1 + s) % 2, (-1, 0, 1)))
            body(Stage(PAIRS - 1, 1, (-1, 0)))
            body(Stage(PAIRS, 0, (-1,)))

        def wait(eng, s, value):
            if value is not None:
                eng.wait_ge(s, value)

        @block.sync
        def _(sp):
            def param(dst, src):
                sp.dma_start(dst, src).then_inc(par, 16)

            param(PH, a["phi"].rearrange("e (k p) d -> p (e k) d", p=P))
            for h, lo in ((0, 0), (1, EH)):
                param(W1[0:EH, h, :].rearrange("k (e n) -> k e n", e=EXPERTS), a["fw1"][:, lo:lo + EH, :].rearrange("e k n -> k e n"))
            param(W1[EH:EA, 1, :], a["fb1"].rearrange("(u e) n -> u (e n)", u=1))
            param(W2[:, :, :], a["fw2"].rearrange("e (k p) d -> p (e k) d", p=P))
            param(B2[:, :, :], a["fb2"].rearrange("(u e) n -> u e n", u=1).broadcast_to([P, EXPERTS, E]))
            sp.nop().then_inc(stored, 1)
            with sp.Fori(0, PAIRS // 2) as i:
                for s in range(2):
                    sp.wait_ge(o_ok, i * 2 + (s + 1))
                    for h in range(2):
                        sp.dma_start(out[bass.ds(i * 2 + (s + HALF * h), 1), :, :].rearrange("b n d -> (b n) d"),
                                     o[SLOT * h:SLOT * h + KT, s, :]).then_inc(o_st, 16)
                    sp.wait_ge(o_st, i * 64 + (32 * s + 32))
                    sp.nop().then_inc(stored, 1)
            sp.wait_ge(o_st, 32 * PAIRS)

        @block.gpsimd
        def _(pool):
            pool.memset(DT[:, :, :, :, :, :], 0.0).then_inc(zero, 1)
            pool.wait_ge(zero, 1)
            pool.memset(YT[EH:EA, :, :, :], 1.0).then_inc(zero, 1)
            pool.wait_ge(zero, 2)
            pool.memset(eps[:, 0:1], 1e-5)
            pool.memset(zs0[:, :], 0.0)
            pool.memset(eps[:, 1:2], -0.5).then_inc(zero, 1)
            pool.wait_ge(zero, 3)

            def body(g):
                for r, ev in g.events:
                    if ev == ("y", 0):
                        wait(pool, m_cp, g.job(0))
                        s = (g.parity + r) % 2
                        src = Y1[:, bass.ds(g.j + r, 1), :] if not isinstance(g.j, int) else Y1[:, g.j + r:g.j + r + 1, :]
                        pool.tensor_copy(YP[:, s, :].unsqueeze(1), src).then_inc(yp, 1)
                    if ev[0] == "out":
                        wait(pool, var, g.times(r, 1, 1))
                        pool.tensor_tensor(mv[:, 1:2], mv[:, 1:2], eps[:, 0:1], ALU.add).then_inc(rstd, 1)
                        wait(pool, rstd, g.times(r, 2, 1))
                        pool.tensor_tensor(mv[:, 1:2], mv[:, 1:2], eps[:, 1:2], ALU.pow).then_inc(rstd, 1)

            stages(pool, body)

        @block.tensor
        def _(pe):
            mm = nc.tensor.matmul
            pe.wait_ge(par, 16 * 6)
            for h in range(2):
                for c in range(SCH):
                    ins = nc.tensor.transpose(ps[0:EH, 2 * h + c // 4, P * (c % 4):P * (c % 4) + P],
                                              PH[:, c, EH * h:EH * h + EH], ident[:, :])
            ins.then_inc(tr, 1)
            pe.wait_ge(prep, 5)

            def body(g):
                for r, ev in g.events:
                    kind, i = ev[0], ev[1] if len(ev) > 1 else None
                    s = (g.parity + r) % 2
                    if kind in JOBS:
                        n = g.jobs[r, ev]
                        b = ps[:, MB + g.bank(n), :]
                        wait(pe, m_cp, g.job(n - ROTATING + 1))
                    if kind == "h":
                        e, half, img, c = unit(i)
                        if i % STEP == 0:
                            wait(pe, m_cp, g.ready(r, ("w", e, 0), ("w", e, 1), ("d", e)))
                        wait(pe, h_act, g.times(r, UNITS, i - 1))
                        for part in range(2):
                            ins = mm(ps[:, HB + i % 2, 0:HH], D[:, e % 2, part, img, P * c:P * c + P],
                                     R[:, e % 2, img, HH * half:HH * half + HH], start=(part == 0), stop=(part == 1))
                        ins.then_inc(h_mm, 1)
                    if kind == "z":
                        e, half, img, c = unit(i)
                        wait(pe, h_lo, g.times(r, UNITS, i + 1))
                        if i % 4 == 0:
                            wait(pe, z_cp, g.times(r, 2 * EXPERTS, 2 * e + half - 1))
                            wait(pe, m_cp, g.ready(r, ("c", e)))
                        w = CT[:, e % 2, :, c, SLOT * img:SLOT * img + P]
                        first = img + c == 0
                        mm(ps[:, ZB + half, 0:HH], w[:, 0, :], HI[:, i % 4, :], start=first, stop=False)
                        mm(ps[:, ZB + half, 0:HH], w[:, 0, :], HL[:, i % 4, :], start=False, stop=False)
                        mm(ps[:, ZB + half, 0:HH], w[:, 1, :], HI[:, i % 4, :], start=False, stop=(img + c == 2)).then_inc(z_mm, 1)
                    if kind == "zt":
                        wait(pe, z_cp, g.times(r, 2 * EXPERTS, 2 * i + ev[2] + 1))
                        for x in range(3):
                            ins = nc.tensor.transpose(b[:, P * x:P * x + P], ZS[:, i % 2, ev[2], P * x:P * x + P], ident[:, :])
                    if kind == "w2":
                        wait(pe, m_cp, g.ready(r, ("zt", i, ev[2])))
                        if i == 0 and ev[2] == 0:
                            wait(pe, olink, g.times(r - 1, OLINKS, O_READ))
                        for x in range(3):
                            ins = mm(ps[:, OB, 0:E], ZT[:, ev[2], x, :], W2[:, 6 * i + 3 * ev[2] + x, :],
                                     start=(i + ev[2] + x == 0), stop=(i == 3 and ev[2] == 1 and x == 2))
                        ins.then_inc(w_mm, 1)
                    if kind == "y":
                        wait(pe, yp, g.times(r, 1, 1))
                        ins = nc.tensor.transpose(b[0:EH, 0:P], YP[:, s, EH * i:EH * i + EH], ident[:, :])
                    if kind == "l":
                        wait(pe, m_cp, g.ready(r, ("y", 0), ("y", 1)))
                        for h in range(2):
                            ins = mm(b[:, :], YT[0:EH, s, h, :], PT[:, h, 512 * i:512 * i + 512], start=(h == 0), stop=(h == 1))
                    if kind == "t":
                        wait(pe, m_cp, g.ready(r, ("l", i)))
                        for c in range(4):
                            lo = P * (4 * i + c)
                            ins = nc.tensor.transpose(b[:, P * c:P * c + P], LS[:, lo:lo + P], ident[:, :])
                    if kind == "w":
                        lo = HID * i + HH * ev[2]
                        for rows, h in HK:
                            ins = mm(b[:, 0:HH], YT[rows, s, h, :], W1[rows, h, lo:lo + HH], start=(h == 0), stop=(h == 1))
                    if kind == "c":
                        wait(pe, c_ex, g.times(r, 1, 1))
                        for c in range(2):
                            lo = SLOTS * i + P * c
                            ins = nc.tensor.transpose(b[:, P * c:P * c + P], C[:, s, lo:lo + P], ident[:, :])
                    if kind == "d":
                        wait(pe, dt_ok, g.times(r, 2, 2))
                        for img in range(2):
                            for c in range(2):
                                v = DT[:, s, 2 * i + c, img, :, :].rearrange("p t n -> p (t n)")
                                ins = nc.tensor.transpose(b[:, SLOTS * img + P * c:SLOTS * img + P * c + P], v, ident[:, :])
                    if kind in JOBS:
                        ins.then_inc(m_mm, 1)

            stages(pe, body)

        @block.scalar
        def _(act):
            def body(g):
                for r, ev in g.events:
                    kind, i = ev[0], ev[1] if len(ev) > 1 else None
                    s = (g.parity + r) % 2
                    if kind in JOBS:
                        n = g.jobs[r, ev]
                        b = ps[:, MB + g.bank(n), :]
                    if kind in ("w", "d", "c"):
                        wait(act, m_mm, g.job(n + 1))
                    if kind == "w":
                        for img in range(2):
                            ins = act.activation(R[IMG[img], i % 2, img, HH * ev[2]:HH * ev[2] + HH], b[IMG[img], 0:HH], ACT.Copy)
                        ins.then_inc(m_hi, 1)
                    if kind == "d":
                        act.activation(D[:, i % 2, 0, :, :], b[:, :].rearrange("p (i n) -> p i n", i=2), ACT.Copy).then_inc(m_hi, 1)
                    if kind == "c":
                        wait(act, z_mm, g.times(r, UNITS, STEP * (i - 1)))
                        for img in range(2):
                            ins = act.activation(CT[:, i % 2, 0, :, P * img:P * img + SLOT],
                                                 b[:, 0:SLOTS].rearrange("p (c n) -> p c n", c=2)[:, :, IMG[img]], ACT.Copy)
                        ins.then_inc(m_hi, 1)
                    if kind == "exp":
                        wait(act, negmax, g.times(r, 1, 1))
                        wait(act, olink, g.times(r - 2, OLINKS, CS_READ))
                        for e in range(EXPERTS):
                            lo = SLOTS * e
                            ins = act.activation(C[:, s, lo:lo + SLOTS], LS[:, lo:lo + SLOTS], ACT.Exp, bias=mx[:, 1:2],
                                                 accum_out=CS[:, s, e:e + 1])
                        ins.then_inc(c_ex, 1)
                        wait(act, lt_sub, g.times(r, 2, 2))
                        act.activation(LT[:, :, :, :], LT[:, :, :, :], ACT.Exp).then_inc(lt_ex, 1)
                    if kind == "h":
                        wait(act, h_mm, g.times(r, UNITS, i + 1))
                        wait(act, z_mm, g.times(r, UNITS, i - 3))
                        act.activation(HI[:, i % 4, :], ps[:, HB + i % 2, 0:HH], ACT.Gelu_apprx_tanh)
                        wait(act, h_lo, g.times(r, UNITS, i - 1))
                        act.activation(HF[:, i % 2, :], ps[:, HB + i % 2, 0:HH], ACT.Gelu_apprx_tanh).then_inc(h_act, 1)

            stages(act, body)

        @block.vector
        def _(dve):
            dve.wait_ge(tr, 1)
            for h in range(2):
                for c in range(2):
                    dve.tensor_copy(PT[:, h, 512 * c:512 * c + 512], ps[0:EH, 2 * h + c, :]).then_inc(prep, 1)
            dve.wait_ge(zero, 3)
            for sl in range(2):
                for part in range(2):
                    ins = dve.tensor_copy(CT[:, sl, part, :, SLOT:P], zs0[:, :].unsqueeze(1).broadcast_to([P, 2, SLOT]))
            ins.then_inc(prep, 1)
            dve.wait_ge(par, 16 * 6)

            def body(g):
                for r, ev in g.events:
                    kind, i = ev[0], ev[1] if len(ev) > 1 else None
                    s = (g.parity + r) % 2

                    def step(n, ins):
                        ins.then_inc(link, 1)
                        wait(dve, link, g.times(r, LINKS, n))

                    def ostep(n, ins):
                        ins.then_inc(olink, 1)
                        wait(dve, olink, g.times(r, OLINKS, n))

                    if kind in JOBS:
                        n = g.jobs[r, ev]
                        b = ps[:, MB + g.bank(n), :]
                        wait(dve, m_mm, g.job(n + 1))
                    if kind in ("w", "d", "c"):
                        order = {"w": {0: 1, 1: 3}.get(ev[2] if kind == "w" else 0, 0), "d": 2, "c": 4}[kind]
                        wait(dve, m_hi, g.times(r, HIGHS, 4 * i + order))
                    if kind == "w":
                        cols = slice(HH * ev[2], HH * ev[2] + HH)
                        for img in range(2):
                            ins = dve.tensor_tensor(R[IMG[1 - img], i % 2, img, cols], b[IMG[img], 0:HH],
                                                    R[IMG[img], i % 2, img, cols].bitcast(F32), ALU.subtract)
                        ins.then_inc(m_cp, 1)
                    if kind == "d":
                        dve.tensor_tensor(D[:, i % 2, 1, :, :], b[:, :].rearrange("p (i n) -> p i n", i=2),
                                          D[:, i % 2, 0, :, :].bitcast(F32), ALU.subtract).then_inc(m_cp, 1)
                    if kind == "c":
                        for img in range(2):
                            cols = slice(P * img, P * img + SLOT)
                            ins = dve.tensor_tensor(CT[:, i % 2, 1, :, cols],
                                                    b[:, 0:SLOTS].rearrange("p (c n) -> p c n", c=2)[:, :, IMG[img]],
                                                    CT[:, i % 2, 0, :, cols].bitcast(F32), ALU.subtract)
                        ins.then_inc(m_cp, 1)
                    if kind == "y":
                        dve.tensor_copy(YT[0:EH, s, i, :], b[0:EH, 0:P]).then_inc(m_cp, 1)
                    if kind == "l":
                        wait(dve, c_ex, g.times(r - 1, 1, 1))
                        dve.tensor_copy(LS[:, 512 * i:512 * i + 512], b[:, :]).then_inc(m_cp, 1)
                        if i == 1:
                            wait(dve, m_cp, g.job(n + 1))
                            step(1, dve.tensor_reduce(mx[:, 0:1], LS[:, :], AX_X, ALU.max))
                            dve.tensor_scalar(mx[:, 1:2], mx[:, 0:1], -1.0, None, ALU.mult).then_inc(negmax, 1)
                    if kind == "t":
                        v = b[:, :].rearrange("p (c i n) -> p c i n", c=4, n=SLOT)[:, :, :, 0:KT]
                        m = mt[:, 8 * i:8 * i + 8]
                        step(2 + i, dve.tensor_reduce(m.rearrange("p (c i) -> p c i", i=2), v, AX_X, ALU.max))
                        wide = m.rearrange("p (c i) -> p c i", i=2).unsqueeze(3).broadcast_to([P, 4, 2, KT])
                        if i == 0:
                            wait(dve, dt_ok, g.times(r - 1, 2, 2))
                        dve.tensor_tensor(LT[:, 4 * i:4 * i + 4, :, :], v, wide, ALU.subtract).then_inc(m_cp, 1)
                        wait(dve, m_cp, g.job(n + 1))
                        dve.memset(scratch[:, :], 0.0).then_inc(lt_sub, 1)
                    if kind == "dt":
                        wait(dve, lt_ex, g.times(r, 1, 1))
                        step(4, dve.tensor_reduce(mt[:, :].rearrange("p (c i) -> p c i", i=2), LT[:, :, :, :], AX_X, ALU.add))
                        step(5, dve.reciprocal(mi[:, :], mt[:, :]))
                        step(6, dve.tensor_tensor(LT[:, :, :, :], LT[:, :, :, :],
                                                  mi[:, :].rearrange("p (c i) -> p c i", i=2).unsqueeze(3).broadcast_to([P, SCH, 2, KT]),
                                                  ALU.mult))
                        for twice in range(2):
                            dve.tensor_copy(DT[:, s, :, :, twice, 0:KT], LT[:, :, :, :]).then_inc(dt_ok, 1)
                    if kind == "h":
                        wait(dve, h_act, g.times(r, UNITS, i + 1))
                        dve.tensor_tensor(HL[:, i % 4, :], HF[:, i % 2, :], HI[:, i % 4, :].bitcast(F32),
                                          ALU.subtract).then_inc(h_lo, 1)
                    if kind == "ze":
                        wait(dve, z_mm, g.times(r, UNITS, STEP * i + 4 * ev[2] + 4))
                        dve.tensor_copy(ZS[:, i % 2, ev[2], :], ps[:, ZB + ev[2], 0:HH]).then_inc(z_cp, 1)
                    if kind == "zt":
                        wait(dve, w_mm, g.times(r, 2 * EXPERTS, 2 * i + ev[2] - 1))
                        dve.tensor_copy(ZT[:, ev[2], :, :], b[:, 0:3 * P].rearrange("p (x n) -> p x n", n=P)).then_inc(m_cp, 1)
                    if kind == "out":
                        wait(dve, c_ex, g.times(r, 1, 1))
                        ostep(1, dve.tensor_scalar(acc[:, :], B2[:, 0, :], CS[:, s, 0:1], None, ALU.mult))
                        for e in range(1, EXPERTS):
                            ostep(1 + e, dve.scalar_tensor_tensor(out=acc[:, :], in0=B2[:, e, :], scalar=CS[:, s, e:e + 1],
                                                                  in1=acc[:, :], op0=ALU.mult, op1=ALU.add))
                        wait(dve, w_mm, g.times(r, 2 * EXPERTS, 2 * EXPERTS))
                        ostep(O_READ, dve.tensor_tensor(acc[:, :], acc[:, :], ps[:, OB, 0:E], ALU.add))
                        ostep(CS_READ, dve.tensor_reduce(ss[:, 0:1], CS[:, s, :], AX_X, ALU.add))
                        ostep(7, dve.reciprocal(ss[:, 1:2], ss[:, 0:1]))
                        y = Y1[:, bass.ds(g.j + r, 1), :] if not isinstance(g.j, int) else Y1[:, g.j + r:g.j + r + 1, :]
                        ostep(8, dve.scalar_tensor_tensor(out=acc[:, :].unsqueeze(1), in0=acc[:, :].unsqueeze(1), scalar=ss[:, 1:2],
                                                          in1=y, op0=ALU.mult, op1=ALU.add))
                        ostep(9, dve.bn_stats(st[:, :], acc[:, :]))
                        dve.memset(scratch[:, :], 0.0)
                        dve.bn_aggr(mv[:, :], st[:, :]).then_inc(var, 1)
                    if kind == "norm":
                        wait(dve, rstd, g.times(r, 2, 2))
                        wait(dve, stored, g.times(r, 1, 1))
                        dve.tensor_scalar(o[:, s, :], acc[:, :], mv[:, 0:1], mv[:, 1:2], ALU.subtract, ALU.mult).then_inc(o_ok, 1)
                        wait(dve, o_ok, g.times(r, 1, 1))

            stages(dve, body)


def tower(nc, a, out):
    with ExitStack() as ctx:
        ident = ctx.enter_context(nc.sbuf_tensor("ident", [P, P], F32))
        Y1 = ctx.enter_context(nc.sbuf_tensor("Y1", [P, HALF, E], F32))
        with ExitStack() as tokens:
            XT = tokens.enter_context(nc.sbuf_tensor("XT", [EH + 1, 2, HALF, P], F32))
            conv_phase(nc, a, XT, Y1, ident)
            attention_phase(nc, a, XT, Y1, ident)
        ffn_phase(nc, a, Y1, ident, out)


_NAMES = {"x": "x", "wqkv": "L0_attn_W_qkv", "bqkv": "L0_attn_b_qkv", "wproj": "L0_attn_W_proj",
          "bproj": "L0_attn_b_proj", "wgp": "L0_attn_W_gp", "alpha": "L0_attn_alpha", "phi": "L0_ffn_phi",
          "fw1": "L0_ffn_w1", "fb1": "L0_ffn_b1", "fw2": "L0_ffn_w2", "fb2": "L0_ffn_b2",
          **{n: "L0_tok_" + n for n in ("w0", "s0", "b0", "wdw", "sdw", "bdw", "wpw", "spw", "bpw",
                                        "w1", "s1", "b1", "w2", "s2", "b2", "w3", "s3", "b3")}}


def kernel(**inputs):
    import concourse.bacc as bacc
    from concourse.bass_utils import run_bass_kernel_spmd

    nc = bacc.Bacc("TRN2", target_bir_lowering=False, num_devices=1)
    arrays, a = {}, {}
    for short, name in _NAMES.items():
        v = np.ascontiguousarray(inputs[name])
        if v.ndim == 0:
            v = v.reshape(1)
        arrays[f"in_{short}"] = v
        a[short] = nc.dram_tensor(f"in_{short}", v.shape, mybir.dt.from_np(v.dtype), kind="ExternalInput").ap()
    out = nc.dram_tensor("out_tokens", (IMAGES, TOKENS, E), F32, kind="ExternalOutput").ap()
    tower(nc, a, out)
    r = run_bass_kernel_spmd(nc, [arrays], core_ids=[0])
    return r.results[0]["out_tokens"]
```

```python
from contextlib import ExitStack

import numpy as np
import concourse.bass as bass
from concourse import mybir

F32 = mybir.dt.float32
F32R = mybir.dt.float32r
ALU = mybir.AluOpType
ACT = mybir.ActivationFunctionType
AX_X = mybir.AxisListType.X

P = 128
IMAGES, CIN, SIDE = 64, 3, 112
GRID = 7
RS = SIDE // GRID
CH = 12
CB = P // RS
CR = CH - CB
REGIONS = GRID * GRID
HALF = IMAGES // 2
E = 192
EH = E // 2
C2 = 48
TOKENS = GRID * GRID
HALO = RS + 2
KX = CIN * HALO
KLO = 64
KS = KLO + KX
XW = SIDE + 2
GW = RS + 2
BC = 4
CHUNKS = HALF // BC
NREG = HALF * RS
Q = RS // 4
SLOT = 64
TW = 441 + REGIONS + 588 + REGIONS
O_DW, O_BDW, O_PW, O_BPW = 0, 441, 490, 1078


def conv_phase(nc, a, XT, Y1, ident):
    x = a["x"]
    with ExitStack() as ctx:
        def sb(name, shape, dt=F32):
            return ctx.enter_context(nc.sbuf_tensor(name, shape, dt))

        def sem(name):
            return ctx.enter_context(nc.semaphore(name))

        space = Y1[:, :, :].rearrange("p j d -> p (j d)")
        X = sb("X", [KX, 2, HALF, XW])
        XS = sb("XS", [KS, 2, 2, BC, XW], F32R)
        G = sb("G", [P, 3, HALF, GRID, GW])
        U = sb("U", [P, 2, HALF, GRID, RS // 2])
        GR = sb("GR", [P, 2, 2, HALF, GW], F32R)
        H1 = space[0:96, 0:3584].rearrange("p (t h b x) -> p t h b x", t=2, h=2, b=HALF)
        H2 = space[0:96, 3584:4480].rearrange("p (h b x) -> p h b x", h=2, b=HALF)
        D = space[:, 0:3072].rearrange("p (s t n) -> p s t n", s=2, t=3)
        ACt = space[:, 3072:3408].rearrange("p (g t y) -> p g t y", g=GRID, t=3)
        AC = space[:, 3584:4256].rearrange("p (k g t y) -> p k g t y", k=2, g=GRID, t=3)
        WDF = space[:, 4480:5248].rearrange("p (k x n) -> p k x n", k=2, x=3)
        W0 = sb("W0", [KS, 2, 3, 5 * 64], F32R)
        WD = sb("WD", [P, 2, 2, 2, 3, P], F32R)
        WP = sb("WP", [P, 2, 448])
        W1 = sb("W1", [P, 2, 4, 96])
        W1U = sb("W1U", [P, 2, 2, 96])
        W2 = sb("W2", [96, 2, 2, 96])
        W3 = sb("W3", [96, 2, 2, 96])
        TAB = sb("TAB", [P, 2, TW])
        BV = sb("BV", [P, 2, 2, GRID])
        mY = sb("mY", [P, HALO])
        mX = sb("mX", [KS, HALO])
        mC = sb("mC", [P, CB])
        m4 = sb("m4", [P, Q])
        SEL = space[0:C2, 4480:5120].rearrange("p (s n) -> p s n", n=P)
        b0v = sb("b0v", [P, 2])
        b1v = sb("b1v", [96, 1])
        b2v = sb("b2v", [96, 1])
        b3v = sb("b3v", [96, 2])
        raw = H1[:, :, :, :, :].rearrange("p t h b x -> p (t h b x)")
        T12 = raw[0:CH, 1344:1344 + TW]
        s12 = raw[0:CH, 2471:2471 + REGIONS + 588]
        w0s = sb("w0s", [CIN, CH, 9])
        s0s = sb("s0s", [CIN, CH])
        w1s = raw[0:C2, 0:192]
        w2s = raw[0:C2, 192:384]
        w3s = raw[:, 384:768].rearrange("o (h n) -> o h n", h=2)
        w2p = raw[0:C2, 768:960].rearrange("o (x y c) -> o x y c", x=2, y=2)
        w3p = raw[:, 960:1344].rearrange("o (h x y c) -> o h x y c", h=2, x=2, y=2)
        s123 = sb("s123", [96, 4])
        b0s = sb("b0s", [CH, 1])
        w1t = raw[0:C2, 3108:3300].rearrange("p (k o) -> p k o", k=4)
        w0c = sb("w0c", [CIN, 9, CH])
        zrow = sb("zrow", [1, SIDE])
        zero_row = sb("zero_row", [P, 1])
        ps = ctx.enter_context(nc.psum_tensor("ps", [P, 8, 512], F32))
        CST_MASKS, CST_DONE = 15, 21
        PREP_DONE = 72
        SCALED = 14
        COPIED = SCALED + 1 + 15 + 2 + 4 + 4 + 6
        TRANSPOSED = COPIED + 6
        TSPLIT = ((0, 490), (490, 980), (980, TW))
        X0, X1 = (U[0:KS, s, :, :, :].rearrange("p b g x -> p (b g x)")[:, 0:3 * CH * RS].rearrange("p (t c y) -> p t c y", t=3, y=RS)
                  for s in range(2))

        x_cleared = sem("x_cleared")
        x_loaded = sem("x_loaded")
        x_hi = sem("x_hi")
        x_split = sem("x_split")
        par = sem("par")
        next_loaded = sem("next_loaded")
        cst = sem("cst")
        prep = sem("prep")
        tr = sem("tr")
        c0_mm = sem("c0_mm")
        c0_act = sem("c0_act")
        wd_ok = sem("wd_ok")
        wp_ok = sem("wp_ok")
        g_hi = sem("g_hi")
        g_lo = sem("g_lo")
        dw_mm = sem("dw_mm")
        dw_act = sem("dw_act")
        pw_mm = sem("pw_mm")
        pw_add = sem("pw_add")
        g3 = sem("g3")
        c1_mm = sem("c1_mm")
        c1_act = sem("c1_act")
        c3_dve = sem("c3_dve")
        chained = sem("chained")
        block = ctx.enter_context(nc.Block())
        NPAR = 26

        @block.sync
        def _(sp):
            def rows(gy_row, first, last):
                for h in range(2):
                    for c in range(CIN):
                        src = x[h * HALF:(h + 1) * HALF, c]
                        p = c * HALO
                        sp.dma_start(X[p + 1:p + 1 + RS, h, :, 1:1 + SIDE],
                                     src[:, bass.ds(gy_row, RS), :].rearrange("b y x -> y b x")).then_inc(x_loaded, 16)
                        if not first:
                            sp.dma_start(X[p:p + 1, h, :, 1:1 + SIDE],
                                         src[:, bass.ds(gy_row - 1, 1), :].rearrange("b y x -> y b x")).then_inc(x_loaded, 16)
                        if not last:
                            sp.dma_start(X[p + HALO - 1:p + HALO, h, :, 1:1 + SIDE],
                                         src[:, bass.ds(gy_row + RS, 1), :].rearrange("b y x -> y b x")).then_inc(x_loaded, 16)
                        else:
                            sp.dma_start(X[p + HALO - 1:p + HALO, h, :, 1:1 + SIDE],
                                         zrow[0:1, :].unsqueeze(1).broadcast_to([1, HALF, SIDE])).then_inc(x_loaded, 16)

            sp.wait_ge(x_cleared, 1)
            rows(0, True, False)
            with sp.Fori(1, GRID - 1) as gy:
                sp.wait_ge(x_split, gy * CHUNKS)
                rows(gy * RS, False, False)
            sp.wait_ge(x_split, (GRID - 1) * CHUNKS)
            rows((GRID - 1) * RS, False, True)
            sp.wait_ge(wd_ok, 3 * GRID * GRID + 1)
            load_attention_weights(sp.dma_start, a, Y1, next_loaded)
            sp.wait_ge(next_loaded, 16 * 4)

        @block.scalar
        def _(act):
            def param(dst, src):
                act.dma_start(dst, src, allow_slow_non_contiguous=True).then_inc(par, 16)

            param(w0s[:, :, :], a["w0"].rearrange("o c a b -> c o (a b)"))
            param(s0s[:, :], a["s0"].rearrange("(a o) -> a o", a=1).broadcast_to([CIN, CH]))
            param(T12[:, O_DW:O_BDW].rearrange("c (r t) -> c r t", t=9), a["wdw"].rearrange("(r c) u a b -> c r (u a b)", c=CH))
            param(s12[:, 0:REGIONS], a["sdw"].rearrange("(r c) -> c r", c=CH))
            param(T12[:, O_BDW:O_PW], a["bdw"].rearrange("(r c) -> c r", c=CH))
            param(T12[:, O_BPW:TW], a["bpw"].rearrange("(r c) -> c r", c=CH))
            param(T12[:, O_PW:O_BPW], a["wpw"].rearrange("q c u v -> c (q u v)"))
            param(s12[:, REGIONS:], a["spw"].rearrange("(a q) -> a q", a=1).broadcast_to([CH, 588]))
            param(b0s[:, :], a["b0"].rearrange("(c u) -> c u", u=1))
            param(w1s[:, :], a["w1"].rearrange("o c a b -> o (c a b)"))
            param(w2s[:, :], a["w2"].rearrange("o c a b -> o (c a b)"))
            param(w3s[:, :, :], a["w3"].rearrange("(h o) c a b -> o h (c a b)", h=2))
            param(s123[0:C2, 0:1], a["s1"].rearrange("(c u) -> c u", u=1))
            param(s123[0:C2, 1:2], a["s2"].rearrange("(c u) -> c u", u=1))
            param(s123[:, 2:4], a["s3"].rearrange("(h o) -> o h", h=2))
            param(b3v[:, :], a["b3"].rearrange("(h o) -> o h", h=2))
            for h in range(2):
                param(b1v[C2 * h:C2 * h + C2, :], a["b1"].rearrange("(c u) -> c u", u=1))
                param(b2v[C2 * h:C2 * h + C2, :], a["b2"].rearrange("(c u) -> c u", u=1))

            act.nop().then_inc(dw_act, 1)
            act.wait_ge(prep, PREP_DONE)
            with act.Fori(0, GRID) as gy:
                def high_part(q):
                    if q >= 2:
                        act.wait_ge(dw_mm, gy * 21 + q - 1)
                    act.activation(GR[:, q % 2, 0], G[:, q % 3, :, q // 3, :], ACT.Copy).then_inc(g_hi, 1)

                for c in range(CHUNKS):
                    s = c % 2 * 3
                    act.wait_ge(c0_mm, gy * CHUNKS + 1 + c + 1)
                    for t in range(3):
                        k = t // 2
                        dst = G[:, t, BC * c:BC * c + BC, :, 1:1 + RS]
                        src = ps[:, s + t, 0:BC * SIDE].rearrange("p (b g x) -> p b g x", b=BC, g=GRID)
                        act.activation(dst, src, ACT.Gelu, bias=b0v[:, k:k + 1]).then_inc(c0_act, 1)
                        if c == CHUNKS - 1 and t < 2:
                            act.wait_ge(c0_act, gy * (3 * CHUNKS) + (3 * c + t + 1))
                            high_part(t)

                def last_gelu(g):
                    for t in range(3):
                        act.wait_ge(pw_add, gy * 21 + 1 + 3 * g + t + 1)
                        v = G[:, t, :, g, 1:1 + RS]
                        if t < 2:
                            act.activation(v, v, ACT.Gelu).then_inc(g3, 1)
                            continue
                        for h in range(2):
                            for odd in range(2):
                                ins = act.activation(U[64 * odd:64 * odd + 64, h, :, g, :], v[64 * h:64 * h + 64, :, odd:RS:2], ACT.Gelu)
                        ins.then_inc(g3, 1)

                act.wait_ge(c0_act, gy * (3 * CHUNKS) + 3 * CHUNKS)
                for g in range(GRID):
                    act.wait_ge(wd_ok, gy * 21 + (3 * g + 4))
                    for t in range(3):
                        act.wait_ge(dw_mm, gy * 21 + 3 * g + t + 1)
                        if 3 * g + t + 2 < 3 * GRID:
                            high_part(3 * g + t + 2)
                        if g >= 2:
                            act.wait_ge(pw_mm, gy * 21 + 1 + 3 * (g - 1))
                        act.activation(D[:, g % 2, t, :], ps[:, t, :], ACT.Gelu,
                                       bias=BV[:, 0, t // 2, g:g + 1]).then_inc(dw_act, 1)
                    if g >= 1:
                        last_gelu(g - 1)
                last_gelu(GRID - 1)
                n = 0
                for h in range(2):
                    for t in range(2):
                        for i in range(2):
                            act.wait_ge(c1_mm, gy * 12 + 1 + n + 1)
                            act.activation(H1[:, t, h, 16 * i:16 * i + 16, :],
                                           ps[0:96, 6 + n % 2, 0:448].rearrange("p (b x) -> p b x", b=16),
                                           ACT.Gelu, bias=b1v[:, 0:1]).then_inc(c1_act, 1)
                            n += 1
                for h in range(2):
                    act.wait_ge(c1_mm, gy * 12 + 1 + n + 1)
                    act.activation(H2[:, h, :, :], ps[0:96, 6 + n % 2, 0:448].rearrange("p (b x) -> p b x", b=HALF),
                                   ACT.Gelu, bias=b2v[:, 0:1]).then_inc(c1_act, 1)
                    n += 1

        @block.gpsimd
        def _(pool):
            n = [0]

            def step(ins):
                n[0] += 1
                ins.then_inc(cst, 1)
                pool.wait_ge(cst, n[0])

            def mark(v, pattern, base, slope):
                step(pool.affine_select(out=v, in_=v, compare_op=ALU.not_equal, fill=1.0, base=base,
                                        pattern=pattern, channel_multiplier=slope))

            pool.memset(zrow[:, :], 0.0)
            pool.memset(X[:, :, :, :], 0.0).then_inc(x_cleared, 1)
            pool.wait_ge(x_cleared, 1)
            step(pool.memset(ident[:, :], 0.0))
            mark(ident[:, :], [[-1, P]], 0, 1)
            step(pool.memset(mY[:, :], 0.0))
            step(pool.memset(SEL[:, :, :], 0.0))
            mark(SEL[0:CH, 0, :].rearrange("c (j y) -> c j y", y=RS), [[-1, CB], [0, RS]], 0, 1)
            mark(SEL[0:CH, 1, :].rearrange("c (h j y) -> c h j y", h=2, y=RS), [[0, 2], [-1, CR], [0, RS]], -CB, 1)
            for lo in (0, KLO):
                mark(SEL[0:CIN, 2, lo:lo + KX].rearrange("c (j y) -> c j y", y=HALO), [[-1, CIN], [0, HALO]], 0, 1)
            mark(SEL[:, 3, :].rearrange("c (j y r) -> c j y r", j=CB, r=4), [[-4, CB], [0, Q], [-1, 4]], 0, 1)
            for h in range(2):
                mark(SEL[:, 4, 64 * h:64 * h + 64].rearrange("c (j y r) -> c j y r", j=CR, r=4),
                     [[-4, CR], [0, Q], [-1, 4]], -4 * CB, 1)
            step(pool.memset(mC[:, :], 1.0))
            step(pool.affine_select(out=mC[:, :], in_=mC[:, :], compare_op=ALU.is_ge, fill=0.0,
                                    base=0, pattern=[[-RS, CB]], channel_multiplier=1))
            step(pool.affine_select(out=mC[:, :], in_=mC[:, :], compare_op=ALU.is_ge, fill=0.0,
                                    base=RS - 1, pattern=[[RS, CB]], channel_multiplier=-1))
            step(pool.memset(zero_row[:, :], 0.0))
            assert n[0] == CST_MASKS, n[0]
            step(pool.memset(WP[:, :, :], 0.0))
            step(pool.memset(W2[:, :, :, :], 0.0))
            step(pool.memset(G[:, :, :, :, 0:1], 0.0))
            step(pool.memset(G[:, :, :, :, GW - 1:GW], 0.0))
            step(pool.memset(XT[:, :, :, :], 0.0))
            step(pool.memset(XT[96:97, 1, :, :], 1.0))
            assert n[0] == CST_DONE, n[0]

        @block.vector
        def _(dve):
            n = [0]

            def step(ins, wait=True):
                n[0] += 1
                ins.then_inc(prep, 1)
                if wait:
                    dve.wait_ge(prep, n[0])

            for s_ in (pw_add, wd_ok, wp_ok, c3_dve):
                dve.nop().then_inc(s_, 1)
            dve.wait_ge(cst, CST_MASKS)
            step(dve.tensor_reduce(mY[:, 1:1 + RS], ident[:, :].rearrange("p (j y) -> p y j", y=RS), AX_X, ALU.add))
            step(dve.tensor_tensor(mX[:, :], ident[0:KS, 0:HALO], ident[0:KS, HALO:2 * HALO], ALU.add))
            for j in (2 * HALO, KLO, KLO + HALO, KLO + 2 * HALO):
                step(dve.tensor_tensor(mX[:, :], mX[:, :], ident[0:KS, j:j + HALO], ALU.add))
            step(dve.tensor_reduce(m4[:, :], mY[:, 1:1 + RS].rearrange("p (j r) -> p j r", r=4), AX_X, ALU.add))
            dve.wait_ge(par, 16 * 20)
            v = T12[:, O_DW:O_BDW].rearrange("c (r t) -> c r t", t=9)
            step(dve.tensor_tensor(v, v, s12[:, 0:REGIONS].unsqueeze(2).broadcast_to([CH, REGIONS, 9]), ALU.mult))
            v = T12[:, O_PW:O_BPW]
            step(dve.tensor_tensor(v, v, s12[:, REGIONS:], ALU.mult))
            step(dve.tensor_tensor(w0c[:, :, :], w0s[:, :, :].rearrange("c o t -> c t o"),
                                   s0s[:, :].unsqueeze(1).broadcast_to([CIN, 9, CH]), ALU.mult))
            step(dve.tensor_scalar(w1s[:, :], w1s[:, :], s123[0:C2, 0:1], None, ALU.mult))
            step(dve.tensor_scalar(w2p[:, :, :, :], w2s[:, :].rearrange("o (c y x) -> o x y c", y=2, x=2),
                                   s123[0:C2, 1:2], None, ALU.mult))
            for h in range(2):
                step(dve.tensor_scalar(w3p[:, h], w3s[:, h, :].rearrange("o (c y x) -> o x y c", y=2, x=2),
                                       s123[:, 2 + h:3 + h], None, ALU.mult))
            assert n[0] == SCALED, n[0]
            dve.wait_ge(tr, 1)
            step(dve.tensor_copy(b0v[:, :], ps[:, 7, 0:2]), False)
            w0r = ps[0:KS, 6, 0:9 * CH].rearrange("p (y x c) -> p y x c", y=3, x=3)
            for dx in range(3):
                for dy in range(3):
                    m = mX[:, dy:dy + RS].unsqueeze(1).broadcast_to([KS, CH, RS])
                    w = w0r[:, dy, dx, :].unsqueeze(2).broadcast_to([KS, CH, RS])
                    if dy == 0:
                        step(dve.tensor_tensor(X0[:, dx], w, m, ALU.mult))
                    else:
                        step(dve.tensor_tensor(X1[:, dx], w, m, ALU.mult))
                        step(dve.tensor_tensor(X0[:, dx], X0[:, dx], X1[:, dx], ALU.add))
            zeros = zero_row[0:KS, 0:1].unsqueeze(1).broadcast_to([KS, 3, 320])
            for part in range(2):
                step(dve.tensor_copy(W0[:, part, :, :], zeros))
            full = X0.rearrange("p t c y -> p t (c y)")
            for lo, n_, to in ((0, P, 0), (P, 64, 192)):
                hi, v = W0[:, 0, :, to:to + n_], full[:, :, lo:lo + n_]
                step(dve.tensor_copy(hi, v))
                step(dve.tensor_tensor(W0[:, 1, :, to:to + n_], v, hi.bitcast(F32), ALU.subtract))
            for slot in range(2):
                for h in range(2):
                    step(dve.tensor_copy(XS[:, slot, h].rearrange("p b x -> p (b x)"), zero_row[0:KS, :].broadcast_to([KS, BC * XW])))
            dve.wait_ge(tr, 2)
            for k in range(2):
                for j, (lo, hi) in enumerate(TSPLIT):
                    step(dve.tensor_copy(TAB[:, k, lo:hi], ps[:, 3 * k + j, 0:hi - lo]), False)
            dve.wait_ge(cst, CST_DONE)
            dve.wait_ge(tr, 3)
            step(dve.tensor_copy(w1t[:, :, :], ps[0:C2, 0, 0:4 * C2].rearrange("p (k o) -> p k o", k=4)), False)
            for kx in range(2):
                for t in range(2):
                    step(dve.tensor_copy(W2[:, t, kx, C2 * t:C2 * t + C2], ps[0:96, 1, C2 * kx:C2 * kx + C2]), False)
            step(dve.tensor_copy(W3[:, :, :, :], ps[0:96, 2, 0:384].rearrange("p (k h o) -> p k h o", k=2, h=2)), False)
            assert n[0] == TRANSPOSED, n[0]
            dve.wait_ge(tr, 4)
            for t in range(2):
                for q in range(2):
                    row = m4[:, 2 * t + q:2 * t + q + 1]
                    step(dve.tensor_scalar(W1[:, t, :, C2 * q:C2 * q + C2], ps[:, 3, 0:4 * C2].rearrange("p (k o) -> p k o", k=4),
                                           row, None, ALU.mult), False)
                    for odd in range(2):
                        v = slice(64 * odd, 64 * odd + 64)
                        taps = ps[v, 4, 0:4 * C2].rearrange("p (k two o) -> p k two o", k=2, two=2)[:, :, odd, :]
                        step(dve.tensor_scalar(W1U[v, t, :, C2 * q:C2 * q + C2], taps, row[v], None, ALU.mult), False)
            dve.wait_ge(prep, n[0])
            while n[0] < PREP_DONE:
                step(dve.nop(), False)
            assert n[0] == PREP_DONE, n[0]

            def split(gy, c):
                if c == 0:
                    dve.wait_ge(x_loaded, gy * (16 * 18) + 16 * 12)
                if not (isinstance(gy, int) and gy == 0 and c < 2):
                    dve.wait_ge(c0_mm, gy * CHUNKS + 1 + c - 1)
                v = X[:, :, BC * c:BC * c + BC, :]
                hi = XS[0:KX, c % 2]
                for h in range(2):
                    ins = dve.tensor_copy(hi[:, h], v[:, h])
                ins.then_inc(x_hi, 1)
                dve.wait_ge(x_hi, gy * CHUNKS + c + 1)
                for h in range(2):
                    ins = dve.tensor_tensor(XS[KLO:KS, c % 2, h], v[:, h], hi[:, h].bitcast(F32), ALU.subtract)
                ins.then_inc(x_split, 1)

            def row(gy, last):
                done = [0]

                def chain(ins):
                    done[0] += 1
                    ins.then_inc(chained, 1)
                    dve.wait_ge(chained, gy * 10 + done[0])

                dve.wait_ge(pw_add, gy * 21 + 1)
                dve.wait_ge(dw_act, gy * 21 + 1)
                dve.wait_ge(wd_ok, gy * 21 + 1)
                dve.wait_ge(wp_ok, gy * GRID + 1)
                dve.wait_ge(pw_mm, gy * 21 + 1)
                for i, o in enumerate((O_BDW, O_BPW)):
                    dve.tensor_copy(BV[:, i], TAB[:, :, bass.ds(gy * GRID + o, GRID)])
                for k in range(2):
                    r = TAB[:, k, bass.ds(gy * (GRID * 9), GRID * 9)].rearrange("p (g y x) -> p g y x", g=GRID, y=3)
                    for dy in range(3):
                        m = mY[:, dy:dy + RS].unsqueeze(1).unsqueeze(1).broadcast_to([P, GRID, 3, RS])
                        w = r[:, :, dy, :].unsqueeze(3).broadcast_to([P, GRID, 3, RS])
                        if dy == 0:
                            chain(dve.tensor_tensor(AC[:, k], w, m, ALU.mult))
                        else:
                            chain(dve.tensor_tensor(ACt[:, :, :, :], w, m, ALU.mult))
                            chain(dve.tensor_tensor(AC[:, k], AC[:, k], ACt[:, :, :, :], ALU.add))

                def low_part(q):
                    if q < 3 * GRID:
                        dve.wait_ge(g_hi, gy * 21 + q + 1)
                        dve.tensor_tensor(GR[:, q % 2, 1], G[:, q % 3, :, q // 3, :], GR[:, q % 2, 0].bitcast(F32),
                                          ALU.subtract).then_inc(g_lo, 1)

                def depthwise_matrices(g):
                    s = g % 2
                    if g >= 2:
                        dve.wait_ge(dw_mm, gy * 21 + 3 * (g - 1))
                    for k in range(2):
                        ins = dve.tensor_tensor(WDF[:, k].rearrange("p x (c y) -> p x c y", y=RS),
                                                AC[:, k, g].unsqueeze(2).broadcast_to([P, 3, CB, RS]),
                                                mC[:, :].unsqueeze(1).unsqueeze(3).broadcast_to([P, 3, CB, RS]), ALU.mult)
                    ins.then_inc(wd_ok, 1)
                    dve.wait_ge(wd_ok, gy * 21 + (3 * g + 2))
                    dve.tensor_copy(WD[:, s, 0], WDF).then_inc(wd_ok, 1)
                    dve.wait_ge(wd_ok, gy * 21 + (3 * g + 3))
                    dve.tensor_tensor(WD[:, s, 1], WDF, WD[:, s, 0].bitcast(F32), ALU.subtract).then_inc(wd_ok, 1)
                    dve.wait_ge(wd_ok, gy * 21 + (3 * g + 4))

                def pointwise_matrices(g):
                    s = g % 2
                    if g >= 2:
                        dve.wait_ge(pw_mm, gy * 21 + 1 + 3 * (g - 1))
                    my = mY[:, 1:1 + RS]
                    for k, col, lo, n_, rows_ in ((0, 0, 0, CH, slice(0, P)), (1, 192, 0, CB, slice(0, P)),
                                                  (1, 320, CB, CR, slice(0, 64)), (1, 384, CB, CR, slice(64, P))):
                        np_ = rows_.stop - rows_.start
                        w = TAB[rows_, k, bass.ds(gy * (GRID * CH) + (O_PW + g * CH + lo), n_)]
                        ins = dve.tensor_tensor(WP[rows_, s, col:col + RS * n_].rearrange("p (c y) -> p c y", y=RS),
                                                w.unsqueeze(2).broadcast_to([np_, n_, RS]),
                                                my[rows_].unsqueeze(1).broadcast_to([np_, n_, RS]), ALU.mult)
                    ins.then_inc(wp_ok, 1)

                def add(g):
                    for t in range(3):
                        dve.wait_ge(pw_mm, gy * 21 + 1 + 3 * g + t + 1)
                        v = G[:, t, :, g, 1:1 + RS]
                        dve.scalar_tensor_tensor(out=v, in0=ps[:, 3 + t, :].rearrange("p (b x) -> p b x", b=HALF),
                                                 scalar=BV[:, 1, t // 2, g:g + 1], in1=v,
                                                 op0=ALU.add, op1=ALU.add).then_inc(pw_add, 1)

                for c in range(2, CHUNKS):
                    split(gy, c)
                    if c >= CHUNKS - 2:
                        depthwise_matrices(c - (CHUNKS - 2))
                        pointwise_matrices(c - (CHUNKS - 2))
                for q in range(5):
                    low_part(q)
                for g in range(GRID):
                    for q in range(3 * g + 5, 3 * g + 8):
                        low_part(q)
                    if g + 2 < GRID:
                        depthwise_matrices(g + 2)
                    add(g)
                    if g + 2 < GRID:
                        pointwise_matrices(g + 2)
                if not last:
                    split(gy + 1, 0)
                    split(gy + 1, 1)
                for o in range(2):
                    dve.wait_ge(c1_mm, gy * 12 + 1 + 11 + o)
                    for h in range(2):
                        dve.tensor_scalar(XT[0:96, o, :, bass.ds(gy * GRID + SLOT * h, GRID)],
                                          ps[0:96, 6 + o, 224 * h:224 * h + 224].rearrange("p (b x) -> p b x", b=HALF),
                                          b3v[:, o:o + 1], None, ALU.add).then_inc(c3_dve, 1)

            split(0, 0)
            split(0, 1)
            with dve.Fori(0, GRID - 1) as gy:
                row(gy, False)
            row(GRID - 1, True)

        @block.tensor
        def _(pe):
            mm = nc.tensor.matmul
            for s in (pw_mm, c1_mm, c0_mm):
                pe.nop().then_inc(s, 1)
            pe.wait_ge(prep, SCALED)
            mm(ps[0:KS, 6, 0:9 * CH], SEL[0:CIN, 2, 0:KS], w0c[:, :, :].rearrange("c t o -> c (t o)"), start=True, stop=True)
            for k in range(2):
                ins = mm(ps[:, 7, k:k + 1], SEL[0:CH, k, :], b0s[:, :], start=True, stop=True)
            ins.then_inc(tr, 1)
            for k in range(2):
                for j, (lo, hi) in enumerate(TSPLIT):
                    ins = mm(ps[:, 3 * k + j, 0:hi - lo], SEL[0:CH, k, :], T12[:, lo:hi], start=True, stop=True)
            ins.then_inc(tr, 1)
            pe.wait_ge(prep, COPIED)
            for kx in range(4):
                nc.tensor.transpose(ps[0:C2, 0, C2 * kx:C2 * kx + C2], w1s[:, kx:kx + 4 * (C2 - 1) + 1:4], ident[0:C2, 0:C2])
            for kx in range(2):
                v = w2p[:, kx].rearrange("o y c -> o (y c)")
                nc.tensor.transpose(ps[0:96, 1, C2 * kx:C2 * kx + C2], v, ident[0:C2, 0:C2])
                for h in range(2):
                    v = w3p[:, h, kx].rearrange("o y c -> o (y c)")
                    ins = nc.tensor.transpose(ps[0:96, 2, 192 * kx + 96 * h:192 * kx + 96 * h + 96], v, ident[0:96, 0:96])
            ins.then_inc(tr, 1)
            pe.wait_ge(prep, TRANSPOSED)
            for k in range(2):
                ins = mm(ps[:, 3 + k, 0:4 * C2], SEL[:, 3 + k, :], w1t[:, :, :].rearrange("p k o -> p (k o)"), start=True, stop=True)
            ins.then_inc(tr, 1)
            pe.wait_ge(prep, PREP_DONE)
            with pe.Fori(0, GRID) as gy:
                for c in range(CHUNKS):
                    s = c % 2 * 3
                    if c == 0:
                        pe.wait_ge(dw_act, gy * 21 + 1)
                        pe.wait_ge(c1_mm, gy * 12 + 1)
                    elif c == 1:
                        pe.wait_ge(pw_add, gy * 21 + 1)
                    else:
                        pe.wait_ge(c0_act, gy * (3 * CHUNKS) + 3 * (c - 1))
                    pe.wait_ge(x_split, gy * CHUNKS + c + 1)
                    for out, h, lo, first, last in ((ps[:, s], 0, 0, True, True), (ps[:, s + 1], 1, 0, True, True),
                                                    (ps[:, s + 2], 0, 192, True, False), (ps[:, s + 2], 1, P, False, True)):
                        for kx in range(3):
                            for part in range(2):
                                ins = mm(out[:, 0:BC * SIDE], W0[:, part, kx, lo:lo + P], XS[:, c % 2, h, :, kx:kx + SIDE],
                                         start=(first and kx + part == 0), stop=(last and kx + part == 3))
                    ins.then_inc(c0_mm, 1)

                def depthwise(g):
                    pe.wait_ge(wd_ok, gy * 21 + (3 * g + 4))
                    for t in range(3):
                        if g == 0:
                            pe.wait_ge(c0_act, gy * (3 * CHUNKS) + (3 * CHUNKS - 2 + t))
                        else:
                            pe.wait_ge(dw_act, gy * 21 + 1 + 3 * (g - 1) + t + 1)
                        pe.wait_ge(g_lo, gy * 21 + (3 * g + t + 1))
                        n = 0
                        for pw, pg in ((0, 0), (0, 1), (1, 0)):
                            for kx in range(3):
                                n += 1
                                ins = mm(ps[:, t, :], WD[:, g % 2, pw, t // 2, kx, :], GR[:, (3 * g + t) % 2, pg, :, kx:kx + RS],
                                         start=(n == 1), stop=(n == 9))
                        ins.then_inc(dw_mm, 1)

                def pointwise(g):
                    pe.wait_ge(wp_ok, gy * GRID + 1 + g + 1)
                    w = WP[:, g % 2, :]
                    d = D[:, g % 2]
                    for t in range(2):
                        pe.wait_ge(dw_act, gy * 21 + 1 + 3 * g + 3)
                        if g >= 1:
                            pe.wait_ge(pw_add, gy * 21 + 1 + 3 * (g - 1) + t + 1)
                        half = slice(64 * t, 64 * t + 64)
                        mm(ps[:, 3 + t, :], w[:, 0:P], d[:, t, :], start=True, stop=False)
                        mm(ps[:, 3 + t, :], w[half, 192:320], d[half, 2, :], start=False, stop=True).then_inc(pw_mm, 1)
                    if g >= 1:
                        pe.wait_ge(pw_add, gy * 21 + 1 + 3 * g)
                    mm(ps[:, 5, :], w[:, 320:448], d[:, 2, :], start=True, stop=False)
                    mm(ps[0:64, 5, :], w[:, P:192], d[:, 0, :], start=False, stop=True)
                    mm(ps[64:P, 5, :], w[:, P:192], d[:, 1, :], start=False, stop=True).then_inc(pw_mm, 1)

                depthwise(0)
                for g in range(GRID):
                    if g + 1 < GRID:
                        depthwise(g + 1)
                    pointwise(g)
                n = 0
                for h in range(2):
                    for t in range(2):
                        for i in range(2):
                            if n < 2:
                                pe.wait_ge(c3_dve, gy * 4 + 1)
                            else:
                                pe.wait_ge(c1_act, gy * 10 + n - 1)
                            out = ps[0:96, 6 + n % 2, 0:448]
                            b = slice(16 * i, 16 * i + 16)
                            pe.wait_ge(g3, gy * 21 + 19 + h)
                            for kx in range(4):
                                mm(out, W1[:, t, kx, :], G[:, h, b, :, 1 + kx:1 + RS:4], start=(kx == 0), stop=False)
                            if n == 0:
                                pe.wait_ge(g3, gy * 21 + 21)
                            for pair in range(2):
                                ins = mm(out, W1U[:, t, pair, :], U[:, h, b, :, pair:RS // 2:2], start=False, stop=(pair == 1))
                            ins.then_inc(c1_mm, 1)
                            n += 1
                for h in range(2):
                    pe.wait_ge(c1_act, gy * 10 + 4 * h + 4)
                    pe.wait_ge(c1_act, gy * 10 + n - 1)
                    out = ps[0:96, 6 + n % 2, 0:448]
                    for t in range(2):
                        for kx in range(2):
                            ins = mm(out, W2[:, t, kx, :], H1[:, t, h, :, kx:28:2], start=(t + kx == 0), stop=(t + kx == 2))
                    ins.then_inc(c1_mm, 1)
                    n += 1
                pe.wait_ge(c1_act, gy * 10 + 10)
                for o in range(2):
                    for h in range(2):
                        for kx in range(2):
                            ins = mm(ps[0:96, 6 + o, 224 * h:224 * h + 224], W3[:, kx, o, :], H2[:, h, :, kx:14:2],
                                     start=(kx == 0), stop=(kx == 1))
                    ins.then_inc(c1_mm, 1)


def attention_weights(Y1):
    space = Y1[:, :, :].rearrange("p j d -> p (j d)")
    lo = HALF * E - 6 * E - 2 * TOKENS - 2 * E
    WQ = space[0:EH + 1, lo:lo + 6 * E].rearrange("p (h n) -> p h n", h=2)
    WGP = space[0:EH, lo + 6 * E:lo + 6 * E + 2 * TOKENS].rearrange("p (h n) -> p h n", h=2)
    WPJ = space[0:EH, lo + 6 * E + 2 * TOKENS:HALF * E].rearrange("p (h n) -> p h n", h=2)
    return WQ, WGP, WPJ


def load_attention_weights(dma, a, Y1, done):
    WQ, WGP, WPJ = attention_weights(Y1)
    dma(WQ[0:EH, :, :], a["wqkv"].rearrange("(h k) n -> k h n", h=2)).then_inc(done, 16)
    dma(WQ[EH:EH + 1, 1, :], a["bqkv"].rearrange("(u n) -> u n", u=1)).then_inc(done, 16)
    dma(WGP[:, :, :], a["wgp"].rearrange("(h k) n -> k h n", h=2)).then_inc(done, 16)
    dma(WPJ[:, :, :], a["wproj"].rearrange("(h k) n -> k h n", h=2)).then_inc(done, 16)


def attention_phase(nc, a, XT, Y1, ident):
    PAIRS = HALF
    GP = 4
    STEPS = PAIRS // GP
    KG = 49
    EA = EH + 1
    HK = ((slice(0, EH), 0), (slice(0, EA), 1))
    with ExitStack() as ctx:
        def sb(name, shape, dt=F32):
            return ctx.enter_context(nc.sbuf_tensor(name, shape, dt))

        def sem(name):
            return ctx.enter_context(nc.semaphore(name))

        WQ, WGP, WPJ = attention_weights(Y1)
        WQT = sb("WQT", [EH, 3, 2, E + 1])
        GM = sb("GM", [EA, 2, E + 1])
        WR = sb("WR", [EA, 2, KG + 2 * E])
        XP = sb("XP", [EA, 2, GP, P])
        UT = sb("UT", [EA, 2, GP, P])
        VP = sb("VP", [P, PAIRS, 2 * E])
        SC = sb("SC", [P, PAIRS, KG])
        GA = sb("GA", [P, PAIRS, KG])
        GG = sb("GG", [P, PAIRS, KG])
        GT = sb("GT", [P, GP, P])
        red = sb("red", [P, PAIRS])
        inv = sb("inv", [P, PAIRS])
        al = sb("al", [P, 3])
        BD = sb("BD", [P, GP, P])
        BT = sb("BT", [P, GP, P])
        st = sb("st", [P, GP, 6])
        ms = sb("ms", [P, GP, 2])
        yb = sb("yb", [P, GP, E])
        scratch = sb("scratch", [P, 1])
        mv = sb("mv", [P, PAIRS, 2])
        eps = sb("eps", [P, PAIRS, 2])
        ps = ctx.enter_context(nc.psum_tensor("psa", [P, 8, 512], F32))

        par = sem("a_par")
        prep = sem("a_prep")
        tr = sem("a_tr")
        zero = sem("a_zero")
        xp = sem("a_xp")
        r_mm = sem("a_r_mm")
        u_mm = sem("a_u_mm")
        u_cp = sem("a_u_cp")
        s_mm = sem("a_s_mm")
        s_cp = sem("a_s_cp")
        glu = sem("a_glu")
        soft = sem("a_soft")
        ex = sem("a_ex")
        gt_mm = sem("a_gt_mm")
        gt_cp = sem("a_gt_cp")
        gg_mm = sem("a_gg_mm")
        gg_cp = sem("a_gg_cp")
        bd = sem("a_bd")
        bt_mm = sem("a_bt_mm")
        bt_cp = sem("a_bt_cp")
        o_mm = sem("a_o_mm")
        o_cp = sem("a_o_cp")
        y_cp = sem("a_y_cp")
        stat = sem("a_stat")
        rstd = sem("a_rstd")
        block = ctx.enter_context(nc.Block())

        BY_DVE = 27

        def normalized(eng, j):
            return eng.tensor_scalar(Y1[:, j, :], Y1[:, j, :], mv[:, j, 0:1], mv[:, j, 1:2], ALU.subtract, ALU.mult)

        @block.sync
        def _(sp):
            def param(dst, src):
                sp.dma_start(dst, src).then_inc(par, 16)

            param(WR[EH:EA, 1, KG + E:], a["bproj"].rearrange("(u n) -> u n", u=1))
            param(al[:, 0:1], a["alpha"].rearrange("(u n) -> u n", u=1).broadcast_to([P, 1]))

        @block.gpsimd
        def _(pool):
            pool.memset(BD[:, :, :], 0.0)
            pool.memset(eps[:, :, 0:1], 1e-5)
            pool.memset(eps[:, :, 1:2], -0.5).then_inc(zero, 1)
            pool.wait_ge(stat, 2 + 3 * STEPS)
            pool.tensor_tensor(mv[:, :, 1:2], mv[:, :, 1:2], eps[:, :, 0:1], ALU.add).then_inc(rstd, 1)
            pool.wait_ge(rstd, 1)
            pool.tensor_tensor(mv[:, :, 1:2], mv[:, :, 1:2], eps[:, :, 1:2], ALU.pow).then_inc(rstd, 1)
            pool.wait_ge(rstd, 2)
            pool.wait_ge(y_cp, STEPS + 1)
            for j in range(BY_DVE, PAIRS):
                normalized(pool, j).then_inc(rstd, 1)
                pool.wait_ge(rstd, 3 + j - BY_DVE)

        @block.tensor
        def _(pe):
            mm = nc.tensor.matmul
            for done in (s_mm, gt_mm, gg_mm, bt_mm, o_mm, r_mm):
                pe.nop().then_inc(done, 1)
            for w in range(3):
                for o in range(2):
                    nc.tensor.transpose(ps[0:EH, 2 * w + o, 0:EH], WQ[0:EH, 0, E * w + EH * o:E * w + EH * o + EH], ident[0:EH, 0:EH])
                    ins = nc.tensor.transpose(ps[0:EH, 2 * w + o, EH:E + 1], WQ[:, 1, E * w + EH * o:E * w + EH * o + EH], ident[0:EA, 0:EA])
            ins.then_inc(tr, 1)
            pe.wait_ge(prep, 6)
            for i, (lo, n) in enumerate(((0, EH), (EH, EA))):
                for o in range(2):
                    mm(ps[0:n, i, 0:E + 1], WQT[:, 0, o, lo:lo + n], WQT[:, 1, o, :], start=(o == 0), stop=(o == 1))
                for o in range(2):
                    mm(ps[0:n, 2 + i, 0:KG], WQT[:, 2, o, lo:lo + n], WGP[:, o, :], start=(o == 0), stop=(o == 1))
                for o in range(2):
                    ins = mm(ps[0:n, 4 + i, 0:E], WQT[:, 2, o, lo:lo + n], WPJ[:, o, :], start=(o == 0), stop=(o == 1))
            ins.then_inc(tr, 1)
            pe.wait_ge(prep, 14)
            pe.wait_ge(par, 16 * 2)

            with pe.Fori(0, STEPS) as g:
                pe.wait_ge(u_cp, g + 1)
                for o, n in ((0, EH), (1, EA)):
                    for rows, h in HK:
                        ins = mm(ps[0:n, o, :], GM[rows, h, EH * o:EH * o + n], XT[rows, h, bass.ds(g * GP, GP), :],
                                 start=(h == 0), stop=(h == 1))
                ins.then_inc(u_mm, 1)
                pe.wait_ge(xp, g + 1)
                for k in range(GP):
                    pe.wait_ge(glu, g * GP + (k + 1))
                    for rows, h in HK:
                        ins = mm(ps[:, 2 + k, 0:KG + 2 * E], XP[rows, h, k, :], WR[rows, h, :], start=(h == 0), stop=(h == 1))
                    ins.then_inc(r_mm, 1)
                pe.wait_ge(u_cp, g + 2)
                pe.wait_ge(s_cp, g + 1)
                for k in range(GP):
                    for i in range(2):
                        c = slice(SLOT * i, SLOT * i + SLOT)
                        for rows, h in HK:
                            ins = mm(ps[c, 6, KG * k:KG * k + KG], UT[rows, h, k, c], XP[rows, h, k, SLOT * i:SLOT * i + KG],
                                     start=(h == 0), stop=(h == 1))
                ins.then_inc(s_mm, 1)
            pe.wait_ge(soft, 5)
            with pe.Fori(0, STEPS) as g:
                pe.wait_ge(gt_cp, g + 1)
                pe.wait_ge(bd, g + 1)
                for k in range(GP):
                    ins = nc.tensor.transpose(ps[:, 0, P * k:P * k + P], BD[:, k, :], ident[:, :])
                ins.then_inc(gt_mm, 1)
                pe.wait_ge(gt_cp, g + 2)
                pe.wait_ge(gg_cp, g + 1)
                for k in range(GP):
                    for i in range(2):
                        c = slice(SLOT * i, SLOT * i + SLOT)
                        ins = mm(ps[c, 1, KG * k:KG * k + KG], GT[:, k, c], GT[:, k, SLOT * i:SLOT * i + KG], start=True, stop=True)
                ins.then_inc(gg_mm, 1)
            with pe.Fori(0, STEPS) as g:
                pe.wait_ge(bd, g + (STEPS + 1))
                pe.wait_ge(bt_cp, g + 1)
                for k in range(GP):
                    ins = nc.tensor.transpose(ps[:, 4, P * k:P * k + P], BD[:, k, :], ident[:, :])
                ins.then_inc(bt_mm, 1)
                pe.wait_ge(bt_cp, g + 2)
                pe.wait_ge(o_cp, g + 1)
                for k in range(GP):
                    lo = E * (k % 2)
                    ins = mm(ps[:, 2 + k // 2, lo:lo + E], BT[:, k, :], VP[:, bass.ds(g * GP + k, 1), 0:E], start=True, stop=True)
                ins.then_inc(o_mm, 1)

        @block.scalar
        def _(act):
            act.nop().then_inc(glu, GP)
            act.nop().then_inc(y_cp, 1)
            act.wait_ge(par, 16 * 2)
            act.activation(al[:, 1:2], al[:, 0:1], ACT.Sigmoid)
            act.activation(al[:, 2:3], al[:, 0:1], ACT.Sigmoid, scale=-1.0).then_inc(ex, 1)
            with act.Fori(0, STEPS) as g:
                for k in range(GP):
                    act.wait_ge(r_mm, g * GP + (k + 2))
                    act.activation(GA[:, bass.ds(g * GP + k, 1), :], ps[:, 2 + k, 0:KG], ACT.Gelu)
                    act.activation(VP[:, bass.ds(g * GP + k, 1), :], ps[:, 2 + k, KG:KG + 2 * E], ACT.Copy).then_inc(glu, 1)
            act.wait_ge(soft, 2)
            act.activation(GA[:, :, :], GA[:, :, :], ACT.Exp).then_inc(ex, 1)
            act.wait_ge(soft, 7)
            act.activation(SC[:, :, :], SC[:, :, :], ACT.Exp).then_inc(ex, 1)
            with act.Fori(0, STEPS) as g:
                act.wait_ge(o_cp, g + 2)
                act.activation(Y1[:, bass.ds(g * GP, GP), :], yb[:, :, :], ACT.Copy).then_inc(y_cp, 1)

        @block.vector
        def _(dve):
            for ready in (u_cp, s_cp, gt_cp, gg_cp, bt_cp, o_cp):
                dve.nop().then_inc(ready, 1)
            dve.wait_ge(tr, 1)
            for w in range(3):
                for o in range(2):
                    dve.tensor_copy(WQT[:, w, o, :], ps[0:EH, 2 * w + o, 0:E + 1]).then_inc(prep, 1)
            dve.wait_ge(tr, 2)
            for i, n in enumerate((EH, EA)):
                dve.tensor_copy(GM[0:n, i, :], ps[0:n, i, 0:E + 1]).then_inc(prep, 1)
                dve.tensor_copy(WR[0:n, i, 0:KG], ps[0:n, 2 + i, 0:KG]).then_inc(prep, 1)
                dve.tensor_copy(WR[0:n, i, KG:KG + E], ps[0:n, 4 + i, 0:E]).then_inc(prep, 1)
            dve.memset(WR[0:EH, :, KG + E:], 0.0).then_inc(prep, 1)
            dve.wait_ge(prep, 13)
            for i in range(2):
                ins = dve.tensor_copy(WR[0:EH, i, KG + E + EH * i:KG + E + EH * i + EH], ident[0:EH, 0:EH])
            ins.then_inc(prep, 1)

            with dve.Fori(0, STEPS) as g:
                dve.wait_ge(s_mm, g + 1)
                dve.tensor_copy(XP[0:EH, 0, :, :], XT[0:EH, 0, bass.ds(g * GP, GP), :])
                dve.tensor_copy(XP[:, 1, :, :], XT[0:EA, 1, bass.ds(g * GP, GP), :]).then_inc(xp, 1)
                dve.wait_ge(u_mm, g + 1)
                dve.tensor_copy(UT[0:EH, 0, :, :], ps[0:EH, 0, :].rearrange("p (k n) -> p k n", k=GP))
                dve.tensor_copy(UT[:, 1, :, :], ps[0:EA, 1, :].rearrange("p (k n) -> p k n", k=GP)).then_inc(u_cp, 1)
                dve.wait_ge(s_mm, g + 2)
                dve.tensor_scalar(SC[:, bass.ds(g * GP, GP), :], ps[:, 6, 0:GP * KG].rearrange("p (k n) -> p k n", k=GP),
                                  float(E) ** -0.5, None, ALU.mult).then_inc(s_cp, 1)

            done = [0]

            def step(ins):
                done[0] += 1
                ins.then_inc(soft, 1)
                dve.wait_ge(soft, done[0])

            def wide(v):
                return v[:, :].unsqueeze(2).broadcast_to([P, PAIRS, KG])

            dve.wait_ge(glu, PAIRS + GP)
            step(dve.tensor_reduce(red[:, :], GA[:, :, :], AX_X, ALU.max))
            step(dve.tensor_tensor(GA[:, :, :], GA[:, :, :], wide(red), ALU.subtract))
            dve.wait_ge(ex, 2)
            step(dve.tensor_reduce(red[:, :], GA[:, :, :], AX_X, ALU.add))
            step(dve.reciprocal(inv[:, :], red[:, :]))
            step(dve.tensor_tensor(GA[:, :, :], GA[:, :, :], wide(inv), ALU.mult))
            dve.wait_ge(zero, 1)

            def group_copy(g):
                dve.wait_ge(gt_mm, g + 1)
                at = bass.ds(g * GP, GP) if not isinstance(g, int) else slice(GP * g, GP * g + GP)
                dve.tensor_copy(BD[:, :, 0:KG], GA[:, at, :]).then_inc(bd, 1)

            def group_step(g, last):
                dve.wait_ge(gg_mm, g + 1)
                dve.wait_ge(gt_mm, g + 2)
                dve.tensor_copy(GT[:, :, :], ps[:, 0, :].rearrange("p (k n) -> p k n", k=GP)).then_inc(gt_cp, 1)
                if not last:
                    group_copy(g + 1)
                dve.wait_ge(gg_mm, g + 2)
                at = bass.ds(g * GP, GP) if not isinstance(g, int) else slice(GP * g, GP * g + GP)
                dve.tensor_copy(GG[:, at, :], ps[:, 1, 0:GP * KG].rearrange("p (k n) -> p k n", k=GP)).then_inc(gg_cp, 1)

            group_copy(0)
            with dve.Fori(0, STEPS - 1) as g:
                group_step(g, False)
            group_step(STEPS - 1, True)
            dve.wait_ge(gg_cp, STEPS + 1)
            dve.wait_ge(s_cp, STEPS + 1)
            dve.tensor_tensor(SC[:, :, :], SC[:, :, :], GG[:, :, :], ALU.mult).then_inc(stat, 1)
            dve.wait_ge(stat, 1)
            step(dve.tensor_reduce(red[:, :], SC[:, :, :], AX_X, ALU.max))
            step(dve.tensor_tensor(SC[:, :, :], SC[:, :, :], wide(red), ALU.subtract))
            dve.wait_ge(ex, 3)
            step(dve.tensor_reduce(red[:, :], SC[:, :, :], AX_X, ALU.add))
            step(dve.reciprocal(inv[:, :], red[:, :]))
            step(dve.tensor_scalar(inv[:, :], inv[:, :], al[:, 2:3], None, ALU.mult))
            step(dve.tensor_tensor(SC[:, :, :], SC[:, :, :], wide(inv), ALU.mult))
            step(dve.scalar_tensor_tensor(out=SC[:, :, :], in0=GG[:, :, :], scalar=al[:, 1:2], in1=SC[:, :, :],
                                          op0=ALU.mult, op1=ALU.add))
            dve.memset(BD[SLOT:P, :, 0:SLOT], 0.0).then_inc(stat, 1)
            dve.wait_ge(stat, 2)

            def weights_copy(g):
                dve.wait_ge(bt_mm, g + 1)
                at = bass.ds(g * GP, GP) if not isinstance(g, int) else slice(GP * g, GP * g + GP)
                for i in range(2):
                    r = slice(SLOT * i, SLOT * i + SLOT)
                    ins = dve.tensor_copy(BD[r, :, SLOT * i:SLOT * i + KG], SC[r, at, :])
                ins.then_inc(bd, 1)

            def output_step(g, last):
                at = bass.ds(g * GP, GP) if not isinstance(g, int) else slice(GP * g, GP * g + GP)
                dve.wait_ge(o_mm, g + 1)
                dve.wait_ge(bt_mm, g + 2)
                dve.tensor_copy(BT[:, :, :], ps[:, 4, :].rearrange("p (k n) -> p k n", k=GP)).then_inc(bt_cp, 1)
                if not last:
                    weights_copy(g + 1)
                dve.wait_ge(y_cp, g + 1)
                dve.wait_ge(o_mm, g + 2)
                dve.tensor_tensor(yb[:, :, :].rearrange("p (b k) d -> p b k d", b=2),
                                  ps[:, 2:4, 0:2 * E].rearrange("p b (k d) -> p b k d", k=2),
                                  VP[:, at, E:].rearrange("p (b k) d -> p b k d", b=2), ALU.add).then_inc(o_cp, 1)
                dve.wait_ge(o_cp, g + 2)
                for k in range(GP):
                    ins = dve.bn_stats(st[:, k, :], yb[:, k, :])
                ins.then_inc(stat, 1)
                dve.wait_ge(stat, g * 3 + 3)
                dve.memset(scratch[:, :], 0.0)
                for k in range(GP):
                    ins = dve.bn_aggr(ms[:, k, :], st[:, k, :])
                ins.then_inc(stat, 1)
                dve.wait_ge(stat, g * 3 + 4)
                dve.tensor_copy(mv[:, at, :], ms[:, :, :]).then_inc(stat, 1)

            weights_copy(0)
            with dve.Fori(0, STEPS - 1) as g:
                output_step(g, False)
            output_step(STEPS - 1, True)
            dve.wait_ge(y_cp, STEPS + 1)
            dve.wait_ge(rstd, 2)
            for j in range(BY_DVE):
                ins = normalized(dve, j)
            step(ins)


EXPERTS, HID = 4, 768
SLOTS = 256
NS = EXPERTS * SLOTS
SCH = NS // P
HH = HID // 2
STEP = 8
UNITS = EXPERTS * STEP
HS = 8
EXP_AT, AHEAD = 21, 4
LAG = 4
ROTATING = 3
JOBS = ("y", "l", "t", "w", "d", "c", "zt")


def unit(u):
    return u // 8, u // 4 % 2, u // 2 % 2, u % 2


MOVED = {("c", 1): -1, ("w2", 1, 1): 2, ("w", 0, 0): -1, ("w2", 2, 0): 2, ("w", 0, 1): 2, ("c", 2): 1}


def pair_items():
    items = [(item, at - UNITS) for item, at in (
        (("y", 0), 1), (("y", 1), 4), (("l", 0), 13), (("l", 1), 15),
        (("t", 0), 20), (("t", 1), 20), (("exp",), EXP_AT), (("dt",), 21))]
    for e in range(EXPERTS):
        s = STEP * (e - 1)
        items += [(("w", e, 0), s + 0), (("d", e), s + 2), (("w", e, 1), s + 3), (("c", e), s + 5)]
        for half in range(2):
            s = STEP * e + 4 * half + LAG
            items += [(("ze", e, half, img), s + 2 * img + 1) for img in range(2)]
            items += [(("zt", e, half), s + 5), (("w2", e, half), s + 9)]
    items = [(item, at + MOVED.get(item, 0)) for item, at in items]
    items += [(("h", u), u) for u in range(UNITS)]
    items += [(("z", u), min(u + LAG, EXP_AT + 1) if EXP_AT - AHEAD <= u < EXP_AT else u + LAG) for u in range(UNITS)]
    return items + [(("out",), UNITS + 8), (("norm",), UNITS + 14)]


ORDER = ("h", "z", "ze", "w2", "out", "y", "l", "zt", "exp", "dt", "w", "d", "c", "t", "norm")
LATER = {"pe": {}, "pool": {}, "act": {}, "dve": {"h": 1}}


def ffn_stage(pairs, engine):
    found = []
    for r in pairs:
        for item, at in pair_items():
            later = LATER[engine].get(item[0], 0)
            t = at + UNITS * r
            assert item[0] not in JOBS or (t // UNITS == (t + later) // UNITS)
            if 0 <= t + later < UNITS:
                found.append((t + later, ORDER.index(item[0]), item, r))
    return [(r, item) for _, _, item, r in sorted(found)]


def jobs_of(pairs):
    jobs = [x for x in ffn_stage(pairs, "pe") if x[1][0] in JOBS]
    return {x: n for n, x in enumerate(jobs)}


JOBS_BEFORE_0 = len(jobs_of((1,)))
JOBS_BEFORE_1 = JOBS_BEFORE_0 + len(jobs_of((0, 1)))
STAGE_JOBS = len(jobs_of((-1, 0, 1)))
assert STAGE_JOBS % ROTATING == 0


class Stage:

    def __init__(self, engine, j, parity, pairs):
        self.j, self.parity = j, parity
        self.events, self.jobs = ffn_stage(pairs, engine), jobs_of(pairs)
        self.fixed = isinstance(j, int) and j < 1
        if self.fixed:
            self.first = JOBS_BEFORE_0 if j == 0 else 0
        else:
            self.first = JOBS_BEFORE_1 - (JOBS_BEFORE_0 if pairs == (-1,) else 0)

    def times(self, r, per, more):
        if isinstance(self.j, int):
            v = (self.j + r) * per + more
            return v if v > 0 else None
        assert (1 + r) * per + more > 0
        return self.j * per + (r * per + more)

    def job(self, n):
        if self.fixed:
            return self.first + n if self.first + n > 0 else None
        return self.times(-1, STAGE_JOBS, self.first + n)

    def bank(self, n):
        return (self.first + n) % ROTATING

    def ready(self, r, *items):
        return self.job(max([self.jobs[r, i] + 1 for i in items if (r, i) in self.jobs], default=0))


def ffn_phase(nc, a, Y1, ident, out):
    PAIRS = HALF
    KT = TOKENS
    EA = EH + 1
    HK = ((slice(0, EH), 0), (slice(0, EA), 1))
    IMG = (slice(0, SLOT), slice(SLOT, P))
    with ExitStack() as ctx:
        def sb(name, shape, dt=F32):
            return ctx.enter_context(nc.sbuf_tensor(name, shape, dt))

        def sem(name):
            return ctx.enter_context(nc.semaphore(name))

        PT = sb("PT", [EH, 2, 2, NS], F32R)
        W1 = sb("FW1", [EA, 2, 2, EXPERTS * HID], F32R)
        W2 = sb("FW2", [P, EXPERTS * HID // P, E])
        B2 = sb("FB2", [P, EXPERTS, E])
        YP = sb("YP", [P, 2, E])
        YT = sb("YT", [EA, 2, 2, 2, P], F32R)
        LS = sb("LS", [P, NS])
        C = sb("C", [P, 2, NS])
        CS = sb("CS", [P, 2, EXPERTS])
        LT = sb("LT", [P, SCH, 2, KT])
        DT = sb("DT", [P, SCH, 2, 2, SLOT])
        CT = sb("CT", [P, 2, 2, 2, 2, SLOT], F32R)
        D = sb("FD", [P, 2, 2, 2, SLOTS], F32R)
        R = sb("R", [P, 2, 2, HID], F32R)
        HF = sb("HF", [P, 4, HH])
        HI = sb("HI", [P, HS, HH], F32R)
        HL = sb("HL", [P, HS, HH], F32R)
        ZF = sb("ZF", [P, 2, HH])
        ZS = sb("ZS", [P, 2, 2, HH])
        ZT = sb("ZT", [P, 2, 3, P])
        ones = sb("ones", [P, 2])
        mx = sb("mx", [P, 2])
        mt = sb("mt", [P, 2 * SCH])
        mi = sb("mi", [P, 2 * SCH])
        ss = sb("ss", [P, 2])
        acc = sb("acc", [P, E])
        o = sb("fo", [P, 2, E])
        st = sb("fst", [P, 6])
        scratch = sb("fscratch", [P, 1])
        mv = sb("fmv", [P, 2])
        eps = sb("feps", [P, 2])
        DTf, Cf = DT[:, :, :, :, :].rearrange("p c i t n -> p (c i t n)"), C[:, :, :].rearrange("p s n -> p (s n)")
        spaces = [v[:, lo:lo + HID] for v, lo in (
            (DTf, 0), (DTf, HID), (Cf, 0), (Cf, HID), (LS, 0), (LT[:, :, :, :].rearrange("p c i n -> p (c i n)"), 0),
            (HF[:, :, :].rearrange("p s n -> p (s n)"), 0), (ZT[:, :, :, :].rearrange("p s x n -> p (s x n)"), 0))]

        def stage(h, e):
            return spaces[EXPERTS * h + e]

        PH = ZS[:, :, :, :].rearrange("p a b n -> p (a b n)")[:, 0:SCH * E].rearrange("p (c d) -> p c d", d=E)
        ps = ctx.enter_context(nc.psum_tensor("psf", [P, 8, 512], F32))
        HB, ZB, OB, MB = 0, 2, 4, 5

        par_phi = sem("f_par_phi")
        par = sem("f_par")
        par_last = sem("f_par_last")
        prep = sem("f_prep")
        tr = sem("f_tr")
        zero = sem("f_zero")
        yp = sem("f_yp")
        m_mm = sem("f_m_mm")
        m_hi = sem("f_m_hi")
        m_cp = sem("f_m_cp")
        negmax = sem("f_negmax")
        c_ex = sem("f_c_ex")
        lt_sub = sem("f_lt_sub")
        lt_ex = sem("f_lt_ex")
        dt_ok = sem("f_dt_ok")
        h_mm = sem("f_h_mm")
        h_act = sem("f_h_act")
        h_lo = sem("f_h_lo")
        z_mm = sem("f_z_mm")
        z_hi = sem("f_z_hi")
        z_cp = sem("f_z_cp")
        y_hi = sem("f_y_hi")
        p_hi = sem("f_p_hi")
        w_mm = sem("f_w_mm")
        link = sem("f_link")
        olink = sem("f_olink")
        var = sem("f_var")
        rstd = sem("f_rstd")
        o_ok = sem("f_o_ok")
        o_st = sem("f_o_st")
        stored = sem("f_stored")
        block = ctx.enter_context(nc.Block())
        LINKS, OLINKS, O_READ, CS_READ = 5, 9, 5, 6
        NPAR = 3 * EXPERTS
        HIGHS = 4 * EXPERTS

        def stages(eng, name, body):
            body(Stage(name, -1, 1, (1,)))
            body(Stage(name, 0, 0, (0, 1)))
            with eng.Fori(0, PAIRS // 2 - 1) as i:
                for s in range(2):
                    body(Stage(name, i * 2 + (1 + s), (1 + s) % 2, (-1, 0, 1)))
            body(Stage(name, PAIRS - 1, 1, (-1, 0)))
            body(Stage(name, PAIRS, 0, (-1,)))

        def wait(eng, s, value):
            if value is not None:
                eng.wait_ge(s, value)

        def wait_low(eng, g, r, u):
            wait(eng, h_lo, g.times(r, UNITS, u + 1))

        @block.sync
        def _(sp):
            def param(dst, src, loaded=par):
                sp.dma_start(dst, src).then_inc(loaded, 16)

            param(PH, a["phi"].rearrange("e (k p) d -> p (e k) d", p=P), par_phi)
            for e in range(EXPERTS):
                for h in range(2):
                    param(stage(h, e)[0:EH], a["fw1"][e, EH * h:EH * h + EH, :])
                param(stage(1, e)[EH:EA], a["fb1"][e:e + 1, :])
            param(W2[:, :, :], a["fw2"].rearrange("e (k p) d -> p (e k) d", p=P), par_last)
            param(B2[:, :, :], a["fb2"].rearrange("(u e) n -> u e n", u=1).broadcast_to([P, EXPERTS, E]), par_last)
            sp.nop().then_inc(stored, 1)
            with sp.Fori(0, PAIRS // 2) as i:
                for s in range(2):
                    sp.wait_ge(o_ok, i * 2 + (s + 1))
                    for h in range(2):
                        sp.dma_start(out[bass.ds(i * 2 + (s + HALF * h), 1), :, :].rearrange("b n d -> (b n) d"),
                                     o[SLOT * h:SLOT * h + KT, s, :]).then_inc(o_st, 16)
                    sp.wait_ge(o_st, i * 64 + (32 * s + 32))
                    sp.nop().then_inc(stored, 1)
            sp.wait_ge(o_st, 32 * PAIRS)

        @block.gpsimd
        def _(pool):
            pool.memset(ones[:, 0:1], 1.0)
            pool.memset(ones[:, 1:2], 0.0)
            pool.memset(eps[:, 0:1], 1e-5)
            pool.memset(eps[:, 1:2], -0.5).then_inc(zero, 1)
            pool.wait_ge(prep, 4 + 1)
            pool.memset(DT[:, :, :, :, KT:SLOT], 0.0).then_inc(zero, 1)
            pool.wait_ge(zero, 2)

            def body(g):
                for r, ev in g.events:
                    if ev == ("y", 0):
                        wait(pool, m_cp, g.job(0))
                        s = (g.parity + r) % 2
                        src = Y1[:, bass.ds(g.j + r, 1), :] if not isinstance(g.j, int) else Y1[:, g.j + r:g.j + r + 1, :]
                        pool.tensor_copy(YP[:, s, :].unsqueeze(1), src).then_inc(yp, 1)
                    if ev[0] == "dt":
                        wait(pool, link, g.times(r, LINKS, 5))
                        wait(pool, m_cp, g.ready(r - 1, ("d", EXPERTS - 1)))
                        for twice in range(2):
                            for half in range(2):
                                cs = slice(SCH // 2 * half, SCH // 2 * half + SCH // 2)
                                pool.tensor_tensor(DT[:, cs, :, twice, 0:KT], LT[:, cs, :, :],
                                                   mi[:, :].rearrange("p (c i) -> p c i", i=2)[:, cs].unsqueeze(3).broadcast_to([P, SCH // 2, 2, KT]),
                                                   ALU.mult).then_inc(dt_ok, 1)
                                wait(pool, dt_ok, g.times(r, 4, 2 * twice + half + 1))
                    if ev[0] == "out":
                        wait(pool, var, g.times(r, 1, 1))
                        pool.tensor_tensor(mv[:, 1:2], mv[:, 1:2], eps[:, 0:1], ALU.add).then_inc(rstd, 1)
                        wait(pool, rstd, g.times(r, 2, 1))
                        pool.tensor_tensor(mv[:, 1:2], mv[:, 1:2], eps[:, 1:2], ALU.pow).then_inc(rstd, 1)

            stages(pool, "pool", body)

        @block.tensor
        def _(pe):
            mm = nc.tensor.matmul
            pe.wait_ge(par_phi, 16)
            for h in range(2):
                for c in range(SCH):
                    ins = nc.tensor.transpose(ps[0:EH, 2 * h + c // 4, P * (c % 4):P * (c % 4) + P],
                                              PH[:, c, EH * h:EH * h + EH], ident[:, :])
            ins.then_inc(tr, 1)
            pe.wait_ge(prep, 4 + 2 + 4)
            pe.wait_ge(zero, 2)

            def body(g):
                for r, ev in g.events:
                    kind, i = ev[0], ev[1] if len(ev) > 1 else None
                    s = (g.parity + r) % 2
                    if kind in JOBS:
                        n = g.jobs[r, ev]
                        b = ps[:, MB + g.bank(n), :]
                        wait(pe, m_cp, g.job(n - ROTATING + 1))
                    if kind == "h":
                        e, half, img, c = unit(i)
                        if i % STEP == 0:
                            wait(pe, m_cp, g.ready(r, ("w", e, 0), ("w", e, 1), ("d", e)))
                        wait(pe, h_act, g.times(r, UNITS, i - 1))
                        for part in range(2):
                            ins = mm(ps[:, HB + i % 2, 0:HH], D[:, e % 2, part, img, P * c:P * c + P],
                                     R[:, e % 2, img, HH * half:HH * half + HH], start=(part == 0), stop=(part == 1))
                        ins.then_inc(h_mm, 1)
                    if kind == "z":
                        e, half, img, c = unit(i)
                        wait_low(pe, g, r, i)
                        if c == 0:
                            k = i // 2
                            wait(pe, z_cp, g.times(r, UNITS // 2, k - 1))
                        if i % 4 == 0:
                            wait(pe, m_cp, g.ready(r, ("c", e)))
                        w = CT[:, e % 2, img, c, :, :].rearrange("p t n -> p (t n)")
                        mm(ps[:, ZB + i // 2 % 2, 0:HH], w, HI[:, i % HS, :], start=(c == 0), stop=False)
                        mm(ps[:, ZB + i // 2 % 2, 0:HH], w, HL[:, i % HS, :], start=False, stop=(c == 1)).then_inc(z_mm, 1)
                    if kind == "zt":
                        wait(pe, z_cp, g.times(r, UNITS // 2, 4 * i + 2 * ev[2] + 2))
                        for x in range(3):
                            ins = nc.tensor.transpose(b[:, P * x:P * x + P], ZS[:, i % 2, ev[2], P * x:P * x + P], ident[:, :])
                    if kind == "w2":
                        wait(pe, m_cp, g.ready(r, ("zt", i, ev[2])))
                        if i == 0 and ev[2] == 0:
                            if g.fixed:
                                pe.wait_ge(par_last, 16 * 2)
                            wait(pe, olink, g.times(r - 1, OLINKS, O_READ))
                        for x in range(3):
                            ins = mm(ps[:, OB, 0:E], ZT[:, ev[2], x, :], W2[:, 6 * i + 3 * ev[2] + x, :],
                                     start=(i + ev[2] + x == 0), stop=(i == 3 and ev[2] == 1 and x == 2))
                        ins.then_inc(w_mm, 1)
                    if kind == "y":
                        wait(pe, yp, g.times(r, 1, 1))
                        ins = nc.tensor.transpose(b[0:EH, 0:P], YP[:, s, EH * i:EH * i + EH], ident[:, :])
                    if kind == "l":
                        wait(pe, m_cp, g.ready(r, ("y", 0), ("y", 1)))
                        for n, (py, pw) in enumerate(((0, 0), (0, 1), (1, 0))):
                            for h in range(2):
                                ins = mm(b[:, :], YT[0:EH, s, py, h, :], PT[:, pw, h, 512 * i:512 * i + 512],
                                         start=(n + h == 0), stop=(n + h == 3))
                    if kind == "t":
                        wait(pe, m_cp, g.ready(r, ("l", i)))
                        for c in range(4):
                            lo = P * (4 * i + c)
                            ins = nc.tensor.transpose(b[:, P * c:P * c + P], LS[:, lo:lo + P], ident[:, :])
                    if kind == "w":
                        lo = HID * i + HH * ev[2]
                        for n, (py, pw) in enumerate(((0, 0), (0, 1), (1, 0))):
                            for rows, h in HK:
                                ins = mm(b[:, 0:HH], YT[rows, s, py, h, :], W1[rows, pw, h, lo:lo + HH],
                                         start=(n + h == 0), stop=(n + h == 3))
                    if kind == "c":
                        wait(pe, c_ex, g.times(r, 1, 1))
                        for c in range(2):
                            lo = SLOTS * i + P * c
                            ins = nc.tensor.transpose(b[:, P * c:P * c + P], C[:, s, lo:lo + P], ident[:, :])
                    if kind == "d":
                        wait(pe, dt_ok, g.times(r, 4, 4))
                        for img in range(2):
                            for c in range(2):
                                v = DT[:, 2 * i + c, img, :, :].rearrange("p t n -> p (t n)")
                                ins = nc.tensor.transpose(b[:, SLOTS * img + P * c:SLOTS * img + P * c + P], v, ident[:, :])
                    if kind in JOBS:
                        ins.then_inc(m_mm, 1)

            stages(pe, "pe", body)

        @block.scalar
        def _(act):
            act.wait_ge(tr, 1)
            for h in range(2):
                ins = act.activation(PT[:, 0, h, :].rearrange("p (c n) -> p c n", c=2), ps[0:EH, 2 * h:2 * h + 2, :], ACT.Copy)
            ins.then_inc(p_hi, 1)
            act.wait_ge(par, 16 * NPAR)
            for h, n in ((0, EH), (1, EA)):
                for e in range(EXPERTS):
                    ins = act.activation(W1[0:n, 0, h, HID * e:HID * e + HID], stage(h, e)[0:n], ACT.Copy)
                ins.then_inc(p_hi, 1)

            def body(g):
                for r, ev in g.events:
                    kind, i = ev[0], ev[1] if len(ev) > 1 else None
                    s = (g.parity + r) % 2
                    if kind in JOBS:
                        n = g.jobs[r, ev]
                        b = ps[:, MB + g.bank(n), :]
                    if kind in ("y", "w", "d", "c"):
                        wait(act, m_mm, g.job(n + 1))
                    if kind == "y":
                        act.activation(YT[0:EH, s, 0, i, :], b[0:EH, 0:P], ACT.Copy).then_inc(y_hi, 1)
                    if kind == "w":
                        for img in range(2):
                            ins = act.activation(R[IMG[img], i % 2, img, HH * ev[2]:HH * ev[2] + HH], b[IMG[img], 0:HH], ACT.Copy)
                        ins.then_inc(m_hi, 1)
                    if kind == "d":
                        act.activation(D[:, i % 2, 0, :, :], b[:, :].rearrange("p (i n) -> p i n", i=2), ACT.Copy).then_inc(m_hi, 1)
                    if kind == "c":
                        wait(act, z_mm, g.times(r, UNITS, STEP * (i - 1)))
                        act.activation(CT[:, i % 2, :, :, 0, :], b[:, 0:SLOTS].rearrange("p (c i n) -> p i c n", c=2, i=2),
                                       ACT.Copy).then_inc(m_hi, 1)
                    if kind == "exp":
                        wait(act, negmax, g.times(r, 1, 1))
                        wait(act, olink, g.times(r - 2, OLINKS, CS_READ))
                        for e in range(EXPERTS):
                            lo = SLOTS * e
                            ins = act.activation(C[:, s, lo:lo + SLOTS], LS[:, lo:lo + SLOTS], ACT.Exp, bias=mx[:, 1:2],
                                                 accum_out=CS[:, s, e:e + 1])
                        ins.then_inc(c_ex, 1)
                        wait(act, lt_sub, g.times(r, 2, 2))
                        act.activation(LT[:, :, :, :], LT[:, :, :, :], ACT.Exp).then_inc(lt_ex, 1)
                    if kind == "ze":
                        k = 4 * i + 2 * ev[2] + ev[3]
                        wait(act, z_mm, g.times(r, UNITS, 2 * k + 2))
                        wait(act, z_cp, g.times(r, UNITS // 2, k - 1))
                        act.activation(ZF[IMG[1], k % 2, :], ps[IMG[0], ZB + k % 2, 0:HH], ACT.Copy).then_inc(z_hi, 1)
                    if kind == "h":
                        wait(act, h_mm, g.times(r, UNITS, i + 1))
                        wait(act, z_mm, g.times(r, UNITS, i - HS + 1))
                        act.activation(HI[:, i % HS, :], ps[:, HB + i % 2, 0:HH], ACT.Gelu_apprx_tanh)
                        wait_low(act, g, r, i - 4)
                        act.activation(HF[:, i % 4, :], ps[:, HB + i % 2, 0:HH], ACT.Gelu_apprx_tanh).then_inc(h_act, 1)

            stages(act, "act", body)

        @block.vector
        def _(dve):
            dve.wait_ge(p_hi, 1)
            for h in range(2):
                for c in range(2):
                    n = slice(512 * c, 512 * c + 512)
                    dve.tensor_tensor(PT[:, 1, h, n], ps[0:EH, 2 * h + c, :], PT[:, 0, h, n].bitcast(F32), ALU.subtract).then_inc(prep, 1)
            for h, n in ((0, EH), (1, EA)):
                dve.wait_ge(p_hi, 2 + h)
                for e in range(EXPERTS):
                    lo = slice(HID * e, HID * e + HID)
                    ins = dve.tensor_tensor(W1[0:n, 1, h, lo], stage(h, e)[0:n], W1[0:n, 0, h, lo].bitcast(F32), ALU.subtract)
                ins.then_inc(prep, 1)
            dve.wait_ge(zero, 1)
            for part in range(2):
                for slot in range(2):
                    dve.tensor_copy(YT[EH:EA, slot, part, :, :].rearrange("p h n -> p (h n)"),
                                    ones[EH:EA, part:part + 1].broadcast_to([1, 2 * P])).then_inc(prep, 1)

            def body(g):
                for r, ev in g.events:
                    kind, i = ev[0], ev[1] if len(ev) > 1 else None
                    s = (g.parity + r) % 2

                    def step(n, ins):
                        ins.then_inc(link, 1)
                        wait(dve, link, g.times(r, LINKS, n))

                    def ostep(n, ins):
                        ins.then_inc(olink, 1)
                        wait(dve, olink, g.times(r, OLINKS, n))

                    if kind in JOBS:
                        n = g.jobs[r, ev]
                        b = ps[:, MB + g.bank(n), :]
                        wait(dve, m_mm, g.job(n + 1))
                    if kind in ("w", "d", "c"):
                        order = {"w": {0: 1, 1: 3}.get(ev[2] if kind == "w" else 0, 0), "d": 2, "c": 4}[kind]
                        wait(dve, m_hi, g.times(r, HIGHS, 4 * i + order))
                    if kind == "w":
                        cols = slice(HH * ev[2], HH * ev[2] + HH)
                        for img in range(2):
                            ins = dve.tensor_tensor(R[IMG[1 - img], i % 2, img, cols], b[IMG[img], 0:HH],
                                                    R[IMG[img], i % 2, img, cols].bitcast(F32), ALU.subtract)
                        ins.then_inc(m_cp, 1)
                    if kind == "d":
                        dve.tensor_tensor(D[:, i % 2, 1, :, :], b[:, :].rearrange("p (i n) -> p i n", i=2),
                                          D[:, i % 2, 0, :, :].bitcast(F32), ALU.subtract).then_inc(m_cp, 1)
                    if kind == "c":
                        dve.tensor_tensor(CT[:, i % 2, :, :, 1, :], b[:, 0:SLOTS].rearrange("p (c i n) -> p i c n", c=2, i=2),
                                          CT[:, i % 2, :, :, 0, :].bitcast(F32), ALU.subtract).then_inc(m_cp, 1)
                    if kind == "y":
                        wait(dve, y_hi, g.times(r, 2, i + 1))
                        dve.tensor_tensor(YT[0:EH, s, 1, i, :], b[0:EH, 0:P], YT[0:EH, s, 0, i, :].bitcast(F32),
                                          ALU.subtract).then_inc(m_cp, 1)
                    if kind == "l":
                        wait(dve, c_ex, g.times(r - 1, 1, 1))
                        dve.tensor_copy(LS[:, 512 * i:512 * i + 512], b[:, :]).then_inc(m_cp, 1)
                        if i == 1:
                            wait(dve, m_cp, g.job(n + 1))
                            step(1, dve.tensor_reduce(mx[:, 0:1], LS[:, :], AX_X, ALU.max))
                            dve.tensor_scalar(mx[:, 1:2], mx[:, 0:1], -1.0, None, ALU.mult).then_inc(negmax, 1)
                    if kind == "t":
                        v = b[:, :].rearrange("p (c i n) -> p c i n", c=4, n=SLOT)[:, :, :, 0:KT]
                        m = mt[:, 8 * i:8 * i + 8]
                        step(2 + i, dve.tensor_reduce(m.rearrange("p (c i) -> p c i", i=2), v, AX_X, ALU.max))
                        wide = m.rearrange("p (c i) -> p c i", i=2).unsqueeze(3).broadcast_to([P, 4, 2, KT])
                        if i == 0:
                            wait(dve, dt_ok, g.times(r - 1, 4, 4))
                        dve.tensor_tensor(LT[:, 4 * i:4 * i + 4, :, :], v, wide, ALU.subtract).then_inc(m_cp, 1)
                        wait(dve, m_cp, g.job(n + 1))
                        dve.memset(scratch[:, :], 0.0).then_inc(lt_sub, 1)
                    if kind == "dt":
                        wait(dve, lt_ex, g.times(r, 1, 1))
                        step(4, dve.tensor_reduce(mt[:, :].rearrange("p (c i) -> p c i", i=2), LT[:, :, :, :], AX_X, ALU.add))
                        step(5, dve.reciprocal(mi[:, :], mt[:, :]))
                    if g.fixed and ev == ("h", UNITS // 2):
                        dve.wait_ge(par_last, 16 * 2)
                    if kind == "h":
                        wait(dve, h_act, g.times(r, UNITS, i + 1))
                        dve.tensor_tensor(HL[:, i % HS, :], HF[:, i % 4, :], HI[:, i % HS, :].bitcast(F32),
                                          ALU.subtract).then_inc(h_lo, 1)
                    if kind == "ze":
                        k = 4 * i + 2 * ev[2] + ev[3]
                        wait(dve, z_hi, g.times(r, UNITS // 2, k + 1))
                        dve.tensor_tensor(ZS[IMG[ev[3]], i % 2, ev[2], :], ps[IMG[1], ZB + k % 2, 0:HH], ZF[IMG[1], k % 2, :],
                                          ALU.add).then_inc(z_cp, 1)
                    if kind == "zt":
                        wait(dve, w_mm, g.times(r, 2 * EXPERTS, 2 * i + ev[2] - 1))
                        dve.tensor_copy(ZT[:, ev[2], :, :], b[:, 0:3 * P].rearrange("p (x n) -> p x n", n=P)).then_inc(m_cp, 1)
                    if kind == "out":
                        wait(dve, c_ex, g.times(r, 1, 1))
                        ostep(1, dve.tensor_scalar(acc[:, :], B2[:, 0, :], CS[:, s, 0:1], None, ALU.mult))
                        for e in range(1, EXPERTS):
                            ostep(1 + e, dve.scalar_tensor_tensor(out=acc[:, :], in0=B2[:, e, :], scalar=CS[:, s, e:e + 1],
                                                                  in1=acc[:, :], op0=ALU.mult, op1=ALU.add))
                        wait(dve, w_mm, g.times(r, 2 * EXPERTS, 2 * EXPERTS))
                        ostep(O_READ, dve.tensor_tensor(acc[:, :], acc[:, :], ps[:, OB, 0:E], ALU.add))
                        ostep(CS_READ, dve.tensor_reduce(ss[:, 0:1], CS[:, s, :], AX_X, ALU.add))
                        ostep(7, dve.reciprocal(ss[:, 1:2], ss[:, 0:1]))
                        y = Y1[:, bass.ds(g.j + r, 1), :] if not isinstance(g.j, int) else Y1[:, g.j + r:g.j + r + 1, :]
                        ostep(8, dve.scalar_tensor_tensor(out=acc[:, :].unsqueeze(1), in0=acc[:, :].unsqueeze(1), scalar=ss[:, 1:2],
                                                          in1=y, op0=ALU.mult, op1=ALU.add))
                        ostep(9, dve.bn_stats(st[:, :], acc[:, :]))
                        dve.memset(scratch[:, :], 0.0)
                        dve.bn_aggr(mv[:, :], st[:, :]).then_inc(var, 1)
                    if kind == "norm":
                        wait(dve, rstd, g.times(r, 2, 2))
                        wait(dve, stored, g.times(r, 1, 1))
                        dve.tensor_scalar(o[:, s, :], acc[:, :], mv[:, 0:1], mv[:, 1:2], ALU.subtract, ALU.mult).then_inc(o_ok, 1)
                        wait(dve, o_ok, g.times(r, 1, 1))

            stages(dve, "dve", body)


def tower(nc, a, out):
    with ExitStack() as ctx:
        ident = ctx.enter_context(nc.sbuf_tensor("ident", [P, P], F32))
        Y1 = ctx.enter_context(nc.sbuf_tensor("Y1", [P, HALF, E], F32))
        with ExitStack() as tokens:
            XT = tokens.enter_context(nc.sbuf_tensor("XT", [EH + 1, 2, HALF, P], F32))
            conv_phase(nc, a, XT, Y1, ident)
            attention_phase(nc, a, XT, Y1, ident)
        ffn_phase(nc, a, Y1, ident, out)


_NAMES = {"x": "x", "wqkv": "L0_attn_W_qkv", "bqkv": "L0_attn_b_qkv", "wproj": "L0_attn_W_proj",
          "bproj": "L0_attn_b_proj", "wgp": "L0_attn_W_gp", "alpha": "L0_attn_alpha", "phi": "L0_ffn_phi",
          "fw1": "L0_ffn_w1", "fb1": "L0_ffn_b1", "fw2": "L0_ffn_w2", "fb2": "L0_ffn_b2",
          **{n: "L0_tok_" + n for n in ("w0", "s0", "b0", "wdw", "sdw", "bdw", "wpw", "spw", "bpw",
                                        "w1", "s1", "b1", "w2", "s2", "b2", "w3", "s3", "b3")}}


def kernel(**inputs):
    import concourse.bacc as bacc
    from concourse.bass_utils import run_bass_kernel_spmd

    nc = bacc.Bacc("TRN2", target_bir_lowering=False, num_devices=1)
    arrays, a = {}, {}
    for short, name in _NAMES.items():
        v = np.ascontiguousarray(inputs[name])
        if v.ndim == 0:
            v = v.reshape(1)
        arrays[f"in_{short}"] = v
        a[short] = nc.dram_tensor(f"in_{short}", v.shape, mybir.dt.from_np(v.dtype), kind="ExternalInput").ap()
    out = nc.dram_tensor("out_tokens", (IMAGES, TOKENS, E), F32, kind="ExternalOutput").ap()
    tower(nc, a, out)
    r = run_bass_kernel_spmd(nc, [arrays], core_ids=[0])
    return r.results[0]["out_tokens"]
```
